# Optimizing a Trainium2 kernel written in Bass

```python
import numpy as np
import jax
import jax.numpy as jnp

def _softmax(x, axis=-1):
    return jax.nn.softmax(x, axis=axis)

def _gelu(x):
    return jax.nn.gelu(x, approximate=True)

def _silu(x):
    return jax.nn.silu(x)

def _sigmoid(x):
    return jax.nn.sigmoid(x)

def _layernorm(x, axis=-1, eps=1e-05):
    m = jnp.mean(x, axis=axis, keepdims=True)
    v = jnp.var(x, axis=axis, keepdims=True)
    return (x - m) / jnp.sqrt(v + eps)

def _scatter_add(tgt, idx, src, axis=0):
    return tgt.at[idx].add(src)

def _segment_sum(src, seg, n):
    return jax.ops.segment_sum(src, seg, n)
kernel_name = 'mk_hybrid_d1_jaxref_r8_c45269'

def setup_inputs(seed: int=0):
    np.random.seed(seed)
    _w = jnp.asarray

    def _L0_attn_a_setup():
        import jax, jax.numpy as jnp
        import numpy as np
        import math
        N_HEAD = 16
        DEG = 2
        EPS = 1e-07
        key = jax.random.key(seed)
        k1, k2 = jax.random.split(key)
        B, T, C = (2, 256, 128)
        x = jax.random.normal(k1, (B, T, C), dtype=jnp.float32)
        W = jax.random.normal(k2, (3 * C + N_HEAD, C), dtype=jnp.float32) * (1.0 / math.sqrt(C))
        return {'x': x, 'W': W}
    _L0_attn_a_in = _L0_attn_a_setup()

    def _L0_attn_b_setup():
        import jax, jax.numpy as jnp
        import numpy as np
        HIDDEN = 128
        EXPAND = 1
        INPUT_DIM = HIDDEN * EXPAND
        CONV_K = 4
        NORM_EPS = 1e-05

        def causal_depthwise_conv(x, w):
            B, T, D = x.shape
            K = w.shape[1]
            xp = jnp.pad(x, ((0, 0), (K - 1, 0), (0, 0)))
            out = jnp.zeros_like(x)
            for k in range(K):
                out = out + xp[:, k:k + T, :] * w[:, k]
            return out

        def hgrn_forward(x, Wi, Wf, Wg, conv_i, conv_f, g_norm_weight, Wo):
            B, T, H = x.shape
            i_raw = jnp.einsum('bth,hd->btd', x, Wi)
            f_raw = jnp.einsum('bth,hd->btd', x, Wf)
            g_raw = jnp.einsum('bth,hd->btd', x, Wg)
            i_raw = causal_depthwise_conv(i_raw, conv_i)
            f_raw = causal_depthwise_conv(f_raw, conv_f)
            forget_gate = jax.nn.sigmoid(f_raw)
            i = jax.nn.silu(i_raw) * (1.0 - forget_gate)

            def step(h, fi):
                f_t, i_t = fi
                h = f_t * h + i_t
                return (h, h)
            h0 = jnp.zeros((B, i.shape[-1]), dtype=x.dtype)
            _, o_rec = jax.lax.scan(step, h0, (forget_gate.swapaxes(0, 1), i.swapaxes(0, 1)))
            o_rec = o_rec.swapaxes(0, 1)
            rms = jax.lax.rsqrt(jnp.mean(o_rec * o_rec, axis=-1, keepdims=True) + NORM_EPS)
            o = o_rec * rms * g_norm_weight * jax.nn.silu(g_raw)
            return jnp.einsum('btd,dh->bth', o, Wo)
        key = jax.random.key(seed)
        ks = jax.random.split(key, 8)
        B, T, H, D = (4, 256, HIDDEN, INPUT_DIM)
        s = 1.0 / np.sqrt(H)
        return {'x': jax.random.normal(ks[0], (B, T, H), dtype=jnp.float32), 'Wi': jax.random.normal(ks[1], (H, D), dtype=jnp.float32) * s, 'Wf': jax.random.normal(ks[2], (H, D), dtype=jnp.float32) * s, 'Wg': jax.random.normal(ks[3], (H, D), dtype=jnp.float32) * s, 'conv_i': jax.random.normal(ks[4], (D, CONV_K), dtype=jnp.float32) * 0.5, 'conv_f': jax.random.normal(ks[5], (D, CONV_K), dtype=jnp.float32) * 0.5, 'g_norm_weight': jnp.ones((D,), dtype=jnp.float32), 'Wo': jax.random.normal(ks[6], (D, H), dtype=jnp.float32) / np.sqrt(D)}
    _L0_attn_b_in = _L0_attn_b_setup()

    def _L0_ffn_setup():
        import jax, jax.numpy as jnp
        import numpy as np
        TOP_K = 2
        NUM_EXPERTS = 8
        DIM = 128
        HIDDEN = 352
        BS, SLEN = (2, 128)

        def _grouped_ffn(x, w1, w2, w3, counts):
            num_experts = w1.shape[0]
            ends = jnp.cumsum(counts)
            starts = ends - counts
            t = jnp.arange(x.shape[0])
            out = jnp.zeros((x.shape[0], w2.shape[-1]), x.dtype)
            for e in range(num_experts):
                m = ((t >= starts[e]) & (t < ends[e])).astype(x.dtype)[:, None]
                xe = x * m
                h = jax.nn.silu(xe @ w1[e]) * (xe @ w3[e])
                out = out + h @ w2[e] * m
            return out
        key = jax.random.key(seed)
        k = jax.random.split(key, 5)
        std = 0.02
        return {'x': jax.random.normal(k[0], (BS, SLEN, DIM), jnp.float32), 'gate_w': jax.random.normal(k[1], (NUM_EXPERTS, DIM), jnp.float32) * std, 'expert_bias': jnp.zeros((NUM_EXPERTS,), jnp.float32), 'w1': jax.random.normal(k[2], (NUM_EXPERTS, DIM, HIDDEN), jnp.float32) * std, 'w2': jax.random.normal(k[3], (NUM_EXPERTS, HIDDEN, DIM), jnp.float32) * std, 'w3': jax.random.normal(k[4], (NUM_EXPERTS, DIM, HIDDEN), jnp.float32) * std}
    _L0_ffn_in = _L0_ffn_setup()
    _d = {'L0_attn_a_x': _L0_attn_a_in['x'], 'L0_attn_a_W': _L0_attn_a_in['W'], 'L0_attn_b_Wi': _L0_attn_b_in['Wi'], 'L0_attn_b_Wf': _L0_attn_b_in['Wf'], 'L0_attn_b_Wg': _L0_attn_b_in['Wg'], 'L0_attn_b_conv_i': _L0_attn_b_in['conv_i'], 'L0_attn_b_conv_f': _L0_attn_b_in['conv_f'], 'L0_attn_b_g_norm_weight': _L0_attn_b_in['g_norm_weight'], 'L0_attn_b_Wo': _L0_attn_b_in['Wo'], 'L0_ffn_gate_w': _L0_ffn_in['gate_w'], 'L0_ffn_expert_bias': _L0_ffn_in['expert_bias'], 'L0_ffn_w1': _L0_ffn_in['w1'], 'L0_ffn_w2': _L0_ffn_in['w2'], 'L0_ffn_w3': _L0_ffn_in['w3']}
    _x0 = _d['L0_attn_a_x']
    _d['L0_attn_a_x'] = jax.random.normal(jax.random.fold_in(jax.random.key(seed), 1), (4, 512, 128), dtype=_x0.dtype)
    del _x0
    return _d

def reference(L0_attn_a_x, L0_attn_a_W, L0_attn_b_Wi, L0_attn_b_Wf, L0_attn_b_Wg, L0_attn_b_conv_i, L0_attn_b_conv_f, L0_attn_b_g_norm_weight, L0_attn_b_Wo, L0_ffn_gate_w, L0_ffn_expert_bias, L0_ffn_w1, L0_ffn_w2, L0_ffn_w3):

    def _L0_attn_a_ref(x, W):
        import jax, jax.numpy as jnp
        import numpy as np
        import math
        N_HEAD = 16
        DEG = 2
        EPS = 1e-07
        B, T, C = x.shape
        nh = N_HEAD
        hs = C // nh
        scale = 1.0 / math.sqrt(hs)
        qkvgr = jnp.einsum('btc,oc->bto', x, W)
        q, k, v = (qkvgr[..., :C], qkvgr[..., C:2 * C], qkvgr[..., 2 * C:3 * C])
        log_g = jax.nn.log_sigmoid(qkvgr[..., 3 * C:].astype(jnp.float32))
        log_G = jnp.cumsum(log_g, axis=1).transpose(0, 2, 1)

        def heads(a):
            return a.reshape(B, T, nh, hs).transpose(0, 2, 1, 3)
        Q, K, V = (heads(q), heads(k), heads(v))
        S = jnp.einsum('bhtd,bhsd->bhts', Q, K)
        Tm = DEG * jnp.log(jnp.abs(S) + EPS) + jnp.log(jnp.float32(scale))
        Z = Tm + log_G[..., :, None] - log_G[..., None, :]
        mask = jnp.tril(jnp.ones((T, T), dtype=bool))
        Z = jnp.where(mask, Z, -jnp.inf)
        Z_rowmax = jax.lax.stop_gradient(jnp.max(Z, axis=-1, keepdims=True))
        P = jnp.exp(Z - Z_rowmax)
        norm = jnp.sum(P, axis=-1)
        O = jnp.einsum('bhts,bhsd->bhtd', P, V)
        y = O / norm[..., None]
        return y.transpose(0, 2, 1, 3).reshape(B, T, C)

    def _L0_attn_b_ref(x, Wi, Wf, Wg, conv_i, conv_f, g_norm_weight, Wo):
        import jax, jax.numpy as jnp
        import numpy as np
        HIDDEN = 128
        EXPAND = 1
        INPUT_DIM = HIDDEN * EXPAND
        CONV_K = 4
        NORM_EPS = 1e-05

        def causal_depthwise_conv(x, w):
            B, T, D = x.shape
            K = w.shape[1]
            xp = jnp.pad(x, ((0, 0), (K - 1, 0), (0, 0)))
            out = jnp.zeros_like(x)
            for k in range(K):
                out = out + xp[:, k:k + T, :] * w[:, k]
            return out

        def hgrn_forward(x, Wi, Wf, Wg, conv_i, conv_f, g_norm_weight, Wo):
            B, T, H = x.shape
            i_raw = jnp.einsum('bth,hd->btd', x, Wi)
            f_raw = jnp.einsum('bth,hd->btd', x, Wf)
            g_raw = jnp.einsum('bth,hd->btd', x, Wg)
            i_raw = causal_depthwise_conv(i_raw, conv_i)
            f_raw = causal_depthwise_conv(f_raw, conv_f)
            forget_gate = jax.nn.sigmoid(f_raw)
            i = jax.nn.silu(i_raw) * (1.0 - forget_gate)

            def step(h, fi):
                f_t, i_t = fi
                h = f_t * h + i_t
                return (h, h)
            h0 = jnp.zeros((B, i.shape[-1]), dtype=x.dtype)
            _, o_rec = jax.lax.scan(step, h0, (forget_gate.swapaxes(0, 1), i.swapaxes(0, 1)))
            o_rec = o_rec.swapaxes(0, 1)
            rms = jax.lax.rsqrt(jnp.mean(o_rec * o_rec, axis=-1, keepdims=True) + NORM_EPS)
            o = o_rec * rms * g_norm_weight * jax.nn.silu(g_raw)
            return jnp.einsum('btd,dh->bth', o, Wo)
        return hgrn_forward(x, Wi, Wf, Wg, conv_i, conv_f, g_norm_weight, Wo)

    def _L0_ffn_ref(x, gate_w, expert_bias, w1, w2, w3):
        import jax, jax.numpy as jnp
        import numpy as np
        TOP_K = 2
        NUM_EXPERTS = 8
        DIM = 128
        HIDDEN = 352
        BS, SLEN = (2, 128)

        def _grouped_ffn(x, w1, w2, w3, counts):
            num_experts = w1.shape[0]
            ends = jnp.cumsum(counts)
            starts = ends - counts
            t = jnp.arange(x.shape[0])
            out = jnp.zeros((x.shape[0], w2.shape[-1]), x.dtype)
            for e in range(num_experts):
                m = ((t >= starts[e]) & (t < ends[e])).astype(x.dtype)[:, None]
                xe = x * m
                h = jax.nn.silu(xe @ w1[e]) * (xe @ w3[e])
                out = out + h @ w2[e] * m
            return out
        bs, slen, dim = x.shape
        num_experts = gate_w.shape[0]
        xf = x.reshape(bs * slen, dim)
        scores = jax.nn.softmax((xf @ gate_w.T).astype(jnp.float32), axis=-1)
        _, sel = jax.lax.top_k(scores + expert_bias, TOP_K)
        top_scores = jnp.take_along_axis(scores, sel, axis=1).reshape(-1)
        sel_flat = sel.reshape(-1)
        counts = jnp.zeros((num_experts,), jnp.int32).at[sel_flat].add(1)
        order = jnp.argsort(sel_flat, stable=True)
        top_scores_sorted = top_scores[order]
        token_idx = order // TOP_K
        routed = xf[token_idx] * top_scores_sorted[:, None].astype(xf.dtype)
        routed_out = _grouped_ffn(routed, w1, w2, w3, counts)
        out = jnp.zeros_like(xf).at[token_idx].add(routed_out)
        return out.reshape(bs, slen, dim)
    x = L0_attn_a_x
    x = x + _L0_attn_a_ref(_layernorm(x, axis=-1), L0_attn_a_W)
    x = x + _L0_ffn_ref(_layernorm(x, axis=-1), L0_ffn_gate_w, L0_ffn_expert_bias, L0_ffn_w1, L0_ffn_w2, L0_ffn_w3)
    x = x + _L0_attn_b_ref(_layernorm(x, axis=-1), L0_attn_b_Wi, L0_attn_b_Wf, L0_attn_b_Wg, L0_attn_b_conv_i, L0_attn_b_conv_f, L0_attn_b_g_norm_weight, L0_attn_b_Wo)
    x = x + _L0_ffn_ref(_layernorm(x, axis=-1), L0_ffn_gate_w, L0_ffn_expert_bias, L0_ffn_w1, L0_ffn_w2, L0_ffn_w3)
    return x

_drawn_inputs = setup_inputs


def setup_inputs(seed=0):
    import zlib

    import numpy as np

    out = dict(_drawn_inputs(seed))
    spreads = {'L0_attn_b_g_norm_weight': (1.0, 0.2), 'L0_ffn_expert_bias': (0.0, 0.8)}
    factors = {'L0_ffn_gate_w': 8.0, 'L0_ffn_w1': 8.0, 'L0_ffn_w2': 8.0, 'L0_ffn_w3': 8.0}
    for name, (base, spread) in spreads.items():
        noise = np.random.default_rng([zlib.crc32(name.encode()), seed]).standard_normal(out[name].shape)
        drawn = base * np.exp(spread * noise) if base else spread * noise
        out[name] = jnp.asarray(drawn.astype(out[name].dtype))
    for name, factor in factors.items():
        out[name] = (out[name] * factor).astype(out[name].dtype)
    return out
```

```python
from contextlib import ExitStack

import concourse.bass as bass
from concourse import mybir

F32 = mybir.dt.float32
BF16 = mybir.dt.bfloat16
I32 = mybir.dt.int32
U32 = mybir.dt.uint32
ALU = mybir.AluOpType
ACT = mybir.ActivationFunctionType
AX = mybir.AxisListType
ADD, SUB, MUL = ALU.add, ALU.subtract, ALU.mult

P = 128
B, T, C = 4, 512, 128
NT = B * T // P
TB = T // P
H, HS = 16, 8
VW = HS + 1
GH = 4
NG = H // GH
GROUPS = B * NG
NE, HID = 8, 352
HC = [(0, 128), (128, 128), (256, 96)]
TOPK = 2
JOBS = 40
LN_EPS = 1e-5
LOG_EPS = 1e-7
CONV_K = 4
NEG = -1e30

OFF = [(i, j) for i in range(1, TB) for j in range(i)]
PAIR = {ij: n for n, ij in enumerate(OFF + [(j, j) for j in range(TB)])}
NOFF = len(OFF)
UNITS = 10


def unit_plan():
    plan = []
    for r in range(0, GH, 2):
        plan += [("diag", r), ("far", r), ("diag", r + 1), ("far", r + 1), ("mid", r)]
    return plan


PLAN = unit_plan()


def block_at(r, i, j):
    if i == j:
        return PLAN.index(("diag", r)), P * j
    if j == 1:
        return PLAN.index(("mid", r - r % 2)), 256 * (r % 2) + P * (i - 2)
    u = PLAN.index(("far", r))
    return (u, P * (i - 1)) if j == 0 else (u, 384)


def build(nc, x, W, Wi, Wf, Wg, conv_i, conv_f, gnw, Wo, gate_w, ebias, w1, w2, w3, out):
    x_rows = x.rearrange("b (t p) c -> p (b t) c", p=P)
    out_rows = out.rearrange("b (t p) c -> p (b t) c", p=P)
    xr = nc.dram_tensor("routed_rows", [JOBS * P, C], F32, kind="Internal").ap()
    parts_d = nc.dram_tensor("parts", [2, 2, H, 5, HS, T], BF16, kind="Internal").ap()
    gates_d = nc.dram_tensor("gates", [2, 2, H, 3, T], BF16, kind="Internal").ap()
    yr = nc.dram_tensor("routed_out", [JOBS * P, C], F32, kind="Internal").ap()

    with ExitStack() as ctx:
        def sb(name, shape, dt=F32):
            return ctx.enter_context(nc.sbuf_tensor(name, shape, dt))

        def sem(name):
            return ctx.enter_context(nc.semaphore(name))

        ps = ctx.enter_context(nc.psum_tensor("ps", [P, 8, 512], F32))

        ident = sb("ident", [P, P])
        identb = sb("identb", [P, P], BF16)
        tri = sb("tri", [P, P])
        ones = sb("ones", [P, P])
        trib = sb("trib", [P, P], BF16)
        onesb = sb("onesb", [P, P], BF16)
        negmask = sb("negmask", [P, TB, P], BF16)
        iom8 = sb("iom8", [P, NE])
        io40 = sb("io40", [P, JOBS])
        io128 = sb("io128", [P, NT])
        carry1 = sb("carry1", [P, NE, NT])
        zeros = sb("zeros", [P, 640])
        ebt = sb("ebt", [P, NE])
        WT = sb("WT", [P, 3 * C + H])
        gwT = sb("gwT", [P, NE])
        xt = sb("xt", [P, NT, C])
        PP = sb("PP", [P, 2, UNITS, 512])
        room = PP[:].rearrange("p a u t -> p (a u t)")
        xh = room[:, 0:NT * C].rearrange("p (i c) -> p i c", i=NT)
        xT = room[:, NT * C:2 * NT * C]
        st6 = sb("st6", [P, NT, 6])
        mv = sb("mv", [P, NT, 2])
        lnv = sb("lnv", [P, NT])
        lns = sb("lns", [P, NT])
        lnr = sb("lnr", [P, NT])
        lnt = sb("lnt", [P, NT])

        s_const = sem("s_const")
        s_x = sem("s_x")
        s_w = sem("s_w")
        s_gw = sem("s_gw")
        s_eb = sem("s_eb")
        s_zero = sem("s_zero")
        s_dve = sem("s_dve")
        s_act = sem("s_act")
        s_pool = sem("s_pool")
        s_var = sem("s_var")
        s_std = sem("s_std")
        s_norm = sem("s_norm")
        s_xTp = sem("s_xTp")
        s_xT = sem("s_xT")
        s_out = sem("s_out")
        count = {"dve": 0, "act": 0, "pool": 0}

        def link(ins, sems={"dve": s_dve, "act": s_act, "pool": s_pool}, engs={"dve": nc.vector, "act": nc.scalar, "pool": nc.gpsimd}, who="dve"):
            count[who] += 1
            ins.then_inc(sems[who], 1)
            engs[who].wait_ge(sems[who], count[who])

        def bc(ap, shape):
            return ap.to_broadcast(shape)

        def norm_vector(n, first_wait):
            v = nc.vector
            first_wait()
            if n:
                v.wait_ge(s_xTp, 4 * n)
            for i in range(NT):
                ins = v.bn_stats(st6[:, i, :], xt[:, i, :])
            link(ins)
            for i in range(NT):
                ins = v.bn_aggr(mv[:, i, :], st6[:, i, :])
            link(ins)
            v.tensor_scalar(lnv[:, :], mv[:, :, 1], LN_EPS, None, ADD).then_inc(s_var, 1)
            v.wait_ge(s_var, n + 1)
            v.wait_ge(s_std, n + 1)
            link(v.reciprocal(lnr[:, :], lns[:, :]))
            newton(lnr, lnv, lnt)
            for i in range(NT):
                v.tensor_scalar(xh[:, i, :], xt[:, i, :], mv[:, i, 0:1], lnr[:, i:i + 1], SUB, MUL).then_inc(s_norm, 1)

        def newton(r, v, t):
            link(nc.vector.tensor_tensor(t[:, :], v[:, :], r[:, :], MUL))
            link(nc.vector.tensor_tensor(t[:, :], t[:, :], r[:, :], MUL))
            link(nc.vector.tensor_scalar(t[:, :], t[:, :], -0.5, 1.5, MUL, ADD))
            link(nc.vector.tensor_tensor(r[:, :], r[:, :], t[:, :], MUL))

        def norm_scalar(n):
            a = nc.scalar
            a.wait_ge(s_var, n + 1)
            a.activation(lns[:, :], lnv[:, :], ACT.Sqrt).then_inc(s_std, 1)

        def turn_tensor(n, c):
            pe = nc.tensor
            if 4 * n + c >= 2:
                pe.wait_ge(s_xT, 4 * n + c - 1)
            pe.wait_ge(s_norm, NT * n + 4 * c + 4)
            for k in range(4):
                i = 4 * c + k
                ins = pe.transpose(ps[:, c % 2, P * k:P * k + P], xh[:, i, :], ident[:, :])
            ins.then_inc(s_xTp, 1)

        def turn_scalar(n, c):
            a = nc.scalar
            a.wait_ge(s_xTp, 4 * n + c + 1)
            a.activation(xT[:, 512 * c:512 * c + 512], ps[:, c % 2, :], ACT.Copy).then_inc(s_xT, 1)

        att = ctx.enter_context(ExitStack())

        def asb(name, shape, dt=F32):
            return att.enter_context(nc.sbuf_tensor(name, shape, dt))

        Wrows = asb("Wrows", [P, 3, C])
        Wgr = asb("Wgr", [H, C])
        gwr = asb("gwr", [NE, C])
        qk = asb("qk", [P, 2, B, T])
        part = asb("part", [P, 2, 2, 3, T], BF16)
        rest = asb("rest", [P, 2, T])
        mx = asb("mx", [P, B, 2])
        mxa = asb("mxa", [P, B, 2])
        fs = asb("fs", [P, B])
        feps = asb("feps", [P, B])
        va = asb("va", [P, NT, H, VW])
        z = asb("z", [P, NT, H])
        az = asb("az", [P, NT, H])
        lg = asb("lg", [P, NT, H])
        Gt = asb("Gt", [P, B, TB, H])
        Ct = asb("Ct", [P, B, TB, H])
        dec = asb("dec", [P, B, NOFF, H])
        rowf = asb("rowf", [P, B, TB, H])
        GT = asb("GT", [H, B, T])
        gp = asb("gp", [H, 2, 3, T], BF16)
        gr = asb("gr", [H, T])
        vp = asb("vp", [P, 2, len(PAIR), H, VW])
        QS = asb("QS", [102, 2, 8, T], BF16)
        KS = asb("KS", [102, 2, 8, T], BF16)
        A = asb("A", [P, 4, 512])
        E = asb("E", [P, 4, 512])
        OT = asb("OT", [P, 7, P])
        tmp = asb("tmp", [P, 3, GH, VW])
        YS = asb("YS", [P, TB, H, VW])
        rn = asb("rn", [P, TB, H])

        s_wT = sem("s_wT")
        s_wTc = sem("s_wTc")
        s_qkp = sem("s_qkp")
        s_qk = sem("s_qk")
        s_vzp = sem("s_vzp")
        s_vz = sem("s_vz")
        s_z = sem("s_z")
        s_l = sem("s_l")
        s_lg = sem("s_lg")
        s_gp = sem("s_gp")
        s_gt = sem("s_gt")
        s_dif = sem("s_dif")
        s_exp = sem("s_exp")
        s_gTp = sem("s_gTp")
        s_gT = sem("s_gT")
        s_mx = sem("s_mx")
        s_mxa = sem("s_mxa")
        s_fs = sem("s_fs")
        s_part = sem("s_part")
        s_gpart = sem("s_gpart")
        s_vp = sem("s_vp")
        s_store = sem("s_store")
        s_stack = [sem("s_stack0"), sem("s_stack1")]
        s_fill = sem("s_fill")
        s_S = sem("s_S")
        s_A = sem("s_A")
        s_Q = sem("s_Q")
        s_D = sem("s_D")
        s_E = sem("s_E")
        s_PD = sem("s_PD")
        s_pv = sem("s_pv")
        s_O = sem("s_O")
        s_OT = sem("s_OT")
        s_Y = sem("s_Y")
        s_xa = sem("s_xa")

        BK_S, BK_D, BK_OFF, BK_DIA, BK_T = 0, 3, 4, 5, 6
        NCONST = 13
        STACKS = 16 * 8
        STORES = 16 * 10

        def proj_sync():
            sp = nc.sync
            for b in range(B):
                sp.dma_start(xt[:, TB * b:TB * b + TB, :], x_rows[:, TB * b:TB * b + TB, :]).then_inc(s_x, 16)
            sp.dma_start(Wrows[:, :, :], W[0:3 * C, :].rearrange("(n p) c -> p n c", p=P)).then_inc(s_w, 16)
            sp.dma_start(Wgr[:, :], W[3 * C:3 * C + H, :]).then_inc(s_w, 16)
            sp.dma_start(gwr[:, :], gate_w).then_inc(s_w, 16)
            sp.dma_start(ebt[:, :], ebias.partition_broadcast(P)).then_inc(s_eb, 16)

        def clear_sync():
            sp = nc.sync
            sp.wait_ge(s_const, NCONST)
            xr_z = xr.rearrange("(p n) c -> p (n c)", p=P)
            for n in range(8):
                sp.dma_start(xr_z[:, 640 * n:640 * n + 640], zeros[:, :]).then_inc(s_zero, 16)

        def stack_sync(n):
            sp, b, half, slot = nc.sync, n // 2, n % 2, n % 2
            if half == 0:
                sp.wait_ge(s_part, 6 * (b + 1))
                if b >= 2:
                    sp.wait_ge(s_stack[0], STACKS * (b - 1))
                    sp.wait_ge(s_stack[1], STACKS * (b - 1))
                for which, pieces in ((0, 3), (1, 5)):
                    for k in range(pieces):
                        sp.dma_start(parts_d[b % 2, which, :, k, :, :], part[:, b % 2, which, k % 3, :]).then_inc(s_store, 16)
                sp.wait_ge(s_gpart, b + 1)
                for n2 in range(2):
                    sp.dma_start(gates_d[b % 2, n2], gp[:, n2, :, :]).then_inc(s_store, 16)
                sp.wait_ge(s_store, STORES * (b + 1))
            if n >= 2:
                sp.wait_ge(s_S, UNITS * 2 * (n - 1))
            heads = slice(8 * half, 8 * half + 8)
            for k in range(3):
                sp.dma_start(QS[24 * k:24 * k + 24, slot, :, :],
                             parts_d[b % 2, 0, heads, 0:3, :, :].rearrange("h k d t -> (k d) h t")).then_inc(s_stack[slot], 16)
                sp.dma_start(KS[24 * k:24 * k + 24, slot, :, :],
                             parts_d[b % 2, 1, heads, k:k + 3, :, :].rearrange("h k d t -> (k d) h t")).then_inc(s_stack[slot], 16)
            if n >= 2:
                sp.wait_ge(s_D, 8 * (n - 1))
            sp.dma_start(QS[96:99, slot, :, :], gates_d[b % 2, 0, heads].rearrange("h k t -> k h t")).then_inc(s_stack[slot], 16)
            sp.dma_start(KS[99:102, slot, :, :], gates_d[b % 2, 1, heads].rearrange("h k t -> k h t")).then_inc(s_stack[slot], 16)

        def const_pool():
            g = nc.gpsimd

            def part1(t, v):
                link(g.memset(t[:], v), who="pool")

            def triangle(t, op, fill, base, pattern, cm):
                g.affine_select(out=t[:], in_=t[:], compare_op=op, fill=fill, base=base,
                                pattern=pattern, channel_multiplier=cm).then_inc(s_const, 1)

            part1(ident, 0.0)
            triangle(ident, ALU.not_equal, 1.0, 0, [[-1, P]], 1)
            part1(tri, 1.0)
            triangle(tri, ALU.is_ge, 0.0, 0, [[1, P]], -1)
            g.memset(ones[:, :], 1.0).then_inc(s_const, 1)
            g.memset(va[:, :, :, HS:VW], 1.0).then_inc(s_const, 1)
            part1(identb, 0.0)
            triangle(identb, ALU.not_equal, 1.0, 0, [[-1, P]], 1)
            part1(negmask, 0.0)
            triangle(negmask, ALU.is_ge, NEG, 0, [[0, TB], [1, P]], -1)
            bound_pool()
            decayed_pool(0)
            part1(trib, 1.0)
            triangle(trib, ALU.is_ge, 0.0, -1, [[1, P]], -1)
            g.memset(onesb[:, :], 1.0).then_inc(s_const, 1)
            g.memset(zeros[:, :], 0.0).then_inc(s_const, 1)
            g.iota(iom8[:, :], [[1, NE]], base=-8, channel_multiplier=0, allow_small_or_imprecise_dtypes=True).then_inc(s_const, 1)
            g.iota(io40[:, :], [[1, JOBS]], base=0, channel_multiplier=0, allow_small_or_imprecise_dtypes=True).then_inc(s_const, 1)
            g.iota(io128[:, :], [[P, NT]], base=0, channel_multiplier=0, allow_small_or_imprecise_dtypes=True).then_inc(s_const, 1)
            part1(carry1, 1.0)
            g.memset(carry1[:, :, 0:1], 0.0).then_inc(s_const, 1)

        def stacks_vector():
            v = nc.vector
            for t in (QS, KS):
                v.memset(t[64:96].bitcast(F32), 0.0).then_inc(s_fill, 1)
                v.memset(t[96:102], 1.0).then_inc(s_fill, 1)

        def bound_pool():
            g = nc.gpsimd
            g.wait_ge(s_mx, 8)
            g.partition_all_reduce(mxa[:, :, :].rearrange("p b n -> p (b n)"), mx[:, :, :].rearrange("p b n -> p (b n)"),
                                   P, bass.bass_isa.ReduceOp.max).then_inc(s_mxa, 1)

        def proj_tensor():
            pe = nc.tensor
            pe.wait_ge(s_const, 1)
            pe.wait_ge(s_w, 48)
            for n in range(3):
                pe.transpose(ps[:, 7, P * n:P * n + P], Wrows[:, n, :], ident[:, :])
            pe.transpose(ps[:, 7, 3 * P:3 * P + H], Wgr[:, :], ident[0:H, 0:H])
            pe.transpose(ps[:, 7, 3 * P + H:3 * P + H + NE], gwr[:, :], ident[0:NE, 0:NE]).then_inc(s_wT, 1)
            for b in range(B):
                turn_tensor(0, b)
                pe.wait_ge(s_xT, b + 1)
                if b == 0:
                    pe.wait_ge(s_wTc, 2)
                for n in range(2):
                    if b:
                        pe.wait_ge(s_qk, 2 * b - 1 + n)
                    pe.matmul(ps[:, 2 + n, :], WT[:, C * n:C * n + C], xT[:, T * b:T * b + T],
                              start=True, stop=True).then_inc(s_qkp, 1)
                if b:
                    pe.wait_ge(s_vz, 2 * b)
                for t in range(TB):
                    i = TB * b + t
                    ins = pe.matmul(ps[:, 4 + t // 2, 256 * (t % 2):256 * (t % 2) + C + H], xT[:, P * i:P * i + P],
                                    WT[:, 2 * C:3 * C + H], start=True, stop=True)
                ins.then_inc(s_vzp, 1)

        def gates_tensor():
            pe = nc.tensor
            pe.wait_ge(s_lg, 1)
            pe.wait_ge(s_const, 3)
            for b in range(B):
                for i in range(TB):
                    for n, (o, own) in enumerate(((0, True), (256, False))):
                        if i == 0 and not own:
                            continue
                        dst = ps[:, 6, o + H * (TB * b + i):o + H * (TB * b + i) + H]
                        terms = [(ones, j) for j in range(i)] + ([(tri, i)] if own else [])
                        for k, (m, j) in enumerate(terms):
                            ins = pe.matmul(dst, m[:, :], lg[:, TB * b + j, :], start=(k == 0), stop=(k == len(terms) - 1))
            ins.then_inc(s_gp, 1)
            pe.wait_ge(s_gt, 1)
            pe.wait_ge(s_qk, 2 * B)
            pe.wait_ge(s_xT, B)
            for b in range(B):
                for i in range(TB):
                    ins = pe.transpose(ps[0:H, b, P * i:P * i + P], Gt[:, b, i, :], ident[:, :])
                ins.then_inc(s_gTp, 1)

        def proj_scalar():
            a = nc.scalar
            a.wait_ge(s_wT, 1)
            a.activation(WT[:, :], ps[:, 7, 0:3 * C + H], ACT.Copy).then_inc(s_wTc, 1)
            a.activation(gwT[:, :], ps[:, 7, 3 * C + H:3 * C + H + NE], ACT.Copy).then_inc(s_wTc, 1)
            for b in range(B):
                turn_scalar(0, b)
                for n in range(2):
                    a.wait_ge(s_qkp, 2 * b + n + 1)
                    a.activation(qk[:, n, b, :], ps[:, 2 + n, :], ACT.Copy).then_inc(s_qk, 1)
                a.wait_ge(s_vzp, b + 1)
                a.wait_ge(s_const, 4)
                for t in range(0, TB, 2):
                    i = TB * b + t
                    src = ps[:, 4 + t // 2, :].rearrange("p (n c) -> p n c", n=2)
                    for k in range(2):
                        a.activation(va[:, i + k, :, 0:HS], src[:, k, 0:C].rearrange("p (h d) -> p h d", h=H), ACT.Copy)
                    a.activation(z[:, i:i + 2, :], src[:, :, C:C + H], ACT.Copy).then_inc(s_vz, 1)
            a.wait_ge(s_vz, 2 * B)
            link(a.activation(az[:], z[:], ACT.Abs), who="act")
            link(a.activation(az[:], az[:], ACT.Exp, scale=-1.0), who="act")
            a.activation(az[:], az[:], ACT.Ln, bias=1.0).then_inc(s_l, 1)
            a.wait_ge(s_dif, 1)
            a.activation(dec[:], dec[:], ACT.Exp).then_inc(s_exp, 1)
            a.activation(rowf[:, :, 1:TB, :], rowf[:, :, 1:TB, :], ACT.Exp).then_inc(s_exp, 1)

        def gates_vector():
            v = nc.vector
            v.wait_ge(s_l, 1)
            v.scalar_tensor_tensor(lg[:], z[:], 0.0, az[:], ALU.min, SUB).then_inc(s_lg, 1)
            v.wait_ge(s_gp, 1)
            link(v.tensor_copy(Gt[:].rearrange("p b t h -> p (b t h)"), ps[:, 6, 0:256]))
            v.tensor_copy(Ct[:, :, 1:TB, :], ps[:, 6, 256:512].rearrange("p (b t h) -> p b t h", b=B, t=TB)[:, :, 1:TB, :]).then_inc(s_gt, 1)
            v.wait_ge(s_gt, 1)
            n = 0
            for i in range(1, TB):
                v.tensor_tensor(dec[:, :, n:n + i, :], bc(Ct[:, :, i:i + 1, :], [P, B, i, H]), Gt[:, :, 0:i, :], SUB)
                n += i
            v.tensor_tensor(rowf[:, :, 1:TB, :], Gt[:, :, 1:TB, :], Ct[:, :, 1:TB, :], SUB).then_inc(s_dif, 1)
            for b in range(B):
                v.wait_ge(s_gTp, b + 1)
                v.tensor_copy(GT[:, b, :], ps[0:H, b, :]).then_inc(s_gT, 1)

        def bound_vector():
            v = nc.vector
            for b in range(B):
                for n in range(2):
                    v.wait_ge(s_qk, 2 * b + n + 1)
                    v.tensor_reduce(mx[:, b, n:n + 1], qk[:, n, b, :], AX.X, ALU.max, apply_absolute_value=True).then_inc(s_mx, 1)
            v.wait_ge(s_mxa, 1)
            link(v.tensor_scalar(mxa[:, :, :], mxa[:, :, :], 1e-8, None, MUL))
            link(v.tensor_tensor(fs[:, :], mxa[:, :, 0], mxa[:, :, 1], MUL))
            link(v.tensor_scalar(fs[:, :], fs[:, :], 1e-20, 1e30, ALU.max, ALU.min))
            link(v.reciprocal(fs[:, :], fs[:, :]))
            link(v.tensor_scalar(fs[:, :], fs[:, :], 1.25, 1.0, MUL, ALU.min))
            v.tensor_scalar(feps[:, :], fs[:, :], LOG_EPS, None, MUL).then_inc(s_fs, 1)

        def parts_vector(b):
            v = nc.vector
            if b >= 2:
                v.wait_ge(s_store, STORES * (b - 1))
            link(v.tensor_scalar(qk[:, 0, b, :], qk[:, 0, b, :], fs[:, b:b + 1], None, MUL))
            for n in range(2):
                p3 = part[:, b % 2, n]
                v.tensor_copy(p3[:, 0, :], qk[:, n, b, :]).then_inc(s_part, 1)
            v.wait_ge(s_part, 6 * b + 2)
            for n in range(2):
                ins = v.tensor_tensor(rest[:, n, :], qk[:, n, b, :], part[:, b % 2, n, 0, :], SUB)
            link(ins)
            for n in range(2):
                v.tensor_copy(part[:, b % 2, n, 1, :], rest[:, n, :]).then_inc(s_part, 1)
            v.wait_ge(s_part, 6 * b + 4)
            for n in range(2):
                v.tensor_tensor(part[:, b % 2, n, 2, :], rest[:, n, :], part[:, b % 2, n, 1, :], SUB).then_inc(s_part, 1)
            if b:
                v.wait_ge(s_store, STORES * b)
            v.wait_ge(s_gT, b + 1)
            link(v.tensor_copy(gp[:, 0, 0, :], GT[:, b, :]))
            link(v.tensor_tensor(gr[:, :], GT[:, b, :], gp[:, 0, 0, :], SUB))
            link(v.tensor_copy(gp[:, 0, 1, :], gr[:, :]))
            link(v.tensor_tensor(gp[:, 0, 2, :], gr[:, :], gp[:, 0, 1, :], SUB))
            v.tensor_scalar(gp[:, 1, :, :], gp[:, 0, :, :], -1.0, None, MUL).then_inc(s_gpart, 1)

        def decayed_pool(b):
            g = nc.gpsimd
            if b == 0:
                g.wait_ge(s_exp, 2)
                g.wait_ge(s_vz, 2 * B)
            if b >= 2:
                g.wait_ge(s_pv, UNITS * NG * (b - 1))
            slot, n = b % 2, 0
            for i in range(1, TB):
                for j in range(i):
                    g.tensor_tensor(vp[:, slot, n, :, :], va[:, TB * b + j, :, :],
                                    bc(dec[:, b, n, :].unsqueeze(2), [P, H, VW]), MUL).then_inc(s_vp, 1)
                    n += 1
            for j in range(TB):
                g.tensor_copy(vp[:, slot, NOFF + j, :, :], va[:, TB * b + j, :, :]).then_inc(s_vp, 1)

        def scores_tensor(G, u):
            pe = nc.tensor
            b, g = divmod(G, NG)
            n, half = 2 * b + g // 2, g % 2
            slot = n % 2
            kind, r = PLAN[u]
            U = UNITS * G + u
            if u == 0 and half == 0:
                pe.wait_ge(s_stack[slot], STACKS * (b + 1))
            if U >= 3:
                pe.wait_ge(s_A, U - 2)
            bank = ps[:, BK_S + U % 3, :]

            def block(col, width, r, j, t0):
                h = 4 * half + r
                return pe.matmul(bank[:, col:col + width], KS[0:96, slot, h, P * j:P * j + P],
                                 QS[0:96, slot, h, t0:t0 + width], start=True, stop=True)

            if kind == "diag":
                for j in range(TB):
                    ins = block(P * j, P, r, j, P * j)
            elif kind == "far":
                block(0, 384, r, 0, P)
                ins = block(384, P, r, 2, 3 * P)
            else:
                block(0, 256, r, 1, 2 * P)
                ins = block(256, 256, r + 1, 1, 2 * P)
            ins.then_inc(s_S, 1)
            if kind == "diag":
                hh = GH * G + r
                if hh >= 1:
                    pe.wait_ge(s_E, hh)
                h = 4 * half + r
                dst = ps[:, BK_D, :]
                for j in range(TB):
                    pe.matmul(dst[:, P * j:P * j + P], KS[96:102, slot, h, P * j:P * j + P], QS[96:102, slot, h, P * j:P * j + P],
                              start=(j == 0), stop=False, skip_group_check=True)
                pe.matmul(dst, identb[:, :], negmask[:, :, :].rearrange("p j t -> p (j t)"), start=False, stop=True,
                          skip_group_check=True).then_inc(s_D, 1)

        def sums_tensor(G, n):
            pe = nc.tensor
            b, g = divmod(G, NG)
            i, j = (OFF + [(k, k) for k in range(TB)])[n]
            if n == 0:
                pe.wait_ge(s_vp, len(PAIR) * (b + 1))
                pe.wait_ge(s_Q, UNITS * (G + 1))
                pe.wait_ge(s_PD, GH * (G + 1))
                if G:
                    pe.wait_ge(s_O, G)
            bank = BK_OFF if i != j else BK_DIA
            for r in range(GH):
                u, col = block_at(r, i, j)
                ins = pe.matmul(ps[32 * r:32 * r + VW, bank, P * i:P * i + P], vp[:, b % 2, n, GH * g + r, :],
                                PP[:, G % 2, u, col:col + P], start=(n in (0, NOFF)), stop=False, skip_group_check=True)
            ins.then_inc(s_pv, 1)

        def turn_sums_tensor(G):
            pe = nc.tensor
            pe.wait_ge(s_O, G + 1)
            if G:
                pe.wait_ge(s_Y, G)
            flat = ps[:, BK_T:BK_T + 2, :].rearrange("p a b -> p (a b)")
            for k in range(7):
                ins = pe.transpose(flat[:, P * k:P * k + P], OT[:, k, :], ident[:, :])
            ins.then_inc(s_OT, 1)

        def heads_tensor():
            pe = nc.tensor
            pe.wait_ge(s_gT, B)
            pe.wait_ge(s_vz, 2 * B)
            pe.wait_ge(s_zb, 2)
            pe.wait_ge(s_fill, 4)
            pe.wait_ge(s_const, 6)
            for G in range(GROUPS + 1):
                for u in range(UNITS):
                    if G < GROUPS:
                        scores_tensor(G, u)
                    if G:
                        sums_tensor(G - 1, u)
                    if u == 4 and G >= 2:
                        turn_sums_tensor(G - 2)
            turn_sums_tensor(GROUPS - 1)

        s_zb = sem("s_zb")

        def heads_vector():
            v = nc.vector
            v.wait_ge(s_vz, 2 * B)
            for k in (BK_OFF, BK_DIA):
                v.memset(ps[:, k, :], 0.0).then_inc(s_zb, 1)
            for G in range(GROUPS + 1):
                b, g = divmod(G, NG)
                for u in range(UNITS):
                    if G < GROUPS:
                        U = UNITS * G + u
                        v.wait_ge(s_S, U + 1)
                        if U >= 4:
                            v.wait_ge(s_Q, U - 3)
                        v.tensor_scalar(A[:, U % 4, :].bitcast(I32), ps[:, BK_S + U % 3, :].bitcast(I32),
                                        0x7fffffff, None, ALU.bitwise_and).then_inc(s_A, 1)
                    if u == 8 and G >= 2:
                        combine_vector(G - 2)
                if g == 0 and 1 <= b < B - 1:
                    parts_vector(b + 1)
            combine_vector(GROUPS - 1)

        def combine_vector(G):
            v = nc.vector
            b, g = divmod(G, NG)
            v.wait_ge(s_OT, G + 1)
            flat = ps[:, BK_T:BK_T + 2, :].rearrange("p a b -> p (a b)").rearrange("p (k r c) -> p k r c", r=GH, c=32)[:, 0:7, :, 0:VW]
            hs = slice(GH * g, GH * g + GH)
            link(v.tensor_tensor(tmp[:], flat[:, 0:3, :, :], bc(rowf[:, b, 1:TB, hs].unsqueeze(3), [P, 3, GH, VW]), MUL))
            link(v.tensor_copy(YS[:, 0, hs, :], flat[:, 3, :, :]))
            v.tensor_tensor(YS[:, 1:TB, hs, :], flat[:, 4:7, :, :], tmp[:], ADD).then_inc(s_Y, 1)
            v.wait_ge(s_Y, G + 1)
            if g == NG - 1:
                link(v.reciprocal(rn[:, :, :], YS[:, :, :, HS]))
                link(v.tensor_tensor(YS[:, :, :, 0:HS], YS[:, :, :, 0:HS], bc(rn[:, :, :].unsqueeze(3), [P, TB, H, HS]), MUL))
                xb = xt[:, TB * b:TB * b + TB, :].rearrange("p t (h d) -> p t h d", h=H)
                v.tensor_tensor(xb, xb, YS[:, :, :, 0:HS], ADD).then_inc(s_xa, 1)
                v.wait_ge(s_xa, b + 1)

        def square_scalar(G, u):
            a = nc.scalar
            b = G // NG
            U = UNITS * G + u
            a.wait_ge(s_A, U + 1)
            if G >= 2 and u == 0:
                a.wait_ge(s_pv, UNITS * (G - 1))
            a.activation(PP[:, G % 2, u, :], A[:, U % 4, :], ACT.Square, bias=feps[:, b:b + 1]).then_inc(s_Q, 1)

        def gate_scalar(G, r):
            a = nc.scalar
            hh = GH * G + r
            a.wait_ge(s_D, hh + 1)
            if hh >= 4:
                a.wait_ge(s_PD, hh - 3)
            a.activation(E[:, hh % 4, :], ps[:, BK_D, :], ACT.Exp).then_inc(s_E, 1)

        def take_sums_scalar(G):
            a = nc.scalar
            a.wait_ge(s_pv, UNITS * (G + 1))
            if G:
                a.wait_ge(s_OT, G)
            a.activation(OT[:, 0:3, :].rearrange("p k t -> p (k t)"), ps[:, BK_OFF, P:512], ACT.Copy)
            a.activation(OT[:, 3:7, :].rearrange("p k t -> p (k t)"), ps[:, BK_DIA, :], ACT.Copy).then_inc(s_O, 1)

        def heads_scalar():
            a = nc.scalar
            a.wait_ge(s_fs, 1)
            for G in range(GROUPS):
                if G >= 2:
                    take_sums_scalar(G - 2)
                for u in range(UNITS):
                    if PLAN[u][0] == "diag":
                        gate_scalar(G, PLAN[u][1])
                    square_scalar(G, u)
            take_sums_scalar(GROUPS - 2)
            take_sums_scalar(GROUPS - 1)

        def heads_pool():
            g = nc.gpsimd
            for G in range(GROUPS):
                for r in range(GH):
                    u = PLAN.index(("diag", r))
                    hh = GH * G + r
                    g.wait_ge(s_E, hh + 1)
                    g.wait_ge(s_Q, UNITS * G + u + 1)
                    w = PP[:, G % 2, u, :]
                    g.tensor_tensor(w, w, E[:, hh % 4, :], MUL).then_inc(s_PD, 1)
                if G % NG == 1 and G // NG + 1 < B:
                    decayed_pool(G // NG + 1)

        att.close()

        w13 = sb("w13", [P, NE, 2, HID])
        w2s = sb("w2s", [P, NE, len(HC), C])
        L8 = sb("L8", [P, NT, NE])
        V8 = sb("V8", [P, NT, NE])
        Q8 = sb("Q8", [P, NT, NE])
        oh = sb("oh", [P, TOPK, NT, NE])
        m1 = sb("m1", [P, NT])
        m2 = sb("m2", [P, NT])
        wts = sb("wts", [P, TOPK, NT])
        chosen = sb("chosen", [P, NT, NE], BF16)
        totE = sb("totE", [P, NE, NT])
        cumE = sb("cumE", [P, NE, NT])
        base = sb("base", [P, NT, NE])
        tiles = sb("tiles", [P, NE])
        ends = sb("ends", [P, NE])
        first = sb("first", [P, NE])
        cmp16 = sb("cmp16", [P, NE, NT])
        cmp40 = sb("cmp40", [P, JOBS, NE])
        slotf = sb("slotf", [P, TOPK, NT])
        slots = sb("slots", [P, TOPK, NT], U32)
        jobf = sb("jobf", [P, JOBS])
        job_expert = sb("job_expert", [P, JOBS], I32)
        xs = sb("xs", [P, TOPK, NT, C])
        rows = sb("rows", [P, 4, C])
        rowsT = sb("rowsT", [P, 2, P])
        silu = sb("silu", [P, 2, HID])
        hid = sb("hid", [P, 2, HID])
        hidT = sb("hidT", [P, 2, len(HC), P])
        ysb = sb("ysb", [P, 4, C])

        s_ww = sem("s_ww")
        s_lgp = sem("s_lgp")
        s_rd = sem("s_rd")
        s_re = sem("s_re")
        s_M = sem("s_M")
        s_rank = sem("s_rank")
        s_slot = sem("s_slot")
        s_job = sem("s_job")
        s_scat = sem("s_scat")
        s_row = [sem(f"s_row{k}") for k in range(4)]
        s_rTp = sem("s_rTp")
        s_rT = sem("s_rT")
        s_AB = sem("s_AB")
        s_silu = sem("s_silu")
        s_hid = sem("s_hid")
        s_hTp = sem("s_hTp")
        s_hT = sem("s_hT")
        s_yp = sem("s_yp")
        s_y = sem("s_y")
        s_yst = [sem(f"s_yst{k}") for k in range(4)]
        s_gat = [sem(f"s_gat{k}") for k in range(B)]
        s_xm = sem("s_xm")
        PJ = JOBS // 4

        def weights_sync():
            sp = nc.sync
            sp.wait_ge(s_xa, B)
            sp.dma_start(w13[:, :, 0, :], w1.rearrange("e c h -> c e h")).then_inc(s_ww, 16)
            sp.dma_start(w13[:, :, 1, :], w3.rearrange("e c h -> c e h")).then_inc(s_ww, 16)
            for k, (h0, hw) in enumerate(HC):
                sp.dma_start(w2s[0:hw, :, k, :], w2[:, h0:h0 + hw, :].rearrange("e p c -> p e c")).then_inc(s_ww, 16)

        def route_tensor(n):
            pe = nc.tensor
            for c in range(4):
                turn_tensor(1 + 2 * n, c)
            pe.wait_ge(s_xT, 4 * (2 + 2 * n))
            for i in range(NT):
                ins = pe.matmul(ps[:, 7, NE * i:NE * i + NE], xT[:, P * i:P * i + P], gwT[:, :], start=True, stop=True)
            ins.then_inc(s_lgp, 1)
            pe.wait_ge(s_M, n + 1)
            if n == 0:
                pe.wait_ge(s_const, NCONST)
            flat = chosen[:].rearrange("p t e -> p (t e)")
            pe.matmul(ps[:, 6, 0:P], trib[:, :], flat, start=True, stop=True)
            pe.matmul(ps[:, 6, P:2 * P], onesb[:, :], flat, start=True, stop=True).then_inc(s_rank, 1)

        def route_scalar(n):
            a = nc.scalar
            norm_scalar(1 + 2 * n)
            for c in range(4):
                turn_scalar(1 + 2 * n, c)
            a.wait_ge(s_rd, n + 1)
            a.activation(L8[:], L8[:], ACT.Exp).then_inc(s_re, 1)

        def route_vector(n):
            v = nc.vector

            def e8(ap):
                return bc(ap.unsqueeze(2), [P, NT, NE])

            v.wait_ge(s_lgp, n + 1)
            lgt = ps[:, 7, 0:P].rearrange("p (t e) -> p t e", e=NE)
            link(v.tensor_reduce(m1[:, :], lgt, AX.X, ALU.max))
            v.tensor_tensor(L8[:], lgt, e8(m1[:, :]), SUB).then_inc(s_rd, 1)
            v.wait_ge(s_re, n + 1)
            link(v.tensor_reduce(m1[:, :], L8[:], AX.X, ADD))
            link(v.reciprocal(m1[:, :], m1[:, :]))
            link(v.tensor_tensor(L8[:], L8[:], e8(m1[:, :]), MUL))
            link(v.tensor_tensor(V8[:], L8[:], bc(ebt[:, :].unsqueeze(1), [P, NT, NE]), ADD))
            for k in range(TOPK):
                link(v.tensor_reduce(m1[:, :], V8[:], AX.X, ALU.max))
                link(v.tensor_tensor(Q8[:], V8[:], e8(m1[:, :]), ALU.is_equal))
                link(v.tensor_tensor(Q8[:], Q8[:], bc(iom8[:, :].unsqueeze(1), [P, NT, NE]), MUL))
                link(v.tensor_reduce(m2[:, :], Q8[:], AX.X, ALU.min))
                link(v.tensor_tensor(oh[:, k], bc(iom8[:, :].unsqueeze(1), [P, NT, NE]), e8(m2[:, :]), ALU.is_equal))
                link(v.tensor_tensor(Q8[:], oh[:, k], L8[:], MUL))
                link(v.tensor_reduce(wts[:, k, :], Q8[:], AX.X, ADD))
                if k == 0:
                    link(v.scalar_tensor_tensor(V8[:], oh[:, 0], NEG, V8[:], MUL, ADD))
            v.tensor_tensor(chosen[:], oh[:, 0], oh[:, 1], ADD).then_inc(s_M, 1)
            if n:
                v.wait_ge(s_xm, B * n)
            for k in range(TOPK):
                ins = v.tensor_tensor(xs[:, k], xh[:, :, :], bc(wts[:, k, :].unsqueeze(2), [P, NT, C]), MUL)
            link(ins)
            v.wait_ge(s_rank, n + 1)
            rank = ps[:, 6, 0:P].rearrange("p (t e) -> p t e", e=NE)
            tot = ps[:, 6, P:2 * P].rearrange("p (t e) -> p e t", e=NE)
            link(v.tensor_copy(totE[:], tot))
            link(v.tensor_tensor_scan(cumE[:].rearrange("p e t -> p (e t)"), carry1[:].rearrange("p e t -> p (e t)"),
                                      totE[:].rearrange("p e t -> p (e t)"), 0.0, MUL, ADD))
            link(v.tensor_tensor(cmp16[:], bc(cumE[:, :, NT - 1:NT], [P, NE, NT]), bc(io128[:, :].unsqueeze(1), [P, NE, NT]), ALU.is_gt))
            link(v.tensor_reduce(tiles[:, :], cmp16[:], AX.X, ADD))
            link(v.tensor_tensor_scan(ends[:, :], ones[:, 0:NE], tiles[:, :], 0.0, MUL, ADD))
            link(v.tensor_tensor(first[:, :], ends[:, :], tiles[:, :], SUB))
            link(v.tensor_scalar(first[:, :], first[:, :], float(P), None, MUL))
            link(v.tensor_tensor(cumE[:], cumE[:], totE[:], SUB))
            link(v.tensor_tensor(base[:].rearrange("p t e -> p e t"), cumE[:], bc(first[:, :].unsqueeze(2), [P, NE, NT]), ADD))
            link(v.tensor_tensor(base[:], base[:], rank, ADD))
            for k in range(TOPK):
                link(v.tensor_tensor(Q8[:], oh[:, k], base[:], MUL))
                link(v.tensor_reduce(slotf[:, k, :], Q8[:], AX.X, ADD))
            v.tensor_copy(slots[:], slotf[:]).then_inc(s_slot, 1)
            link(v.tensor_tensor(cmp40[:], bc(io40[:, :].unsqueeze(2), [P, JOBS, NE]), bc(ends[:, :].unsqueeze(1), [P, JOBS, NE]), ALU.is_ge))
            link(v.tensor_reduce(jobf[:, :], cmp40[:], AX.X, ADD))
            link(v.tensor_scalar(jobf[:, :], jobf[:, :], float(NE - 1), None, ALU.min))
            v.tensor_copy(job_expert[:, :], jobf[:, :]).then_inc(s_job, 1)

        def scatter_pool(n):
            g = nc.gpsimd
            g.wait_ge(s_slot, n + 1)
            g.wait_ge(s_zero, 128)
            for i in range(NT):
                for k in range(TOPK):
                    g.indirect_dma_start(xr, bass.IndirectOffsetOnAxis(ap=slots[:, k, i:i + 1], axis=0),
                                         xs[:, k, i, :], None).then_inc(s_scat, 16)

        def gather_pool(n):
            g = nc.gpsimd
            for k in range(4):
                g.wait_ge(s_yst[k], 16 * PJ * (n + 1))
            g.wait_ge(s_scat, 16 * TOPK * NT * (n + 1))
            for i in range(NT):
                for k in range(TOPK):
                    g.indirect_dma_start(xs[:, k, i, :], None, yr,
                                         bass.IndirectOffsetOnAxis(ap=slots[:, k, i:i + 1], axis=0)).then_inc(s_gat[i // TB], 16)

        def add_vector(n):
            v = nc.vector
            for b in range(B):
                t = slice(TB * b, TB * b + TB)
                v.wait_ge(s_gat[b], 16 * TOPK * TB * (n + 1))
                link(v.tensor_tensor(xs[:, 0, t, :], xs[:, 0, t, :], xs[:, 1, t, :], ADD))
                v.tensor_tensor(xt[:, t, :], xt[:, t, :], xs[:, 0, t, :], ADD).then_inc(s_xm, 1)
            v.wait_ge(s_xm, B * (n + 1))

        def looped(eng, step, lo, hi, last):
            for s in range(4 * lo):
                step(s // 4, s % 4, s)
            with eng.Fori(lo, hi) as q:
                for k in range(4):
                    step(q, k, None)
            for s in range(4 * hi, last + 1):
                step(s // 4, s % 4, s)

        def jobs_sync(n):
            sp = nc.sync
            sp.wait_ge(s_scat, 16 * TOPK * NT * (n + 1))

            def load(q, k):
                sp.wait_ge(s_rTp, JOBS * n + 4 * q + k - 3)
                sp.dma_start(rows[:, k, :], xr[bass.ds((4 * q + k) * P, P), :]).then_inc(s_row[k], 16)

            def store(q, k):
                sp.wait_ge(s_y, JOBS * n + 4 * q + k + 1)
                sp.dma_start(yr[bass.ds((4 * q + k) * P, P), :], ysb[:, k, :]).then_inc(s_yst[k], 16)

            def step(q, k, s):
                if s is None or s < JOBS:
                    if s is None or n or s >= 4:
                        load(q, k)
                    else:
                        sp.dma_start(rows[:, k, :], xr[P * k:P * k + P, :]).then_inc(s_row[k], 16)
                if s is None or s >= 6:
                    store(*((q - 2, k + 2) if k < 2 else (q - 1, k - 2)))

            looped(sp, step, 2, PJ, JOBS + 5)

        def jobs_tensor(n):
            pe = nc.tensor
            pe.wait_ge(s_job, n + 1)
            if n == 0:
                pe.wait_ge(s_ww, 16 * 5)

            def turn(q, k):
                J = JOBS * n + 4 * q + k
                pe.wait_ge(s_row[k], 16 * (PJ * n + q + 1))
                if n or not isinstance(J, int) or J >= 1:
                    pe.wait_ge(s_rT, J)
                pe.transpose(ps[:, 6, 0:P], rows[:, k, :], ident[:, :]).then_inc(s_rTp, 1)

            def up(q, k):
                e = pe.value_load(job_expert[0:1, bass.ds(4 * q + k, 1)], min_val=0, max_val=NE - 1)
                J = JOBS * n + 4 * q + k
                pe.wait_ge(s_rT, J + 1)
                if n or not isinstance(J, int) or J >= 2:
                    pe.wait_ge(s_hid, J - 1)
                for m in range(2):
                    ins = pe.matmul(ps[:, 2 * (k % 2) + m, 0:HID], rowsT[:, k % 2, :], w13[:, bass.ds(e, 1), m, :].squeeze(1),
                                    start=True, stop=True)
                ins.then_inc(s_AB, 1)

            def turn_hidden(q, k):
                J = JOBS * n + 4 * q + k
                pe.wait_ge(s_hid, J + 1)
                if n or not isinstance(J, int) or J >= 2:
                    pe.wait_ge(s_hT, J - 1)
                for c, (h0, hw) in enumerate(HC):
                    ins = pe.transpose(ps[0:hw, 4 + k % 2, P * c:P * c + P], hid[:, k % 2, h0:h0 + hw], ident[:, :])
                ins.then_inc(s_hTp, 1)

            def down(q, k):
                e = pe.value_load(job_expert[0:1, bass.ds(4 * q + k, 1)], min_val=0, max_val=NE - 1)
                J = JOBS * n + 4 * q + k
                pe.wait_ge(s_hT, J + 1)
                if n or not isinstance(J, int) or J >= 1:
                    pe.wait_ge(s_y, J)
                for c, (h0, hw) in enumerate(HC):
                    ins = pe.matmul(ps[:, 7, 0:P], hidT[0:hw, k % 2, c, :], w2s[0:hw, bass.ds(e, 1), c, :].squeeze(1),
                                    start=(c == 0), stop=(c == len(HC) - 1))
                ins.then_inc(s_yp, 1)

            def before(q, k, d):
                return (q, k - d) if k >= d else (q - 1, k + 4 - d)

            def step(q, k, s):
                if s is None or s < JOBS:
                    up(q, k)
                if s is None or s < JOBS - 1:
                    turn(*((q, k + 1) if k < 3 else (q + 1, 0)))
                if s is None or 1 <= s <= JOBS:
                    turn_hidden(*before(q, k, 1))
                if s is None or 2 <= s:
                    down(*before(q, k, 2))

            turn(0, 0)
            looped(pe, step, 1, PJ - 1, JOBS + 1)

        def jobs_scalar(n):
            a = nc.scalar

            def gate(q, k):
                J = JOBS * n + 4 * q + k
                a.wait_ge(s_AB, J + 1)
                if n or not isinstance(J, int) or J >= 2:
                    a.wait_ge(s_hid, J - 1)
                a.activation(silu[:, k % 2, :], ps[:, 2 * (k % 2), 0:HID], ACT.Silu).then_inc(s_silu, 1)

            def take_hidden(q, k):
                J = JOBS * n + 4 * q + k
                a.wait_ge(s_hTp, J + 1)
                if n or not isinstance(J, int) or J >= 2:
                    a.wait_ge(s_yp, J - 1)
                a.activation(hidT[:, k % 2, 0:2, :].rearrange("p c t -> p (c t)"), ps[:, 4 + k % 2, 0:2 * P], ACT.Copy)
                a.activation(hidT[0:96, k % 2, 2, :], ps[0:96, 4 + k % 2, 2 * P:3 * P], ACT.Copy).then_inc(s_hT, 1)

            def step(q, k, s):
                if s is None or s < JOBS:
                    gate(q, k)
                if s is None or s >= 1:
                    take_hidden(*((q, k - 1) if k else (q - 1, 3)))

            looped(a, step, 1, PJ, JOBS)

        def jobs_vector(n):
            v = nc.vector

            def take_rows(q, k):
                J = JOBS * n + 4 * q + k
                v.wait_ge(s_rTp, J + 1)
                if n or not isinstance(J, int) or J >= 2:
                    v.wait_ge(s_AB, J - 1)
                v.tensor_copy(rowsT[:, k % 2, :], ps[:, 6, 0:P]).then_inc(s_rT, 1)

            def mix(q, k):
                J = JOBS * n + 4 * q + k
                v.wait_ge(s_silu, J + 1)
                if n or not isinstance(J, int) or J >= 2:
                    v.wait_ge(s_hTp, J - 1)
                v.tensor_tensor(hid[:, k % 2, :], silu[:, k % 2, :], ps[:, 2 * (k % 2) + 1, 0:HID], MUL).then_inc(s_hid, 1)

            def take_out(q, k):
                J = JOBS * n + 4 * q + k
                v.wait_ge(s_yp, J + 1)
                if n or not isinstance(J, int) or J >= 4:
                    v.wait_ge(s_yst[k], 16 * (PJ * n + q))
                v.tensor_copy(ysb[:, k, :], ps[:, 7, 0:P]).then_inc(s_y, 1)

            def step(q, k, s):
                if s is None or s < JOBS - 1:
                    take_rows(*((q, k + 1) if k < 3 else (q + 1, 0)))
                if s is None or s < JOBS:
                    mix(q, k)
                if s is None or s >= 2:
                    take_out(*((q, k - 2) if k >= 2 else (q - 1, k + 2)))

            take_rows(0, 0)
            looped(v, step, 1, PJ - 1, JOBS + 1)

        win = sb("win", [P, 3, C])
        wout = sb("wout", [P, C])
        cw = sb("cw", [P, 2, CONV_K])
        gn = sb("gn", [P, 1])
        cv = sb("cv", [P, 2, 2, T])
        sg = sb("sg", [P, 2, 4, T])
        gi = sb("gi", [P, 2, T])
        rec = sb("rec", [P, 2, T])
        gg = sb("gg", [P, 2, T])
        osq = sb("osq", [P, 2, T])
        og = sb("og", [P, 2, T])
        osb = sb("osb", [P, NT, C])
        rms = sb("rms", [P, NT])

        s_wh = sem("s_wh")
        s_raw = sem("s_raw")
        s_tap = sem("s_tap")
        s_cv = sem("s_cv")
        s_sig = sem("s_sig")
        s_gi = sem("s_gi")
        s_rec = sem("s_rec")
        s_gg = sem("s_gg")
        s_osq = sem("s_osq")
        s_og = sem("s_og")
        s_ho = sem("s_ho")
        s_osb = sem("s_osb")
        s_ms = sem("s_ms")
        s_rt = sem("s_rt")
        s_xr = sem("s_xr")

        def rec_sync():
            sp = nc.sync
            for k, w in enumerate((Wi, Wf, Wg)):
                sp.dma_start(win[:, k, :], w).then_inc(s_wh, 16)
            sp.dma_start(wout[:, :], Wo).then_inc(s_wh, 16)
            sp.dma_start(cw[:, 0, :], conv_i).then_inc(s_wh, 16)
            sp.dma_start(cw[:, 1, :], conv_f).then_inc(s_wh, 16)
            sp.dma_start(gn[:, :], gnw.rearrange("(d a) -> d a", a=1)).then_inc(s_wh, 16)

        def raw_bank(b, k):
            return ps[:, 6 if k == 2 else 2 + k, :]

        def rec_tensor():
            pe = nc.tensor
            pe.wait_ge(s_wh, 16 * 7)

            def project(b):
                pe.wait_ge(s_xT, 8 + b + 1)
                if b:
                    pe.wait_ge(s_gg, b)
                    pe.wait_ge(s_cv, 2 * b)
                for k in range(3):
                    pe.matmul(raw_bank(b, k), win[:, k, :], xT[:, T * b:T * b + T], start=True, stop=True).then_inc(s_raw, 1)

            def finish(b):
                pe.wait_ge(s_og, b + 1)
                pe.wait_ge(s_osq, b + 1)
                if b >= 2:
                    pe.wait_ge(s_osb, b - 1)
                for t in range(TB):
                    pe.matmul(ps[:, 4 + b % 2, P * t:P * t + P], og[:, b % 2, P * t:P * t + P], wout[:, :], start=True, stop=True)
                for t in range(TB):
                    i = TB * b + t
                    ins = pe.matmul(ps[:, 7, i:i + 1], osq[:, b % 2, P * t:P * t + P], ones[:, 0:1], start=True, stop=True)
                ins.then_inc(s_ho, 1)

            for b in range(B):
                turn_tensor(2, b)
                project(b)
                if b:
                    finish(b - 1)
            finish(B - 1)

        def rec_scalar():
            a = nc.scalar
            norm_scalar(2)
            for b in range(B):
                turn_scalar(2, b)
                for k in range(2):
                    a.wait_ge(s_raw, 3 * b + k + 1)
                    if b >= 2 and k == 0:
                        a.wait_ge(s_gi, b - 1)
                    a.activation(cv[:, b % 2, k, :], raw_bank(b, k), ACT.Identity,
                                 scale=cw[:, k, CONV_K - 1:CONV_K]).then_inc(s_tap, 1)
                a.wait_ge(s_raw, 3 * b + 3)
                if b >= 2:
                    a.wait_ge(s_gg, b - 1)
                    a.wait_ge(s_rec, b - 1)
                a.activation(sg[:, b % 2, 3, :], raw_bank(b, 2), ACT.Sigmoid).then_inc(s_sig, 1)
                a.wait_ge(s_cv, 2 * b + 2)
                a.activation(sg[:, b % 2, 2, :], cv[:, b % 2, 0, :], ACT.Sigmoid).then_inc(s_sig, 1)
                a.activation(sg[:, b % 2, 1, :], cv[:, b % 2, 1, :], ACT.Sigmoid, scale=-1.0).then_inc(s_sig, 1)
                a.activation(sg[:, b % 2, 0, :], cv[:, b % 2, 1, :], ACT.Sigmoid).then_inc(s_sig, 1)
                a.wait_ge(s_rec, b + 1)
                if b >= 2:
                    a.wait_ge(s_ho, b - 1)
                a.activation(osq[:, b % 2, :], rec[:, b % 2, :], ACT.Square).then_inc(s_osq, 1)
                if b:
                    take_out_scalar(b - 1)
            take_out_scalar(B - 1)
            a.wait_ge(s_ms, 1)
            a.activation(lns[:, :], lnv[:, :], ACT.Sqrt).then_inc(s_rt, 1)

        def take_out_scalar(b):
            nc.scalar.wait_ge(s_ho, b + 1)
            nc.scalar.activation(osb[:, TB * b:TB * b + TB, :].rearrange("p t c -> p (t c)"), ps[:, 4 + b % 2, :], ACT.Copy).then_inc(s_osb, 1)

        def rec_vector():
            v = nc.vector
            v.wait_ge(s_wh, 16 * 7)
            for b in range(B):
                for k in range(2):
                    v.wait_ge(s_tap, 2 * b + k + 1)
                    for tap in range(CONV_K - 1):
                        d = CONV_K - 1 - tap
                        acc = cv[:, b % 2, k, d:T]
                        ins = v.scalar_tensor_tensor(acc, raw_bank(b, k)[:, 0:T - d], cw[:, k, tap:tap + 1], acc, MUL, ADD)
                        if tap < CONV_K - 2:
                            link(ins)
                    ins.then_inc(s_cv, 1)
                v.wait_ge(s_sig, 4 * b + 1)
                if b >= 2:
                    v.wait_ge(s_og, b - 1)
                v.scalar_tensor_tensor(gg[:, b % 2, :], raw_bank(b, 2), gn[:, 0:1], sg[:, b % 2, 3, :], MUL, MUL).then_inc(s_gg, 1)
                v.wait_ge(s_sig, 4 * b + 4)
                v.wait_ge(s_cv, 2 * b + 2)
                link(v.tensor_tensor(gi[:, b % 2, :], cv[:, b % 2, 0, :], sg[:, b % 2, 2, :], MUL))
                v.tensor_tensor(gi[:, b % 2, :], gi[:, b % 2, :], sg[:, b % 2, 1, :], MUL).then_inc(s_gi, 1)
                v.wait_ge(s_gi, b + 1)
                if b >= 2:
                    v.wait_ge(s_osq, b - 1)
                v.tensor_tensor_scan(rec[:, b % 2, :], sg[:, b % 2, 0, :], gi[:, b % 2, :], 0.0, MUL, ADD).then_inc(s_rec, 1)
            v.wait_ge(s_ho, B)
            v.tensor_scalar(lnv[:, :], ps[:, 7, 0:NT], 1.0 / C, LN_EPS, MUL, ADD).then_inc(s_ms, 1)
            v.wait_ge(s_ms, 1)
            v.wait_ge(s_rt, 1)
            link(v.reciprocal(rms[:, :], lns[:, :]))
            newton(rms, lnv, lnt)
            v.wait_ge(s_osb, B)
            for i in range(NT):
                v.scalar_tensor_tensor(xt[:, i, :], osb[:, i, :], rms[:, i:i + 1], xt[:, i, :], MUL, ADD).then_inc(s_xr, 1)
            v.wait_ge(s_xr, NT)

        def rec_pool():
            g = nc.gpsimd
            for b in range(B):
                g.wait_ge(s_gg, b + 1)
                g.wait_ge(s_rec, b + 1)
                if b >= 2:
                    g.wait_ge(s_ho, b - 1)
                g.tensor_tensor(og[:, b % 2, :], rec[:, b % 2, :], gg[:, b % 2, :], MUL).then_inc(s_og, 1)

        block = ctx.enter_context(nc.Block())

        @block.sync
        def _(sp):
            proj_sync()
            sp.wait_ge(s_fill, 4)
            for n in range(2 * B):
                stack_sync(n)
                if n == 1:
                    clear_sync()
            weights_sync()
            rec_sync()
            jobs_sync(0)
            jobs_sync(1)
            for b in range(B):
                sp.wait_ge(s_xm, B + b + 1)
                sp.dma_start(out_rows[:, TB * b:TB * b + TB, :], xt[:, TB * b:TB * b + TB, :]).then_inc(s_out, 16)
            sp.wait_ge(s_out, 16 * B)

        @block.gpsimd
        def _(g):
            const_pool()
            heads_pool()
            scatter_pool(0)
            gather_pool(0)
            rec_pool()
            scatter_pool(1)
            gather_pool(1)

        @block.scalar
        def _(a):
            norm_scalar(0)
            proj_scalar()
            heads_scalar()
            route_scalar(0)
            jobs_scalar(0)
            rec_scalar()
            route_scalar(1)
            jobs_scalar(1)

        @block.tensor
        def _(pe):
            proj_tensor()
            gates_tensor()
            heads_tensor()
            route_tensor(0)
            jobs_tensor(0)
            rec_tensor()
            route_tensor(1)
            jobs_tensor(1)

        @block.vector
        def _(v):
            stacks_vector()
            norm_vector(0, lambda: v.wait_ge(s_x, 64))
            bound_vector()
            gates_vector()
            parts_vector(0)
            parts_vector(1)
            heads_vector()
            norm_vector(1, lambda: v.wait_ge(s_xa, B))
            v.wait_ge(s_eb, 16)
            route_vector(0)
            jobs_vector(0)
            add_vector(0)
            norm_vector(2, lambda: v.wait_ge(s_xm, B))
            rec_vector()
            norm_vector(3, lambda: v.wait_ge(s_xr, NT))
            route_vector(1)
            jobs_vector(1)
            add_vector(1)


_INS = ['L0_attn_a_x', 'L0_attn_a_W', 'L0_attn_b_Wi', 'L0_attn_b_Wf', 'L0_attn_b_Wg', 'L0_attn_b_conv_i',
        'L0_attn_b_conv_f', 'L0_attn_b_g_norm_weight', 'L0_attn_b_Wo', 'L0_ffn_gate_w', 'L0_ffn_expert_bias',
        'L0_ffn_w1', 'L0_ffn_w2', 'L0_ffn_w3']


def kernel(**inputs):
    import numpy as _np
    import concourse.bacc as _bacc
    from concourse import mybir as _mybir
    from concourse.bass_utils import run_bass_kernel_spmd as _run

    nc = _bacc.Bacc("TRN2", target_bir_lowering=False, num_devices=1)
    arrays, args = {}, []
    for name in _INS:
        a = _np.ascontiguousarray(inputs[name])
        arrays[f"in_{name}_dram"] = a
        args.append(nc.dram_tensor(f"in_{name}_dram", a.shape, _mybir.dt.from_np(a.dtype), kind="ExternalInput").ap())
    args.append(nc.dram_tensor("out_0_dram", (B, T, C), F32, kind="ExternalOutput").ap())
    build(nc, *args)
    r = _run(nc, [arrays], core_ids=[0])
    return r.results[0]["out_0_dram"]
```

```python
from contextlib import ExitStack

import concourse.bass as bass
from concourse import mybir

F32 = mybir.dt.float32
BF16 = mybir.dt.bfloat16
I32 = mybir.dt.int32
U32 = mybir.dt.uint32
ALU = mybir.AluOpType
ACT = mybir.ActivationFunctionType
AX = mybir.AxisListType
ADD, SUB, MUL = ALU.add, ALU.subtract, ALU.mult

P = 128
B, T, C = 4, 512, 128
NT = B * T // P
TB = T // P
H, HS = 16, 8
VW = HS + 1
GH = 4
NG = H // GH
GROUPS = B * NG
NE, HID = 8, 352
HC = [(0, 128), (128, 128), (256, 96)]
HP = P * len(HC)
TOPK = 2
HT = NT // 2
JOBS = 24
LN_EPS = 1e-5
LOG_EPS = 1e-7
CONV_K = 4
NEG = -1e30

OFF = [(i, j) for i in range(1, TB) for j in range(i)]
PAIR = {ij: n for n, ij in enumerate(OFF + [(j, j) for j in range(TB)])}
NOFF = len(OFF)
UNITS = 10


def unit_plan():
    plan = []
    for r in range(0, GH, 2):
        plan += [("diag", r), ("far", r), ("diag", r + 1), ("far", r + 1), ("mid", r)]
    return plan


PLAN = unit_plan()


def block_at(r, i, j):
    if i == j:
        return PLAN.index(("diag", r)), P * j
    if j == 1:
        return PLAN.index(("mid", r - r % 2)), 256 * (r % 2) + P * (i - 2)
    u = PLAN.index(("far", r))
    return (u, P * (i - 1)) if j == 0 else (u, 384)


def build(nc, x, W, Wi, Wf, Wg, conv_i, conv_f, gnw, Wo, gate_w, ebias, w1, w2, w3, out):
    x_rows = x.rearrange("b (t p) c -> p (b t) c", p=P)
    out_rows = out.rearrange("b (t p) c -> p (b t) c", p=P)
    xr = [nc.dram_tensor(f"routed_rows{hf}", [JOBS * P, C], F32, kind="Internal").ap() for hf in range(2)]
    parts_d = nc.dram_tensor("parts", [2, 2, H, 5, HS, T], BF16, kind="Internal").ap()
    gates_d = nc.dram_tensor("gates", [2, 2, H, 3, T], BF16, kind="Internal").ap()
    yr = [nc.dram_tensor(f"routed_out{hf}", [JOBS * P, C], F32, kind="Internal").ap() for hf in range(2)]

    with ExitStack() as ctx:
        def sb(name, shape, dt=F32):
            return ctx.enter_context(nc.sbuf_tensor(name, shape, dt))

        def sem(name):
            return ctx.enter_context(nc.semaphore(name))

        ps = ctx.enter_context(nc.psum_tensor("ps", [P, 8, 512], F32))

        ident = sb("ident", [P, P])
        identb = sb("identb", [P, P], BF16)
        tri = sb("tri", [P, P])
        ones = sb("ones", [P, P])
        trib = sb("trib", [P, P], BF16)
        onesb = sb("onesb", [P, P], BF16)
        negmask = sb("negmask", [P, TB, P], BF16)
        iom8 = sb("iom8", [P, NE])
        iojob = sb("iojob", [P, JOBS])
        io128 = sb("io128", [P, HT])
        carry1 = sb("carry1", [P, NE, HT])
        zeros = sb("zeros", [P, C])
        mhalf = sb("mhalf", [P, HT])
        ebt = sb("ebt", [P, NE])
        WT = sb("WT", [P, 3 * C + H])
        gwT = sb("gwT", [P, NE])
        xt = sb("xt", [P, NT, C])
        xh = sb("xh", [P, NT, C])
        xT = sb("xT", [P, NT * P])
        xs = [xT[:, :].rearrange("p (i c) -> p i c", i=NT), xh[:, :, :]]
        st6 = sb("st6", [P, NT, 6])
        mv = sb("mv", [P, NT, 2])
        lnv = sb("lnv", [P, NT])
        lnr = sb("lnr", [P, NT])
        lnt = sb("lnt", [P, NT])

        s_const = sem("s_const")
        s_x = sem("s_x")
        s_w = sem("s_w")
        s_gw = sem("s_gw")
        s_eb = sem("s_eb")
        s_zero = sem("s_zero")
        s_dve = sem("s_dve")
        s_act = sem("s_act")
        s_pool = sem("s_pool")
        s_var = sem("s_var")
        s_std = sem("s_std")
        s_norm = sem("s_norm")
        s_xTp = sem("s_xTp")
        s_xT = sem("s_xT")
        s_out = sem("s_out")
        count = {"dve": 0, "act": 0, "pool": 0}

        def link(ins, sems={"dve": s_dve, "act": s_act, "pool": s_pool}, engs={"dve": nc.vector, "act": nc.scalar, "pool": nc.gpsimd}, who="dve"):
            count[who] += 1
            ins.then_inc(sems[who], 1)
            engs[who].wait_ge(sems[who], count[who])

        def bc(ap, shape):
            return ap.to_broadcast(shape)

        def norm_stats(n, hf):
            v = nc.vector
            t = range(HT * hf, HT * hf + HT)
            for i in t:
                ins = v.bn_stats(st6[:, i, :], xt[:, i, :])
            link(ins)
            for i in t:
                ins = v.bn_aggr(mv[:, i, :], st6[:, i, :])
            ins.then_inc(s_var, 1)

        def norm_root(n, hf):
            g = nc.gpsimd
            t = slice(HT * hf, HT * hf + HT)
            g.wait_ge(s_var, 2 * n + hf + 1)
            link(g.tensor_scalar(lnv[:, t], mv[:, t, 1], LN_EPS, None, ADD), who="pool")
            g.tensor_tensor(lnr[:, t], lnv[:, t], mhalf[:, :], ALU.pow).then_inc(s_std, 1)

        def norm_apply(n, hf):
            v = nc.vector
            if n:
                v.wait_ge(s_xTp, 4 * n - 2 + 2 * hf)
            v.wait_ge(s_std, 2 * n + hf + 1)
            for i in range(HT * hf, HT * hf + HT):
                v.tensor_scalar(xh[:, i, :], xt[:, i, :], mv[:, i, 0:1], lnr[:, i:i + 1], SUB, MUL).then_inc(s_norm, 1)

        def turn_tensor(n, c, bank):
            pe = nc.tensor
            pe.wait_ge(s_norm, NT * n + 4 * c + 4)
            for k in range(4):
                i = 4 * c + k
                ins = pe.transpose(ps[:, bank, P * k:P * k + P], xh[:, i, :], ident[:, :])
            ins.then_inc(s_xTp, 1)

        def turn_scalar(n, c, bank):
            a = nc.scalar
            a.wait_ge(s_xTp, 4 * n + c + 1)
            a.activation(xT[:, 512 * c:512 * c + 512], ps[:, bank, :], ACT.Copy).then_inc(s_xT, 1)

        L8 = sb("L8", [P, HT, NE])
        V8 = sb("V8", [P, HT, NE])
        Q8 = sb("Q8", [P, HT, NE])
        oh = sb("oh", [P, TOPK, HT, NE])
        m1 = sb("m1", [P, HT])
        m2 = sb("m2", [P, HT])
        wts = sb("wts", [P, TOPK, HT])
        chosen = sb("chosen", [P, HT, NE], BF16)
        totE = sb("totE", [P, NE, HT])
        cumE = sb("cumE", [P, NE, HT])
        base = sb("base", [P, HT, NE])
        tiles = sb("tiles", [P, NE])
        ends = sb("ends", [P, NE])
        first = sb("first", [P, NE])
        cmp16 = sb("cmp16", [P, NE, HT])
        cmpj = sb("cmpj", [P, JOBS, NE])
        slotf = sb("slotf", [P, TOPK, HT])
        slots = sb("slots", [P, 2, TOPK, HT], U32)
        jobf = sb("jobf", [P, JOBS])
        job_expert = sb("job_expert", [P, 2, JOBS], I32)

        room = sb("room", [P, (2 * B + B) * T])
        qk = room[:, 0:2 * B * T].rearrange("p (n b t) -> p n b t", n=2, b=B)
        GT = room[0:H, 2 * B * T:3 * B * T].rearrange("p (b t) -> p b t", b=B)
        w13 = room[:, 0:NE * 2 * HP].rearrange("p (e m h) -> p e m h", e=NE, m=2)
        room2 = sb("room2", [P, 2 * 3 * T])
        part = room2[:, :].bitcast(BF16).rearrange("p (a n k t) -> p a n k t", a=2, n=2, k=3)
        w2s = room2[:, 0:NE * len(HC) * C].rearrange("p (e k c) -> p e k c", e=NE, k=len(HC))

        att = ctx.enter_context(ExitStack())

        def asb(name, shape, dt=F32):
            return att.enter_context(nc.sbuf_tensor(name, shape, dt))

        Wrows = asb("Wrows", [P, 3, C])
        Wgr = asb("Wgr", [H, C])
        gwr = asb("gwr", [NE, C])
        PP = asb("PP", [P, 2, UNITS, 512])
        rest = asb("rest", [P, 2, T])
        mx = asb("mx", [P, B, 2])
        mxa = asb("mxa", [P, B, 2])
        fs = asb("fs", [P, B])
        feps = asb("feps", [P, B])
        va = asb("va", [P, NT, H, VW])
        z = asb("z", [P, NT, H])
        az = asb("az", [P, NT, H])
        lg = asb("lg", [P, NT, H])
        Gt = asb("Gt", [P, B, TB, H])
        Ct = asb("Ct", [P, B, TB, H])
        dec = asb("dec", [P, B, NOFF, H])
        rowf = asb("rowf", [P, B, TB, H])
        gp = asb("gp", [H, 2, 3, T], BF16)
        gr = asb("gr", [H, T])
        vp = asb("vp", [P, 2, len(PAIR), H, VW])
        QS = asb("QS", [102, 2, 8, T], BF16)
        KS = asb("KS", [102, 2, 8, T], BF16)
        A = asb("A", [P, 4, 512])
        E = asb("E", [P, 4, 512])
        OT = asb("OT", [P, 7, P])
        tmp = asb("tmp", [P, 3, GH, VW])
        YS = asb("YS", [P, TB, H, VW])
        rn = asb("rn", [P, TB, H])

        s_wT = sem("s_wT")
        s_wTc = sem("s_wTc")
        s_qkp = sem("s_qkp")
        s_qk = sem("s_qk")
        s_vzp = sem("s_vzp")
        s_vz = sem("s_vz")
        s_z = sem("s_z")
        s_l = sem("s_l")
        s_lg = sem("s_lg")
        s_gp = sem("s_gp")
        s_gt = sem("s_gt")
        s_dif = sem("s_dif")
        s_exp = sem("s_exp")
        s_gTp = sem("s_gTp")
        s_gT = sem("s_gT")
        s_mx = sem("s_mx")
        s_mxa = sem("s_mxa")
        s_fs = sem("s_fs")
        s_part = sem("s_part")
        s_gpart = sem("s_gpart")
        s_vp = sem("s_vp")
        s_store = sem("s_store")
        s_stack = [sem("s_stack0"), sem("s_stack1")]
        s_fill = sem("s_fill")
        s_zb = sem("s_zb")
        s_S = sem("s_S")
        s_A = sem("s_A")
        s_Q = sem("s_Q")
        s_D = sem("s_D")
        s_E = sem("s_E")
        s_PD = sem("s_PD")
        s_pv = sem("s_pv")
        s_Oo = sem("s_Oo")
        s_Od = sem("s_Od")
        s_OT = sem("s_OT")
        s_Y = sem("s_Y")
        s_xa = sem("s_xa")

        BK_S, BK_D, BK_OFF, BK_DIA, BK_T = 0, 3, 5, 6, 7
        NCONST = 13
        PARTS, GPARTS = 9, 5
        STACKS = 16 * 8
        STORES = 16 * 10

        def proj_sync():
            sp = nc.sync
            for b in range(B):
                sp.dma_start(xt[:, TB * b:TB * b + TB, :], x_rows[:, TB * b:TB * b + TB, :]).then_inc(s_x, 16)
            sp.dma_start(Wrows[:, :, :], W[0:3 * C, :].rearrange("(n p) c -> p n c", p=P)).then_inc(s_w, 16)
            sp.dma_start(Wgr[:, :], W[3 * C:3 * C + H, :]).then_inc(s_w, 16)
            sp.dma_start(gwr[:, :], gate_w).then_inc(s_w, 16)
            sp.dma_start(ebt[:, :], ebias.partition_broadcast(P)).then_inc(s_eb, 16)

        def fill_sync():
            sp = nc.sync
            sp.wait_ge(s_const, 4)
            for t in (QS, KS):
                rows96 = t[72:96].rearrange("p s h t -> p (s h t)").bitcast(F32).rearrange("p (n c) -> p n c", c=C)
                sp.dma_start(rows96, bc(zeros[0:24, :].unsqueeze(1), [24, rows96.shape[1], C])).then_inc(s_fill, 16)
                gates = t[96:102].rearrange("p s h (n c) -> p (s h n) c", c=P)
                sp.dma_start(gates, bc(onesb[0:6, :].unsqueeze(1), [6, gates.shape[1], P])).then_inc(s_fill, 16)

        def clear_sync():
            sp = nc.sync
            sp.wait_ge(s_const, NCONST)
            for hf in range(2):
                sp.dma_start(xr[hf].rearrange("(p n) c -> p n c", p=P),
                             bc(zeros[:, :].unsqueeze(1), [P, JOBS, C])).then_inc(s_zero, 16)

        def stack_sync(n):
            sp, b, half, slot = nc.sync, n // 2, n % 2, n % 2
            if half == 0:
                sp.wait_ge(s_part, PARTS * (b + 1))
                if b >= 2:
                    sp.wait_ge(s_stack[0], STACKS * (b - 1))
                    sp.wait_ge(s_stack[1], STACKS * (b - 1))
                for which, pieces in ((0, 3), (1, 5)):
                    for k in range(pieces):
                        sp.dma_start(parts_d[b % 2, which, :, k, :, :], part[:, b % 2, which, k % 3, :]).then_inc(s_store, 16)
                sp.wait_ge(s_gpart, GPARTS * (b + 1))
                for n2 in range(2):
                    sp.dma_start(gates_d[b % 2, n2], gp[:, n2, :, :]).then_inc(s_store, 16)
                sp.wait_ge(s_store, STORES * (b + 1))
            if n >= 2:
                sp.wait_ge(s_S, UNITS * 2 * (n - 1))
            heads = slice(8 * half, 8 * half + 8)
            for k in range(3):
                sp.dma_start(QS[24 * k:24 * k + 24, slot, :, :],
                             parts_d[b % 2, 0, heads, 0:3, :, :].rearrange("h k d t -> (k d) h t")).then_inc(s_stack[slot], 16)
                sp.dma_start(KS[24 * k:24 * k + 24, slot, :, :],
                             parts_d[b % 2, 1, heads, k:k + 3, :, :].rearrange("h k d t -> (k d) h t")).then_inc(s_stack[slot], 16)
            if n >= 2:
                sp.wait_ge(s_D, 8 * (n - 1))
            sp.dma_start(QS[96:99, slot, :, :], gates_d[b % 2, 0, heads].rearrange("h k t -> k h t")).then_inc(s_stack[slot], 16)
            sp.dma_start(KS[99:102, slot, :, :], gates_d[b % 2, 1, heads].rearrange("h k t -> k h t")).then_inc(s_stack[slot], 16)

        def const_pool():
            g = nc.gpsimd

            def part1(t, v):
                link(g.memset(t[:], v), who="pool")

            def triangle(t, op, fill, base, pattern, cm):
                g.affine_select(out=t[:], in_=t[:], compare_op=op, fill=fill, base=base,
                                pattern=pattern, channel_multiplier=cm).then_inc(s_const, 1)

            part1(ident, 0.0)
            triangle(ident, ALU.not_equal, 1.0, 0, [[-1, P]], 1)
            part1(tri, 1.0)
            triangle(tri, ALU.is_ge, 0.0, 0, [[1, P]], -1)
            g.memset(zeros[:, :], 0.0).then_inc(s_const, 1)
            g.memset(onesb[:, :], 1.0).then_inc(s_const, 1)
            g.memset(ones[:, :], 1.0).then_inc(s_const, 1)
            g.memset(va[:, :, :, HS:VW], 1.0).then_inc(s_const, 1)
            link(g.memset(mhalf[:, :], -0.5), who="pool")
            norm_root(0, 0)
            part1(identb, 0.0)
            triangle(identb, ALU.not_equal, 1.0, 0, [[-1, P]], 1)
            part1(negmask, 0.0)
            triangle(negmask, ALU.is_ge, NEG, 0, [[0, TB], [1, P]], -1)
            norm_root(0, 1)
            bound_pool(0)
            part1(trib, 1.0)
            triangle(trib, ALU.is_ge, 0.0, -1, [[1, P]], -1)
            g.iota(iom8[:, :], [[1, NE]], base=-8, channel_multiplier=0, allow_small_or_imprecise_dtypes=True).then_inc(s_const, 1)
            g.iota(iojob[:, :], [[1, JOBS]], base=0, channel_multiplier=0, allow_small_or_imprecise_dtypes=True).then_inc(s_const, 1)
            g.iota(io128[:, :], [[P, HT]], base=0, channel_multiplier=0, allow_small_or_imprecise_dtypes=True).then_inc(s_const, 1)
            part1(carry1, 1.0)
            g.memset(carry1[:, :, 0:1], 0.0).then_inc(s_const, 1)
            decayed_pool(0)
            bound_pool(1)

        def bound_pool(hf):
            g = nc.gpsimd
            g.wait_ge(s_mx, 4 * (hf + 1))
            b2 = slice(2 * hf, 2 * hf + 2)
            g.partition_all_reduce(mxa[:, b2, :].rearrange("p b n -> p (b n)"), mx[:, b2, :].rearrange("p b n -> p (b n)"),
                                   P, bass.bass_isa.ReduceOp.max).then_inc(s_mxa, 1)

        def weights_tensor():
            pe = nc.tensor
            pe.wait_ge(s_const, 1)
            pe.wait_ge(s_w, 48)
            for n in range(3):
                pe.transpose(ps[:, 7, P * n:P * n + P], Wrows[:, n, :], ident[:, :])
            pe.transpose(ps[:, 7, 3 * P:3 * P + H], Wgr[:, :], ident[0:H, 0:H])
            pe.transpose(ps[:, 7, 3 * P + H:3 * P + H + NE], gwr[:, :], ident[0:NE, 0:NE]).then_inc(s_wT, 1)

        def proj_tensor(b):
            pe = nc.tensor
            if b >= 2:
                pe.wait_ge(s_xT, b - 1)
            turn_tensor(0, b, b % 2)
            pe.wait_ge(s_xT, b + 1)
            if b == 0:
                pe.wait_ge(s_wTc, 2)
            for n in range(2):
                if b:
                    pe.wait_ge(s_qk, 2 * b - 1 + n)
                pe.matmul(ps[:, 2 + n, :], WT[:, C * n:C * n + C], xT[:, T * b:T * b + T],
                          start=True, stop=True).then_inc(s_qkp, 1)
            if b:
                pe.wait_ge(s_vz, 2 * b)
            for t in range(TB):
                i = TB * b + t
                ins = pe.matmul(ps[:, 4 + t // 2, 256 * (t % 2):256 * (t % 2) + C + H], xT[:, P * i:P * i + P],
                                WT[:, 2 * C:3 * C + H], start=True, stop=True)
            ins.then_inc(s_vzp, 1)

        def gates_tensor(hf):
            pe = nc.tensor
            pe.wait_ge(s_lg, hf + 1)
            pe.wait_ge(s_const, 5)
            if hf:
                pe.wait_ge(s_gt, 1)
            for o, m in ((0, tri), (HT * H, ones)):
                ins = pe.matmul(ps[:, 6, o:o + HT * H], m[:, :], lg[:, HT * hf:HT * hf + HT, :].rearrange("p t h -> p (t h)"),
                                start=True, stop=True)
            ins.then_inc(s_gp, 1)
            pe.wait_ge(s_gt, hf + 1)
            for b in range(2 * hf, 2 * hf + 2):
                if b == 0:
                    pe.wait_ge(s_wTc, 2)
                else:
                    pe.wait_ge(s_gT, b)
                for i in range(TB):
                    ins = pe.transpose(ps[0:H, 7, P * i:P * i + P], Gt[:, b, i, :], ident[:, :])
                ins.then_inc(s_gTp, 1)

        def proj_scalar(b):
            a = nc.scalar
            if b == 0:
                a.wait_ge(s_wT, 1)
                a.activation(WT[:, :], ps[:, 7, 0:3 * C + H], ACT.Copy).then_inc(s_wTc, 1)
                a.activation(gwT[:, :], ps[:, 7, 3 * C + H:3 * C + H + NE], ACT.Copy).then_inc(s_wTc, 1)
            turn_scalar(0, b, b % 2)
            for n in range(2):
                a.wait_ge(s_qkp, 2 * b + n + 1)
                a.activation(qk[:, n, b, :], ps[:, 2 + n, :], ACT.Copy).then_inc(s_qk, 1)
            a.wait_ge(s_vzp, b + 1)
            a.wait_ge(s_const, 6)
            for t in range(0, TB, 2):
                i = TB * b + t
                src = ps[:, 4 + t // 2, :].rearrange("p (n c) -> p n c", n=2)
                for k in range(2):
                    a.activation(va[:, i + k, :, 0:HS], src[:, k, 0:C].rearrange("p (h d) -> p h d", h=H), ACT.Copy)
                a.activation(z[:, i:i + 2, :], src[:, :, C:C + H], ACT.Copy).then_inc(s_vz, 1)

        def gates_scalar(hf):
            a = nc.scalar
            t = slice(HT * hf, HT * hf + HT)
            a.wait_ge(s_vz, 4 * (hf + 1))
            link(a.activation(az[:, t], z[:, t], ACT.Abs), who="act")
            link(a.activation(az[:, t], az[:, t], ACT.Exp, scale=-1.0), who="act")
            a.activation(az[:, t], az[:, t], ACT.Ln, bias=1.0).then_inc(s_l, 1)

        def decays_scalar(hf):
            a = nc.scalar
            b2 = slice(2 * hf, 2 * hf + 2)
            a.wait_ge(s_dif, hf + 1)
            a.activation(dec[:, b2], dec[:, b2], ACT.Exp).then_inc(s_exp, 1)
            a.activation(rowf[:, b2, 1:TB, :], rowf[:, b2, 1:TB, :], ACT.Exp).then_inc(s_exp, 1)

        def gates_vector(hf):
            v = nc.vector
            t = slice(HT * hf, HT * hf + HT)
            b2 = slice(2 * hf, 2 * hf + 2)
            v.wait_ge(s_l, hf + 1)
            v.scalar_tensor_tensor(lg[:, t], z[:, t], 0.0, az[:, t], ALU.min, SUB).then_inc(s_lg, 1)
            v.wait_ge(s_gp, hf + 1)
            own, whole = (ps[:, 6, o:o + HT * H].rearrange("p (b t h) -> p b t h", b=2, t=TB) for o in (0, HT * H))
            v.tensor_copy(Gt[:, b2, 0, :], own[:, :, 0])
            link(v.tensor_copy(Ct[:, b2, 1, :], whole[:, :, 0]))
            for i in range(2, TB):
                link(v.tensor_tensor(Ct[:, b2, i, :], Ct[:, b2, i - 1, :], whole[:, :, i - 1], ADD))
            v.tensor_tensor(Gt[:, b2, 1:TB, :], Ct[:, b2, 1:TB, :], own[:, :, 1:TB], ADD).then_inc(s_gt, 1)
            v.wait_ge(s_gt, hf + 1)
            n = 0
            for i in range(1, TB):
                v.tensor_tensor(dec[:, b2, n:n + i, :], bc(Ct[:, b2, i:i + 1, :], [P, 2, i, H]), Gt[:, b2, 0:i, :], SUB)
                n += i
            v.tensor_tensor(rowf[:, b2, 1:TB, :], Gt[:, b2, 1:TB, :], Ct[:, b2, 1:TB, :], SUB).then_inc(s_dif, 1)

        def gate_rows_vector(b):
            v = nc.vector
            v.wait_ge(s_gTp, b + 1)
            v.tensor_copy(GT[:, b, :], ps[0:H, 7, :]).then_inc(s_gT, 1)

        def bound_vector(hf):
            v = nc.vector
            for b in range(2 * hf, 2 * hf + 2):
                for n in range(2):
                    v.wait_ge(s_qk, 2 * b + n + 1)
                    v.tensor_reduce(mx[:, b, n:n + 1], qk[:, n, b, :], AX.X, ALU.max, apply_absolute_value=True).then_inc(s_mx, 1)

        def bound_scale_vector(hf):
            v = nc.vector
            b2 = slice(2 * hf, 2 * hf + 2)
            v.wait_ge(s_mxa, hf + 1)
            link(v.tensor_scalar(mxa[:, b2, :], mxa[:, b2, :], 1e-8, None, MUL))
            link(v.tensor_tensor(fs[:, b2], mxa[:, b2, 0], mxa[:, b2, 1], MUL))
            link(v.tensor_scalar(fs[:, b2], fs[:, b2], 1e-20, 1e30, ALU.max, ALU.min))
            link(v.reciprocal(fs[:, b2], fs[:, b2]))
            link(v.tensor_scalar(fs[:, b2], fs[:, b2], 1.25, 1.0, MUL, ALU.min))
            v.tensor_scalar(feps[:, b2], fs[:, b2], LOG_EPS, None, MUL).then_inc(s_fs, 1)

        def parts_vector(b, step):
            v = nc.vector
            pt = part[:, b % 2]
            done, gdone = PARTS * b, GPARTS * b
            if step == 0:
                if b >= 2:
                    v.wait_ge(s_store, STORES * (b - 1))
                v.tensor_scalar(qk[:, 0, b, :], qk[:, 0, b, :], fs[:, b:b + 1], None, MUL).then_inc(s_part, 1)
            elif step == 1:
                v.wait_ge(s_part, done + 1)
                for n in range(2):
                    v.tensor_copy(pt[:, n, 0, :], qk[:, n, b, :]).then_inc(s_part, 1)
            elif step == 2:
                v.wait_ge(s_part, done + 3)
                for n in range(2):
                    v.tensor_tensor(rest[:, n, :], qk[:, n, b, :], pt[:, n, 0, :], SUB).then_inc(s_part, 1)
            elif step == 3:
                v.wait_ge(s_part, done + 5)
                for n in range(2):
                    v.tensor_copy(pt[:, n, 1, :], rest[:, n, :]).then_inc(s_part, 1)
            elif step == 4:
                v.wait_ge(s_part, done + 7)
                for n in range(2):
                    v.tensor_tensor(pt[:, n, 2, :], rest[:, n, :], pt[:, n, 1, :], SUB).then_inc(s_part, 1)
            elif step == 5:
                if b:
                    v.wait_ge(s_store, STORES * b)
                v.wait_ge(s_gT, b + 1)
                v.tensor_copy(gp[:, 0, 0, :], GT[:, b, :]).then_inc(s_gpart, 1)
            elif step == 6:
                v.wait_ge(s_gpart, gdone + 1)
                v.tensor_tensor(gr[:, :], GT[:, b, :], gp[:, 0, 0, :], SUB).then_inc(s_gpart, 1)
            elif step == 7:
                v.wait_ge(s_gpart, gdone + 2)
                v.tensor_copy(gp[:, 0, 1, :], gr[:, :]).then_inc(s_gpart, 1)
            elif step == 8:
                v.wait_ge(s_gpart, gdone + 3)
                v.tensor_tensor(gp[:, 0, 2, :], gr[:, :], gp[:, 0, 1, :], SUB).then_inc(s_gpart, 1)
            elif step == 9:
                v.wait_ge(s_gpart, gdone + 4)
                v.tensor_scalar(gp[:, 1, :, :], gp[:, 0, :, :], -1.0, None, MUL).then_inc(s_gpart, 1)

        def decayed_pool(b):
            g = nc.gpsimd
            g.wait_ge(s_exp, 2 * (b // 2) + 2)
            g.wait_ge(s_vz, 2 * b + 2)
            if b >= 2:
                g.wait_ge(s_pv, UNITS * NG * (b - 1))
            slot, n = b % 2, 0
            for i in range(1, TB):
                for j in range(i):
                    g.tensor_tensor(vp[:, slot, n, :, :], va[:, TB * b + j, :, :],
                                    bc(dec[:, b, n, :].unsqueeze(2), [P, H, VW]), MUL).then_inc(s_vp, 1)
                    n += 1
            for j in range(TB):
                g.tensor_copy(vp[:, slot, NOFF + j, :, :], va[:, TB * b + j, :, :]).then_inc(s_vp, 1)

        LAG = 4
        LAST = UNITS * (GROUPS + 2) + LAG + 4

        def at(U, offset, stage, width=1):
            G, n = divmod(U - offset, UNITS)
            if 0 <= G < GROUPS and n < width:
                stage(G, n)

        def scores_tensor(G, u):
            pe = nc.tensor
            b, g = divmod(G, NG)
            n, half = 2 * b + g // 2, g % 2
            slot = n % 2
            kind, r = PLAN[u]
            U = UNITS * G + u
            if u == 0 and half == 0:
                pe.wait_ge(s_stack[slot], STACKS * (b + 1))
            if U >= 3:
                pe.wait_ge(s_A, U - 2)
            bank = ps[:, BK_S + U % 3, :]

            def block(col, width, r, j, t0):
                h = 4 * half + r
                return pe.matmul(bank[:, col:col + width], KS[0:96, slot, h, P * j:P * j + P],
                                 QS[0:96, slot, h, t0:t0 + width], start=True, stop=True)

            if kind == "diag":
                for j in range(TB):
                    ins = block(P * j, P, r, j, P * j)
            elif kind == "far":
                block(0, 384, r, 0, P)
                ins = block(384, P, r, 2, 3 * P)
            else:
                block(0, 256, r, 1, 2 * P)
                ins = block(256, 256, r + 1, 1, 2 * P)
            ins.then_inc(s_S, 1)
            if kind == "diag":
                hh = GH * G + r
                if hh >= 2:
                    pe.wait_ge(s_E, hh - 1)
                h = 4 * half + r
                dst = ps[:, BK_D + hh % 2, :]
                for j in range(TB):
                    pe.matmul(dst[:, P * j:P * j + P], KS[96:102, slot, h, P * j:P * j + P], QS[96:102, slot, h, P * j:P * j + P],
                              start=(j == 0), stop=False, skip_group_check=True)
                pe.matmul(dst, identb[:, :], negmask[:, :, :].rearrange("p j t -> p (j t)"), start=False, stop=True,
                          skip_group_check=True).then_inc(s_D, 1)

        def sums_tensor(G, n):
            pe = nc.tensor
            b, g = divmod(G, NG)
            i, j = (OFF + [(k, k) for k in range(TB)])[n]
            if n == 0:
                pe.wait_ge(s_vp, len(PAIR) * (b + 1))
                pe.wait_ge(s_Q, UNITS * (G + 1))
                if G:
                    pe.wait_ge(s_Oo, G)
            if n == NOFF:
                pe.wait_ge(s_PD, GH * (G + 1))
                if G:
                    pe.wait_ge(s_Od, G)
            bank = BK_OFF if i != j else BK_DIA
            for r in range(GH):
                u, col = block_at(r, i, j)
                ins = pe.matmul(ps[32 * r:32 * r + VW, bank, P * i:P * i + P], vp[:, b % 2, n, GH * g + r, :],
                                PP[:, G % 2, u, col:col + P], start=(n in (0, NOFF)), stop=False, skip_group_check=True)
            ins.then_inc(s_pv, 1)

        def turn_sums_tensor(G, part2):
            pe = nc.tensor
            if part2:
                pe.wait_ge(s_Y, 2 * G + 1)
                pe.wait_ge(s_Od, G + 1)
            else:
                pe.wait_ge(s_Oo, G + 1)
                if G:
                    pe.wait_ge(s_Y, 2 * G)
            for k in range(4) if part2 else range(3):
                ins = pe.transpose(ps[:, BK_T, P * k:P * k + P], OT[:, (3 if part2 else 0) + k, :], ident[:, :])
            ins.then_inc(s_OT, 1)

        def heads_tensor():
            pe = nc.tensor
            pe.wait_ge(s_gT, B)
            pe.wait_ge(s_vz, 2 * B)
            pe.wait_ge(s_zb, 2)
            pe.wait_ge(s_fill, 64)
            pe.wait_ge(s_const, 8)
            for U in range(LAST):
                if U < UNITS * GROUPS:
                    scores_tensor(*divmod(U, UNITS))
                at(U, UNITS + LAG, lambda G, n: sums_tensor(G, n), UNITS)
                at(U, 2 * UNITS + LAG - 2, lambda G, n: turn_sums_tensor(G, False))
                at(U, 2 * UNITS + LAG + 2, lambda G, n: turn_sums_tensor(G, True))
                prepare_tensor(0, U)

        def heads_vector():
            v = nc.vector
            v.wait_ge(s_vz, 2 * B)
            for k in (BK_OFF, BK_DIA):
                v.memset(ps[:, k, :], 0.0).then_inc(s_zb, 1)
            for U in range(LAST):
                if U < UNITS * GROUPS:
                    v.wait_ge(s_S, U + 1)
                    if U >= 4:
                        v.wait_ge(s_Q, U - 3)
                    v.tensor_scalar(A[:, U % 4, :].bitcast(I32), ps[:, BK_S + U % 3, :].bitcast(I32),
                                    0x7fffffff, None, ALU.bitwise_and).then_inc(s_A, 1)
                at(U, 2 * UNITS + LAG - 4, lambda G, n: take_sums_vector(G, False))
                at(U, 2 * UNITS + LAG, lambda G, n: take_sums_vector(G, True))
                at(U, 2 * UNITS + LAG - 1, lambda G, n: combine_vector(G, False))
                at(U, 2 * UNITS + LAG + 3, lambda G, n: combine_vector(G, True))
                b, k = divmod(U - 1, UNITS * NG)
                if b + 1 < B and k % 2 == 0 and k < 20:
                    parts_vector(b + 1, k // 2)
                prepare_vector(0, U)

        def combine_vector(G, part2):
            v = nc.vector
            b, g = divmod(G, NG)
            v.wait_ge(s_OT, 2 * G + 1 + part2)
            turned = ps[:, BK_T, :].rearrange("p (k r c) -> p k r c", r=GH, c=32)[:, :, :, 0:VW]
            hs = slice(GH * g, GH * g + GH)
            if not part2:
                v.tensor_tensor(tmp[:], turned[:, 0:3], bc(rowf[:, b, 1:TB, hs].unsqueeze(3), [P, 3, GH, VW]), MUL).then_inc(s_Y, 1)
                return
            v.wait_ge(s_Y, 2 * G + 1)
            link(v.tensor_copy(YS[:, 0, hs, :], turned[:, 0]))
            v.tensor_tensor(YS[:, 1:TB, hs, :], turned[:, 1:4], tmp[:], ADD).then_inc(s_Y, 1)
            v.wait_ge(s_Y, 2 * G + 2)
            if g == NG - 1:
                link(v.reciprocal(rn[:, :, :], YS[:, :, :, HS]))
                link(v.tensor_tensor(YS[:, :, :, 0:HS], YS[:, :, :, 0:HS], bc(rn[:, :, :].unsqueeze(3), [P, TB, H, HS]), MUL))
                xb = xt[:, TB * b:TB * b + TB, :].rearrange("p t (h d) -> p t h d", h=H)
                v.tensor_tensor(xb, xb, YS[:, :, :, 0:HS], ADD).then_inc(s_xa, 1)
                v.wait_ge(s_xa, b + 1)

        def square_scalar(G, u):
            a = nc.scalar
            b = G // NG
            U = UNITS * G + u
            a.wait_ge(s_A, U + 1)
            if G >= 2 and u == 0:
                a.wait_ge(s_pv, UNITS * (G - 1))
            a.activation(PP[:, G % 2, u, :], A[:, U % 4, :], ACT.Square, bias=feps[:, b:b + 1]).then_inc(s_Q, 1)

        def gate_scalar(G, r):
            a = nc.scalar
            hh = GH * G + r
            a.wait_ge(s_D, hh + 1)
            if hh >= 4:
                a.wait_ge(s_PD, hh - 3)
            a.activation(E[:, hh % 4, :], ps[:, BK_D + hh % 2, :], ACT.Exp).then_inc(s_E, 1)

        def take_sums_vector(G, diagonal):
            v = nc.vector
            v.wait_ge(s_pv, UNITS * G + (UNITS if diagonal else NOFF))
            if G:
                v.wait_ge(s_OT, 2 * G - 1 + diagonal)
            if diagonal:
                v.tensor_copy(OT[:, 3:7, :].rearrange("p k t -> p (k t)"), ps[:, BK_DIA, :]).then_inc(s_Od, 1)
            else:
                v.tensor_copy(OT[:, 0:3, :].rearrange("p k t -> p (k t)"), ps[:, BK_OFF, P:512]).then_inc(s_Oo, 1)

        def heads_scalar():
            a = nc.scalar
            a.wait_ge(s_fs, 2)
            for G in range(GROUPS):
                for u in range(UNITS):
                    if PLAN[u][0] == "diag":
                        gate_scalar(G, PLAN[u][1])
                    square_scalar(G, u)
                    prepare_scalar(0, UNITS * G + u)

        def heads_pool():
            g = nc.gpsimd
            for G in range(GROUPS):
                for r in range(GH):
                    u = PLAN.index(("diag", r))
                    hh = GH * G + r
                    g.wait_ge(s_E, hh + 1)
                    g.wait_ge(s_Q, UNITS * G + u + 1)
                    w = PP[:, G % 2, u, :]
                    g.tensor_tensor(w, w, E[:, hh % 4, :], MUL).then_inc(s_PD, 1)
                    prepare_pool(0, UNITS * G + u)
                if G % NG == 1 and G // NG + 1 < B:
                    decayed_pool(G // NG + 1)

        att.close()

        rows = sb("rows", [P, 4, C])
        rowsT = sb("rowsT", [P, 2, P])
        silu = sb("silu", [P, 2, HP])
        hid = sb("hid", [P, 2, HP])
        ysb = sb("ysb", [P, 4, C])
        wj = sb("wj", [P, 2, 2, HP])

        s_ww = sem("s_ww")
        s_lgp = sem("s_lgp")
        s_rd = sem("s_rd")
        s_re = sem("s_re")
        s_M = sem("s_M")
        s_rank = sem("s_rank")
        s_slot = sem("s_slot")
        s_job = sem("s_job")
        s_rk = sem("s_rk")
        s_scat = [sem("s_scat0"), sem("s_scat1")]
        s_row = [sem(f"s_row{k}") for k in range(4)]
        s_rTp = sem("s_rTp")
        s_rT = sem("s_rT")
        s_AB = sem("s_AB")
        s_silu = sem("s_silu")
        s_hid = sem("s_hid")
        s_pad = sem("s_pad")
        s_wj = sem("s_wj")
        s_yp = sem("s_yp")
        s_y = sem("s_y")
        s_yst = [sem(f"s_yst{k}") for k in range(4)]
        s_gat = [sem(f"s_gat{k}") for k in range(B)]
        s_xm = sem("s_xm")
        PJ = JOBS // 4

        def weights_sync():
            sp = nc.sync
            sp.wait_ge(s_part, PARTS * B)
            sp.wait_ge(s_gpart, GPARTS * B)
            sp.dma_start(w13[:, :, 0, 0:HID], w1.rearrange("e c h -> c e h")).then_inc(s_ww, 16)
            sp.dma_start(w13[:, :, 1, 0:HID], w3.rearrange("e c h -> c e h")).then_inc(s_ww, 16)
            sp.wait_ge(s_store, STORES * B)
            for k, (h0, hw) in enumerate(HC):
                sp.dma_start(w2s[0:hw, :, k, :], w2[:, h0:h0 + hw, :].rearrange("e p c -> p e c")).then_inc(s_ww, 16)

        PREP_STATS, PREP_APPLY, PREP_TURN, PREP_LOGITS = 98, 103, 109, 129
        PREP_SOFTMAX, PREP_EXP, PREP_TOP, PREP_RANKS, PREP_SLOTS, PREP_SCALE = 130, 131, 133, 139, 140, 144

        def turned_free(m):
            if m == 0:
                return lambda U: nc.tensor.wait_ge(s_Y, 2 * ((U - 2 * UNITS - LAG - 3) // UNITS + 1))
            return lambda U: None

        def prepare_tensor(m, U=None):
            pe = nc.tensor
            n, hf = 1 + 2 * (m // 2), m % 2
            for k in range(2):
                if U in (None, PREP_TURN + 10 * k):
                    turned_free(m)(U)
                    if U is None and k:
                        pe.wait_ge(s_xT, 4 * n + 2 * hf + k)
                    turn_tensor(n, 2 * hf + k, BK_T)
            if U in (None, PREP_LOGITS):
                turned_free(m)(U)
                pe.wait_ge(s_xT, 4 * n + 2 * hf + 2)
                for i in range(HT):
                    ii = HT * hf + i
                    ins = pe.matmul(ps[:, BK_T, NE * i:NE * i + NE], xT[:, P * ii:P * ii + P], gwT[:, :], start=True, stop=True)
                ins.then_inc(s_lgp, 1)
            if U in (None, PREP_RANKS):
                turned_free(m)(U)
                pe.wait_ge(s_M, m + 1)
                pe.wait_ge(s_const, NCONST)
                flat = chosen[:].rearrange("p t e -> p (t e)")
                pe.matmul(ps[:, BK_T, 0:64], trib[:, :], flat, start=True, stop=True)
                pe.matmul(ps[:, BK_T, 64:128], onesb[:, :], flat, start=True, stop=True).then_inc(s_rank, 1)
            for at_, s_, c in ((PREP_TURN + 2, s_xT, 4 * n + 2 * hf + 1), (PREP_TURN + 12, s_xT, 4 * n + 2 * hf + 2),
                               (PREP_LOGITS + 2, s_rd, m + 1), (PREP_RANKS + 2, s_rk, m + 1)):
                if U == at_:
                    pe.wait_ge(s_, c)

        def prepare_scalar(m, U=None):
            a = nc.scalar
            n, hf = 1 + 2 * (m // 2), m % 2
            for k in range(2):
                if U in (None, PREP_TURN + 10 * k):
                    turn_scalar(n, 2 * hf + k, BK_T)
            if U in (None, PREP_EXP):
                a.wait_ge(s_rd, m + 1)
                a.activation(L8[:], L8[:], ACT.Exp).then_inc(s_re, 1)

        def prepare_vector(m, U=None):
            v = nc.vector
            n, hf = 1 + 2 * (m // 2), m % 2
            ht = slice(HT * hf, HT * hf + HT)

            def e8(ap):
                return bc(ap.unsqueeze(2), [P, HT, NE])

            def iom():
                return bc(iom8[:, :].unsqueeze(1), [P, HT, NE])

            if U in (None, PREP_STATS):
                norm_stats(n, hf)
            if U in (None, PREP_APPLY):
                norm_apply(n, hf)
            if U in (None, PREP_SOFTMAX):
                v.wait_ge(s_lgp, m + 1)
                if m == 0:
                    v.wait_ge(s_eb, 16)
                    v.wait_ge(s_const, NCONST)
                lgt = ps[:, BK_T, 0:64].rearrange("p (t e) -> p t e", e=NE)
                link(v.tensor_reduce(m1[:, :], lgt, AX.X, ALU.max))
                v.tensor_tensor(L8[:], lgt, e8(m1[:, :]), SUB).then_inc(s_rd, 1)
            if U in (None, PREP_TOP):
                v.wait_ge(s_re, m + 1)
                link(v.tensor_reduce(m1[:, :], L8[:], AX.X, ADD))
                link(v.reciprocal(m1[:, :], m1[:, :]))
                link(v.tensor_tensor(L8[:], L8[:], e8(m1[:, :]), MUL))
                link(v.tensor_tensor(V8[:], L8[:], bc(ebt[:, :].unsqueeze(1), [P, HT, NE]), ADD))
            for k in range(TOPK):
                if U not in (None, PREP_TOP + 1 + 2 * k):
                    continue
                link(v.tensor_reduce(m1[:, :], V8[:], AX.X, ALU.max))
                link(v.tensor_tensor(Q8[:], V8[:], e8(m1[:, :]), ALU.is_equal))
                link(v.tensor_tensor(Q8[:], Q8[:], iom(), MUL))
                link(v.tensor_reduce(m2[:, :], Q8[:], AX.X, ALU.min))
                link(v.tensor_tensor(oh[:, k], iom(), e8(m2[:, :]), ALU.is_equal))
                if k == 0:
                    link(v.scalar_tensor_tensor(V8[:], oh[:, 0], NEG, V8[:], MUL, ADD))
                else:
                    v.tensor_tensor(chosen[:], oh[:, 0], oh[:, 1], ADD).then_inc(s_M, 1)
                link(v.tensor_tensor(Q8[:], oh[:, k], L8[:], MUL))
                link(v.tensor_reduce(wts[:, k, :], Q8[:], AX.X, ADD))
            if U in (None, PREP_SLOTS):
                v.wait_ge(s_rank, m + 1)
                rank = ps[:, BK_T, 0:64].rearrange("p (t e) -> p t e", e=NE)
                tot = ps[:, BK_T, 64:128].rearrange("p (t e) -> p e t", e=NE)
                v.tensor_copy(base[:], rank)
                v.tensor_copy(totE[:], tot).then_inc(s_rk, 1)
                v.wait_ge(s_rk, m + 1)
                link(v.tensor_tensor_scan(cumE[:].rearrange("p e t -> p (e t)"), carry1[:].rearrange("p e t -> p (e t)"),
                                          totE[:].rearrange("p e t -> p (e t)"), 0.0, MUL, ADD))
                link(v.tensor_tensor(cmp16[:], bc(cumE[:, :, HT - 1:HT], [P, NE, HT]), bc(io128[:, :].unsqueeze(1), [P, NE, HT]), ALU.is_gt))
                link(v.tensor_reduce(tiles[:, :], cmp16[:], AX.X, ADD))
                link(v.tensor_tensor_scan(ends[:, :], ones[:, 0:NE], tiles[:, :], 0.0, MUL, ADD))
                link(v.tensor_tensor(first[:, :], ends[:, :], tiles[:, :], SUB))
                link(v.tensor_scalar(first[:, :], first[:, :], float(P), None, MUL))
                link(v.tensor_tensor(cumE[:], cumE[:], totE[:], SUB))
                link(v.tensor_tensor(cumE[:], cumE[:], bc(first[:, :].unsqueeze(2), [P, NE, HT]), ADD))
                link(v.tensor_tensor(base[:], base[:], cumE[:].rearrange("p e t -> p t e"), ADD))
            if U in (None, PREP_SLOTS + 2):
                for k in range(TOPK):
                    link(v.tensor_tensor(Q8[:], oh[:, k], base[:], MUL))
                    link(v.tensor_reduce(slotf[:, k, :], Q8[:], AX.X, ADD))
                if m >= 2:
                    v.wait_ge(s_xm, m - 1)
                link(v.tensor_copy(slots[:, hf], slotf[:]))
                link(v.tensor_tensor(cmpj[:], bc(iojob[:, :].unsqueeze(2), [P, JOBS, NE]), bc(ends[:, :].unsqueeze(1), [P, JOBS, NE]), ALU.is_ge))
                link(v.tensor_reduce(jobf[:, :], cmpj[:], AX.X, ADD))
                link(v.tensor_scalar(jobf[:, :], jobf[:, :], float(NE - 1), None, ALU.min))
                v.tensor_copy(job_expert[:, hf, :], jobf[:, :]).then_inc(s_job, 1)
            if U in (None, PREP_SCALE):
                for k in range(TOPK):
                    v.tensor_tensor(xs[k][:, ht, :], xh[:, ht, :], bc(wts[:, k, :].unsqueeze(2), [P, HT, C]), MUL).then_inc(s_slot, 1)

        def pad_pool():
            g = nc.gpsimd
            g.wait_ge(s_part, PARTS * B)
            g.wait_ge(s_gpart, GPARTS * B)
            g.memset(w13[:, :, :, HID:HP], 0.0).then_inc(s_pad, 1)

        def prepare_pool(m, U=None):
            n, hf = 1 + 2 * (m // 2), m % 2
            if U is None or UNITS * 9 + 7 == U:
                norm_root(n, hf)
            if U is None or U >= UNITS * 14 + 2:
                turn = 0 if U is None else GH * (U // UNITS - 14) + [u for u in range(UNITS) if PLAN[u][0] == "diag"].index(U % UNITS) - 1
                todo = range(TOPK * HT) if U is None else range(3 * turn, min(3 * turn + 3, TOPK * HT))
                for r in todo:
                    scatter_pool(m, *divmod(r, TOPK), first=(r == 0))

        def scatter_pool(m, i, k, first):
            g, hf = nc.gpsimd, m % 2
            if first:
                g.wait_ge(s_slot, TOPK * (m + 1))
                g.wait_ge(s_job, m + 1)
                g.wait_ge(s_zero, 32)
            g.indirect_dma_start(xr[hf], bass.IndirectOffsetOnAxis(ap=slots[:, hf, k, i:i + 1], axis=0),
                                 xs[k][:, HT * hf + i, :], None).then_inc(s_scat[hf], 16)

        def gather_pool(m):
            g, hf = nc.gpsimd, m % 2
            for k in range(4):
                g.wait_ge(s_yst[k], 16 * PJ * (m + 1))
            for i in range(HT):
                for k in range(TOPK):
                    g.indirect_dma_start(xs[k][:, HT * hf + i, :], None, yr[hf],
                                         bass.IndirectOffsetOnAxis(ap=slots[:, hf, k, i:i + 1], axis=0)).then_inc(s_gat[2 * hf + i // TB], 16)

        def add_vector(m):
            v, hf = nc.vector, m % 2
            for b in range(2 * hf, 2 * hf + 2):
                t = slice(TB * b, TB * b + TB)
                v.wait_ge(s_gat[b], 16 * TOPK * TB * (m // 2 + 1))
                link(v.tensor_tensor(xh[:, t, :], xs[0][:, t, :], xh[:, t, :], ADD))
                ins = v.tensor_tensor(xt[:, t, :], xt[:, t, :], xh[:, t, :], ADD)
            ins.then_inc(s_xm, 1)
            v.wait_ge(s_xm, m + 1)

        def looped(eng, step, lo, hi, last):
            for s in range(4 * lo):
                step(s // 4, s % 4, s)
            with eng.Fori(lo, hi) as q:
                for k in range(4):
                    step(q, k, None)
            for s in range(4 * hi, last + 1):
                step(s // 4, s % 4, s)

        def before(q, k, d):
            return (q - (d - k + 3) // 4, (k - d) % 4)

        def after(q, k):
            return (q, k + 1) if k < 3 else (q + 1, 0)

        def jobs_sync(m):
            sp = nc.sync
            hf = m % 2
            sp.wait_ge(s_scat[hf], 16 * TOPK * HT * (m // 2 + 1))

            def load(q, k):
                sp.wait_ge(s_rTp, JOBS * m + 4 * q + k - 3)
                sp.dma_start(rows[:, k, :], xr[hf][bass.ds((4 * q + k) * P, P), :]).then_inc(s_row[k], 16)

            def store(q, k):
                sp.wait_ge(s_y, JOBS * m + 4 * q + k + 1)
                sp.dma_start(yr[hf][bass.ds((4 * q + k) * P, P), :], ysb[:, k, :]).then_inc(s_yst[k], 16)

            def step(q, k, s):
                if s is None or s < JOBS:
                    if s is None or m or s >= 4:
                        load(q, k)
                    else:
                        sp.dma_start(rows[:, k, :], xr[hf][P * k:P * k + P, :]).then_inc(s_row[k], 16)
                if s is None or s >= 5:
                    store(*before(q, k, 5))

            looped(sp, step, 2, PJ, JOBS + 4)

        def jobs_tensor(m):
            pe = nc.tensor
            hf = m % 2
            pe.wait_ge(s_job, m + 1)
            if m == 0:
                pe.wait_ge(s_ww, 16 * 5)

            def turn(q, k):
                J = JOBS * m + 4 * q + k
                pe.wait_ge(s_row[k], 16 * (PJ * m + q + 1))
                if m or not isinstance(J, int) or J >= 2:
                    pe.wait_ge(s_rT, J - 1)
                pe.transpose(ps[:, 5 + k % 2, 0:P], rows[:, k, :], ident[:, :]).then_inc(s_rTp, 1)

            def up(q, k):
                J = JOBS * m + 4 * q + k
                pe.wait_ge(s_wj, J + 1)
                pe.wait_ge(s_rT, J + 1)
                if m or not isinstance(J, int) or J >= 2:
                    pe.wait_ge(s_hid, J - 1)
                for w in range(2):
                    for c in range(len(HC)):
                        ins = pe.matmul(ps[:, 2 * (k % 2) + w, P * c:P * c + P],
                                        wj[:, k % 2, w, P * c:P * c + P], rowsT[:, k % 2, :],
                                        start=True, stop=True)
                    ins.then_inc(s_AB, 1)

            def down(q, k):
                e = pe.value_load(job_expert[0:1, hf, bass.ds(4 * q + k, 1)], min_val=0, max_val=NE - 1)
                J = JOBS * m + 4 * q + k
                pe.wait_ge(s_hid, J + 1)
                if m or not isinstance(J, int) or J >= 1:
                    pe.wait_ge(s_y, J)
                for c, (h0, hw) in enumerate(HC):
                    ins = pe.matmul(ps[:, 7, 0:P], hid[0:hw, k % 2, P * c:P * c + P], w2s[0:hw, bass.ds(e, 1), c, :].squeeze(1),
                                    start=(c == 0), stop=(c == len(HC) - 1))
                ins.then_inc(s_yp, 1)

            def step(q, k, s):
                if s is None or s < JOBS - 1:
                    turn(*after(q, k))
                if s is None or s < JOBS:
                    up(q, k)
                if s is None or 1 <= s:
                    down(*before(q, k, 1))

            turn(0, 0)
            looped(pe, step, 1, PJ - 1, JOBS)

        def jobs_scalar(m):
            a = nc.scalar

            def step(q, k, s):
                J = JOBS * m + 4 * q + k
                a.wait_ge(s_AB, 2 * J + 1)
                if m or not isinstance(J, int) or J >= 2:
                    a.wait_ge(s_hid, J - 1)
                a.activation(silu[:, k % 2, :], ps[:, 2 * (k % 2), 0:HP], ACT.Silu).then_inc(s_silu, 1)

            looped(a, step, 1, PJ, JOBS - 1)

        def jobs_vector(m):
            v = nc.vector
            hf = m % 2

            def take_rows(q, k):
                J = JOBS * m + 4 * q + k
                v.wait_ge(s_rTp, J + 1)
                if m or not isinstance(J, int) or J >= 2:
                    v.wait_ge(s_AB, 2 * (J - 1))
                v.tensor_copy(rowsT[:, k % 2, :], ps[:, 5 + k % 2, 0:P]).then_inc(s_rT, 1)

            def take_weights(q, k):
                e = v.value_load(job_expert[0:1, hf, bass.ds(4 * q + k, 1)], min_val=0, max_val=NE - 1)
                J = JOBS * m + 4 * q + k
                if m or not isinstance(J, int) or J >= 2:
                    v.wait_ge(s_AB, 2 * (J - 1))
                v.tensor_copy(wj[:, k % 2, :, :].rearrange("p w h -> p (w h)"),
                              w13[:, bass.ds(e, 1), :, :].rearrange("p e w h -> p (e w h)")).then_inc(s_wj, 1)

            def mix(q, k):
                J = JOBS * m + 4 * q + k
                v.wait_ge(s_silu, J + 1)
                v.wait_ge(s_AB, 2 * J + 2)
                if m or not isinstance(J, int) or J >= 2:
                    v.wait_ge(s_yp, J - 1)
                v.tensor_tensor(hid[:, k % 2, :], silu[:, k % 2, :], ps[:, 2 * (k % 2) + 1, 0:HP], MUL).then_inc(s_hid, 1)

            def take_out(q, k):
                J = JOBS * m + 4 * q + k
                v.wait_ge(s_yp, J + 1)
                if m or not isinstance(J, int) or J >= 4:
                    v.wait_ge(s_yst[k], 16 * (PJ * m + q))
                v.tensor_copy(ysb[:, k, :], ps[:, 7, 0:P]).then_inc(s_y, 1)

            def step(q, k, s):
                if s is None or s < JOBS - 1:
                    take_rows(*after(q, k))
                    take_weights(*after(q, k))
                if s is None or s < JOBS:
                    mix(q, k)
                if s is None or s >= 1:
                    take_out(*before(q, k, 1))

            if m == 0:
                v.wait_ge(s_ww, 16 * 5)
                v.wait_ge(s_pad, 1)
            take_rows(0, 0)
            take_weights(0, 0)
            looped(v, step, 1, PJ - 1, JOBS)

        win = sb("win", [P, 3, C])
        wout = sb("wout", [P, C])
        cw = sb("cw", [P, 2, CONV_K])
        gn = sb("gn", [P, 1])
        cv = sb("cv", [P, 2, 2, T])
        sg = sb("sg", [P, 2, 4, T])
        gi = sb("gi", [P, 2, T])
        rec = sb("rec", [P, 2, T])
        gg = sb("gg", [P, 2, T])
        osq = sb("osq", [P, 2, T])
        og = sb("og", [P, 2, T])
        osb = sb("osb", [P, NT, C])
        msq = sb("msq", [P, NT])
        rms = sb("rms", [P, NT])

        s_wh = sem("s_wh")
        s_raw = sem("s_raw")
        s_tap = sem("s_tap")
        s_cv = sem("s_cv")
        s_sig = sem("s_sig")
        s_gi = sem("s_gi")
        s_rec = sem("s_rec")
        s_gg = sem("s_gg")
        s_osq = sem("s_osq")
        s_og = sem("s_og")
        s_ho = sem("s_ho")
        s_osb = sem("s_osb")
        s_ms = sem("s_ms")
        s_rt = sem("s_rt")
        s_xr = sem("s_xr")

        def rec_sync():
            sp = nc.sync
            for k, w in enumerate((Wi, Wf, Wg)):
                sp.dma_start(win[:, k, :], w).then_inc(s_wh, 16)
            sp.dma_start(wout[:, :], Wo).then_inc(s_wh, 16)
            sp.dma_start(cw[:, 0, :], conv_i).then_inc(s_wh, 16)
            sp.dma_start(cw[:, 1, :], conv_f).then_inc(s_wh, 16)
            sp.dma_start(gn[:, :], gnw.rearrange("(d a) -> d a", a=1)).then_inc(s_wh, 16)

        def raw_bank(b, k):
            return ps[:, 6 if k == 2 else 2 + k, :]

        def square_bank(hf):
            return ps[:, 1 if hf else 7, :]

        def rec_tensor():
            pe = nc.tensor
            pe.wait_ge(s_wh, 16 * 7)

            def project(b):
                pe.wait_ge(s_xT, 8 + b + 1)
                if b:
                    pe.wait_ge(s_gg, b)
                    pe.wait_ge(s_cv, 2 * b)
                for k in range(3):
                    pe.matmul(raw_bank(b, k), win[:, k, :], xT[:, T * b:T * b + T], start=True, stop=True).then_inc(s_raw, 1)

            def finish(b):
                pe.wait_ge(s_og, b + 1)
                pe.wait_ge(s_osq, b + 1)
                if b >= 2:
                    pe.wait_ge(s_osb, b - 1)
                for t in range(TB):
                    pe.matmul(ps[:, 4 + b % 2, P * t:P * t + P], og[:, b % 2, P * t:P * t + P], wout[:, :], start=True, stop=True)
                for t in range(TB):
                    i = TB * b + t
                    ins = pe.matmul(square_bank(b // 2)[:, i:i + 1], osq[:, b % 2, P * t:P * t + P], ones[:, 0:1], start=True, stop=True)
                ins.then_inc(s_ho, 1)

            for b in range(B):
                if b >= 2:
                    pe.wait_ge(s_xT, 8 + b - 1)
                turn_tensor(2, b, b % 2)
                project(b)
                if b:
                    finish(b - 1)
            finish(B - 1)

        def rec_scalar():
            a = nc.scalar
            for b in range(B):
                turn_scalar(2, b, b % 2)
                for k in range(2):
                    a.wait_ge(s_raw, 3 * b + k + 1)
                    if b >= 2 and k == 0:
                        a.wait_ge(s_gi, b - 1)
                    a.activation(cv[:, b % 2, k, :], raw_bank(b, k), ACT.Identity,
                                 scale=cw[:, k, CONV_K - 1:CONV_K]).then_inc(s_tap, 1)
                a.wait_ge(s_raw, 3 * b + 3)
                if b >= 2:
                    a.wait_ge(s_gg, b - 1)
                    a.wait_ge(s_rec, b - 1)
                a.activation(sg[:, b % 2, 3, :], raw_bank(b, 2), ACT.Sigmoid).then_inc(s_sig, 1)
                a.wait_ge(s_cv, 2 * b + 2)
                a.activation(sg[:, b % 2, 2, :], cv[:, b % 2, 0, :], ACT.Sigmoid).then_inc(s_sig, 1)
                a.activation(sg[:, b % 2, 1, :], cv[:, b % 2, 1, :], ACT.Sigmoid, scale=-1.0).then_inc(s_sig, 1)
                a.activation(sg[:, b % 2, 0, :], cv[:, b % 2, 1, :], ACT.Sigmoid).then_inc(s_sig, 1)
                a.wait_ge(s_rec, b + 1)
                if b >= 2:
                    a.wait_ge(s_ho, b - 1)
                a.activation(osq[:, b % 2, :], rec[:, b % 2, :], ACT.Square).then_inc(s_osq, 1)
                if b:
                    take_out_scalar(b - 1)
            take_out_scalar(B - 1)

        def take_out_scalar(b):
            nc.scalar.wait_ge(s_ho, b + 1)
            nc.scalar.activation(osb[:, TB * b:TB * b + TB, :].rearrange("p t c -> p (t c)"), ps[:, 4 + b % 2, :], ACT.Copy).then_inc(s_osb, 1)

        def rec_vector():
            v = nc.vector
            v.wait_ge(s_wh, 16 * 7)
            for b in range(B):
                if b % 2 == 0:
                    add_vector(b // 2)
                    norm_stats(2, b // 2)
                    norm_apply(2, b // 2)
                for k in range(2):
                    v.wait_ge(s_tap, 2 * b + k + 1)
                    for tap in range(CONV_K - 1):
                        d = CONV_K - 1 - tap
                        acc = cv[:, b % 2, k, d:T]
                        ins = v.scalar_tensor_tensor(acc, raw_bank(b, k)[:, 0:T - d], cw[:, k, tap:tap + 1], acc, MUL, ADD)
                        if tap < CONV_K - 2:
                            link(ins)
                    ins.then_inc(s_cv, 1)
                v.wait_ge(s_sig, 4 * b + 1)
                if b >= 2:
                    v.wait_ge(s_og, b - 1)
                v.scalar_tensor_tensor(gg[:, b % 2, :], raw_bank(b, 2), gn[:, 0:1], sg[:, b % 2, 3, :], MUL, MUL).then_inc(s_gg, 1)
                v.wait_ge(s_sig, 4 * b + 4)
                v.wait_ge(s_cv, 2 * b + 2)
                link(v.tensor_tensor(gi[:, b % 2, :], cv[:, b % 2, 0, :], sg[:, b % 2, 2, :], MUL))
                v.tensor_tensor(gi[:, b % 2, :], gi[:, b % 2, :], sg[:, b % 2, 1, :], MUL).then_inc(s_gi, 1)
                v.wait_ge(s_gi, b + 1)
                if b >= 2:
                    v.wait_ge(s_osq, b - 1)
                v.tensor_tensor_scan(rec[:, b % 2, :], sg[:, b % 2, 0, :], gi[:, b % 2, :], 0.0, MUL, ADD).then_inc(s_rec, 1)
            for hf in range(2):
                t = slice(HT * hf, HT * hf + HT)
                v.wait_ge(s_ho, 2 * hf + 2)
                v.tensor_scalar(msq[:, t], square_bank(hf)[:, t], 1.0 / C, LN_EPS, MUL, ADD).then_inc(s_ms, 1)
                v.wait_ge(s_rt, hf + 1)
                v.wait_ge(s_osb, 2 * hf + 2)
                for i in range(HT * hf, HT * hf + HT):
                    v.scalar_tensor_tensor(xt[:, i, :], osb[:, i, :], rms[:, i:i + 1], xt[:, i, :], MUL, ADD).then_inc(s_xr, 1)
            v.wait_ge(s_xr, NT)

        def rec_pool():
            g = nc.gpsimd
            for b in range(B):
                if b % 2 == 0:
                    norm_root(2, b // 2)
                g.wait_ge(s_gg, b + 1)
                g.wait_ge(s_rec, b + 1)
                if b >= 2:
                    g.wait_ge(s_ho, b - 1)
                g.tensor_tensor(og[:, b % 2, :], rec[:, b % 2, :], gg[:, b % 2, :], MUL).then_inc(s_og, 1)
            for hf in range(2):
                t = slice(HT * hf, HT * hf + HT)
                g.wait_ge(s_ms, hf + 1)
                g.tensor_tensor(rms[:, t], msq[:, t], mhalf[:, :], ALU.pow).then_inc(s_rt, 1)

        block = ctx.enter_context(nc.Block())

        @block.sync
        def _(sp):
            proj_sync()
            fill_sync()
            sp.wait_ge(s_fill, 64)
            for n in range(2 * B):
                stack_sync(n)
                if n == 1:
                    clear_sync()
            weights_sync()
            sp.wait_ge(s_xa, B)
            rec_sync()
            for m in range(4):
                jobs_sync(m)
            for hf in range(2):
                sp.wait_ge(s_xm, hf + 3)
                sp.dma_start(out_rows[:, HT * hf:HT * hf + HT, :], xt[:, HT * hf:HT * hf + HT, :]).then_inc(s_out, 16)
            sp.wait_ge(s_out, 32)

        @block.gpsimd
        def _(g):
            const_pool()
            heads_pool()
            pad_pool()
            prepare_pool(1)
            gather_pool(0)
            gather_pool(1)
            rec_pool()
            prepare_pool(2)
            prepare_pool(3)
            gather_pool(2)
            gather_pool(3)

        @block.scalar
        def _(a):
            for hf in range(2):
                proj_scalar(2 * hf)
                proj_scalar(2 * hf + 1)
                gates_scalar(hf)
                decays_scalar(hf)
            heads_scalar()
            prepare_scalar(1)
            jobs_scalar(0)
            jobs_scalar(1)
            rec_scalar()
            for m in (2, 3):
                prepare_scalar(m)
            for m in (2, 3):
                jobs_scalar(m)

        @block.tensor
        def _(pe):
            weights_tensor()
            for hf in range(2):
                proj_tensor(2 * hf)
                proj_tensor(2 * hf + 1)
                gates_tensor(hf)
            heads_tensor()
            prepare_tensor(1)
            jobs_tensor(0)
            jobs_tensor(1)
            rec_tensor()
            for m in (2, 3):
                prepare_tensor(m)
            for m in (2, 3):
                jobs_tensor(m)

        @block.vector
        def _(v):
            v.wait_ge(s_x, 64)
            for hf in range(2):
                norm_stats(0, hf)
                norm_apply(0, hf)
            for hf in range(2):
                bound_vector(hf)
                bound_scale_vector(hf)
                if hf == 0:
                    for k in range(5):
                        parts_vector(0, k)
                gates_vector(hf)
                gate_rows_vector(2 * hf)
                if hf == 0:
                    for k in range(5, 10):
                        parts_vector(0, k)
                gate_rows_vector(2 * hf + 1)
            heads_vector()
            prepare_vector(1)
            jobs_vector(0)
            jobs_vector(1)
            rec_vector()
            for m in (2, 3):
                prepare_vector(m)
            for m in (2, 3):
                jobs_vector(m)
            add_vector(2)
            add_vector(3)


_INS = ['L0_attn_a_x', 'L0_attn_a_W', 'L0_attn_b_Wi', 'L0_attn_b_Wf', 'L0_attn_b_Wg', 'L0_attn_b_conv_i',
        'L0_attn_b_conv_f', 'L0_attn_b_g_norm_weight', 'L0_attn_b_Wo', 'L0_ffn_gate_w', 'L0_ffn_expert_bias',
        'L0_ffn_w1', 'L0_ffn_w2', 'L0_ffn_w3']


def kernel(**inputs):
    import numpy as _np
    import concourse.bacc as _bacc
    from concourse import mybir as _mybir
    from concourse.bass_utils import run_bass_kernel_spmd as _run

    nc = _bacc.Bacc("TRN2", target_bir_lowering=False, num_devices=1)
    arrays, args = {}, []
    for name in _INS:
        a = _np.ascontiguousarray(inputs[name])
        arrays[f"in_{name}_dram"] = a
        args.append(nc.dram_tensor(f"in_{name}_dram", a.shape, _mybir.dt.from_np(a.dtype), kind="ExternalInput").ap())
    args.append(nc.dram_tensor("out_0_dram", (B, T, C), F32, kind="ExternalOutput").ap())
    build(nc, *args)
    r = _run(nc, [arrays], core_ids=[0])
    return r.results[0]["out_0_dram"]
```

```python
from contextlib import ExitStack

import concourse.bass as bass
from concourse import mybir

F32 = mybir.dt.float32
BF16 = mybir.dt.bfloat16
I32 = mybir.dt.int32
U32 = mybir.dt.uint32
ALU = mybir.AluOpType
ACT = mybir.ActivationFunctionType
AX = mybir.AxisListType
ADD, SUB, MUL = ALU.add, ALU.subtract, ALU.mult

P = 128
B, T, C = 4, 512, 128
NT = B * T // P
TB = T // P
H, HS = 16, 8
VW = HS + 1
GH = 4
NG = H // GH
GROUPS = B * NG
NE, HID = 8, 352
HC = [(0, 128), (128, 128), (256, 96)]
HP = P * len(HC)
TOPK = 2
HT = NT // 2
JOBS = 24
LN_EPS = 1e-5
LOG_EPS = 1e-7
CONV_K = 4
NEG = -1e30

OFF = [(i, j) for i in range(1, TB) for j in range(i)]
PAIR = {ij: n for n, ij in enumerate(OFF + [(j, j) for j in range(TB)])}
NOFF = len(OFF)
UNITS = 10


def unit_plan():
    plan = []
    for r in range(0, GH, 2):
        plan += [("diag", r), ("far", r), ("diag", r + 1), ("far", r + 1), ("mid", r)]
    return plan


PLAN = unit_plan()


def block_at(r, i, j):
    if i == j:
        return PLAN.index(("diag", r)), P * j
    if j == 1:
        return PLAN.index(("mid", r - r % 2)), 256 * (r % 2) + P * (i - 2)
    u = PLAN.index(("far", r))
    return (u, P * (i - 1)) if j == 0 else (u, 384)


def build(nc, x, W, Wi, Wf, Wg, conv_i, conv_f, gnw, Wo, gate_w, ebias, w1, w2, w3, out):
    x_rows = x.rearrange("b (t p) c -> p (b t) c", p=P)
    out_rows = out.rearrange("b (t p) c -> p (b t) c", p=P)
    xr = [nc.dram_tensor(f"routed_rows{hf}", [JOBS * P, C], F32, kind="Internal").ap() for hf in range(2)]
    parts_d = nc.dram_tensor("parts", [2, 2, H, 5, HS, T], BF16, kind="Internal").ap()
    gates_d = nc.dram_tensor("gates", [2, 2, H, 3, T], BF16, kind="Internal").ap()
    yr = [nc.dram_tensor(f"routed_out{hf}", [JOBS * P, C], F32, kind="Internal").ap() for hf in range(2)]

    with ExitStack() as ctx:
        def sb(name, shape, dt=F32):
            return ctx.enter_context(nc.sbuf_tensor(name, shape, dt))

        def sem(name):
            return ctx.enter_context(nc.semaphore(name))

        ps = ctx.enter_context(nc.psum_tensor("ps", [P, 8, 512], F32))

        ident = sb("ident", [P, P])
        identb = sb("identb", [P, P], BF16)
        tri = sb("tri", [P, P])
        ones = sb("ones", [P, P])
        trib = sb("trib", [P, P], BF16)
        onesb = sb("onesb", [P, P], BF16)
        negmask = sb("negmask", [P, TB, P], BF16)
        iom8 = sb("iom8", [P, NE])
        iojob = sb("iojob", [P, JOBS])
        io128 = sb("io128", [P, HT])
        carry1 = sb("carry1", [P, NE, HT])
        zeros = sb("zeros", [P, C])
        mhalf = sb("mhalf", [P, HT])
        ebt = sb("ebt", [P, NE])
        WT = sb("WT", [P, 3 * C + H])
        gwT = sb("gwT", [P, NE])
        xt = sb("xt", [P, NT, C])
        xh = sb("xh", [P, NT, C])
        xT = sb("xT", [P, NT * P])
        xs = [xT[:, :].rearrange("p (i c) -> p i c", i=NT), xh[:, :, :]]
        st6 = sb("st6", [P, NT, 6])
        mv = sb("mv", [P, NT, 2])
        lnv = sb("lnv", [P, NT])
        lnr = sb("lnr", [P, NT])
        lnt = sb("lnt", [P, NT])

        s_const = sem("s_const")
        s_x = sem("s_x")
        s_w = sem("s_w")
        s_eb = sem("s_eb")
        s_zero = sem("s_zero")
        s_dve = sem("s_dve")
        s_act = sem("s_act")
        s_pool = sem("s_pool")
        s_var = sem("s_var")
        s_std = sem("s_std")
        s_first_var = sem("s_first_var")
        s_first_std = sem("s_first_std")
        s_norm = sem("s_norm")
        s_xTp = sem("s_xTp")
        s_xT = sem("s_xT")
        s_out = sem("s_out")
        count = {"dve": 0, "act": 0, "pool": 0}

        own = {"dve": (nc.vector, s_dve), "act": (nc.scalar, s_act), "pool": (nc.gpsimd, s_pool)}

        def link(ins, who="dve"):
            count[who] += 1
            engine, done = own[who]
            ins.then_inc(done, 1)
            engine.wait_ge(done, count[who])

        def bc(ap, shape):
            return ap.to_broadcast(shape)

        def norm_tiles(hf, piece):
            return range(HT * hf, HT * hf + HT) if piece is None else range(HT * hf + 2 * piece, HT * hf + 2 * piece + 2)

        def norm_stats(n, hf, piece=None):
            v = nc.vector
            t = norm_tiles(hf, piece)
            for i in t:
                ins = v.bn_stats(st6[:, i, :], xt[:, i, :])
            link(ins)
            for i in t:
                ins = v.bn_aggr(mv[:, i, :], st6[:, i, :])
            if piece in (None, HT // 2 - 1):
                ins.then_inc(s_var, 1)
            elif piece == HT // 4 - 1:
                ins.then_inc(s_first_var, 1)

        def norm_root(n, hf, batch=None):
            g = nc.gpsimd
            lo, w = (HT * hf, HT) if batch is None else (HT * hf + TB * batch, TB)
            t = slice(lo, lo + w)
            if batch == 0:
                g.wait_ge(s_first_var, 1)
            else:
                g.wait_ge(s_var, 2 * n + hf + 1)
            link(g.tensor_scalar(lnv[:, t], mv[:, t, 1], LN_EPS, None, ADD), who="pool")
            g.tensor_tensor(lnr[:, t], lnv[:, t], mhalf[:, 0:w], ALU.pow).then_inc(s_first_std if batch == 0 else s_std, 1)

        def norm_apply(n, hf, piece=None):
            v = nc.vector
            if n:
                v.wait_ge(s_xTp, 4 * n - 2 + 2 * hf)
            if piece is not None and piece < HT // 4:
                v.wait_ge(s_first_std, 1)
            else:
                v.wait_ge(s_std, 2 * n + hf + 1)
            for i in norm_tiles(hf, piece):
                v.tensor_scalar(xh[:, i, :], xt[:, i, :], mv[:, i, 0:1], lnr[:, i:i + 1], SUB, MUL).then_inc(s_norm, 1)

        def turn_tensor(n, c, bank):
            pe = nc.tensor
            pe.wait_ge(s_norm, NT * n + 4 * c + 4)
            for k in range(4):
                i = 4 * c + k
                ins = pe.transpose(ps[:, bank, P * k:P * k + P], xh[:, i, :], ident[:, :])
            ins.then_inc(s_xTp, 1)

        def turn_scalar(n, c, bank):
            a = nc.scalar
            a.wait_ge(s_xTp, 4 * n + c + 1)
            a.activation(xT[:, 512 * c:512 * c + 512], ps[:, bank, :], ACT.Copy).then_inc(s_xT, 1)

        L8 = sb("L8", [P, HT, NE])
        V8 = sb("V8", [P, HT, NE])
        Q8 = sb("Q8", [P, HT, NE])
        oh = sb("oh", [P, TOPK, HT, NE])
        m1 = sb("m1", [P, HT])
        m2 = sb("m2", [P, HT])
        wts = sb("wts", [P, TOPK, HT])
        chosen = sb("chosen", [P, HT, NE], BF16)
        totE = sb("totE", [P, NE, HT])
        cumE = sb("cumE", [P, NE, HT])
        base = sb("base", [P, HT, NE])
        tiles = sb("tiles", [P, NE])
        ends = sb("ends", [P, NE])
        first = sb("first", [P, NE])
        cmp16 = sb("cmp16", [P, NE, HT])
        cmpj = sb("cmpj", [P, JOBS, NE])
        slotf = sb("slotf", [P, TOPK, HT])
        slots = sb("slots", [P, 2, TOPK, HT], U32)
        jobf = sb("jobf", [P, JOBS])
        job_expert = sb("job_expert", [P, 2, JOBS], I32)

        room = sb("room", [P, (2 * B + B) * T])
        qk = room[:, 0:2 * B * T].rearrange("p (n b t) -> p n b t", n=2, b=B)
        GT = room[0:H, 2 * B * T:3 * B * T].rearrange("p (b t) -> p b t", b=B)
        w13 = room[:, 0:NE * 2 * HP].rearrange("p (e m h) -> p e m h", e=NE, m=2)
        room2 = sb("room2", [P, 2 * 3 * T])
        part = room2[:, :].bitcast(BF16).rearrange("p (a n k t) -> p a n k t", a=2, n=2, k=3)
        w2s = room2[:, 0:NE * len(HC) * C].rearrange("p (e k c) -> p e k c", e=NE, k=len(HC))

        att = ctx.enter_context(ExitStack())

        def asb(name, shape, dt=F32):
            return att.enter_context(nc.sbuf_tensor(name, shape, dt))

        Wrows = asb("Wrows", [P, 3, C])
        Wgr = asb("Wgr", [H, C])
        gwr = asb("gwr", [NE, C])
        PP = asb("PP", [P, 2, UNITS, 512])
        rest = asb("rest", [P, 2, T])
        mx = asb("mx", [P, B, 2])
        mxa = asb("mxa", [P, B, 2])
        fs = asb("fs", [P, B])
        feps = asb("feps", [P, B])
        va = asb("va", [P, NT, H, VW])
        z = asb("z", [P, NT, H])
        az = asb("az", [P, NT, H])
        lg = asb("lg", [P, NT, H])
        Gt = asb("Gt", [P, B, TB, H])
        Ct = asb("Ct", [P, B, TB, H])
        dec = asb("dec", [P, B, NOFF, H])
        rowf = asb("rowf", [P, B, TB, H])
        gp = asb("gp", [H, 2, 3, T], BF16)
        gr = asb("gr", [H, T])
        vp = asb("vp", [P, 2, len(PAIR), H, VW])
        QS = asb("QS", [102, 2, 8, T], BF16)
        KS = asb("KS", [102, 2, 8, T], BF16)
        A = asb("A", [P, 4, 512])
        E = asb("E", [P, 4, 512])
        OT = asb("OT", [P, 7, P])
        tmp = asb("tmp", [P, 3, GH, VW])
        YS = asb("YS", [P, TB, H, VW])
        rn = asb("rn", [P, TB, H])

        s_wT = sem("s_wT")
        s_wTc = sem("s_wTc")
        s_qkp = sem("s_qkp")
        s_qk = sem("s_qk")
        s_vzp = sem("s_vzp")
        s_vz = sem("s_vz")
        s_l = sem("s_l")
        s_lg = sem("s_lg")
        s_gp = sem("s_gp")
        s_gt = sem("s_gt")
        s_dif = sem("s_dif")
        s_exp = sem("s_exp")
        s_gTp = sem("s_gTp")
        s_gT = sem("s_gT")
        s_mx = sem("s_mx")
        s_mxa = sem("s_mxa")
        s_fs = sem("s_fs")
        s_part = sem("s_part")
        s_gpart = sem("s_gpart")
        s_vp = sem("s_vp")
        s_store = sem("s_store")
        s_stack = [sem("s_stack0"), sem("s_stack1")]
        s_fill = sem("s_fill")
        s_zb = sem("s_zb")
        s_S = sem("s_S")
        s_A = sem("s_A")
        s_Q = sem("s_Q")
        s_D = sem("s_D")
        s_E = sem("s_E")
        s_PD = sem("s_PD")
        s_pv = sem("s_pv")
        s_Oo = sem("s_Oo")
        s_Od = sem("s_Od")
        s_OT = sem("s_OT")
        s_Y = sem("s_Y")
        s_xa = sem("s_xa")

        BK_S, BK_D, BK_OFF, BK_DIA, BK_T = 0, 3, 5, 6, 7
        NCONST = 13
        PARTS, GPARTS = 9, 5
        STACKS = 16 * 8
        STORES = 16 * 10

        def proj_sync():
            sp = nc.sync
            for b in range(B):
                sp.dma_start(xt[:, TB * b:TB * b + TB, :], x_rows[:, TB * b:TB * b + TB, :]).then_inc(s_x, 16)
            sp.dma_start(Wrows[:, :, :], W[0:3 * C, :].rearrange("(n p) c -> p n c", p=P)).then_inc(s_w, 16)
            sp.dma_start(Wgr[:, :], W[3 * C:3 * C + H, :]).then_inc(s_w, 16)
            sp.dma_start(gwr[:, :], gate_w).then_inc(s_w, 16)
            sp.dma_start(ebt[:, :], ebias.partition_broadcast(P)).then_inc(s_eb, 16)

        def fill_sync():
            sp = nc.sync
            sp.wait_ge(s_const, 4)
            for t in (QS, KS):
                rows96 = t[72:96].rearrange("p s h t -> p (s h t)").bitcast(F32).rearrange("p (n c) -> p n c", c=C)
                sp.dma_start(rows96, bc(zeros[0:24, :].unsqueeze(1), [24, rows96.shape[1], C])).then_inc(s_fill, 16)
                gates = t[96:102].rearrange("p s h (n c) -> p (s h n) c", c=P)
                sp.dma_start(gates, bc(onesb[0:6, :].unsqueeze(1), [6, gates.shape[1], P])).then_inc(s_fill, 16)

        def clear_sync():
            sp = nc.sync
            sp.wait_ge(s_const, NCONST)
            for hf in range(2):
                sp.dma_start(xr[hf].rearrange("(p n) c -> p n c", p=P),
                             bc(zeros[:, :].unsqueeze(1), [P, JOBS, C])).then_inc(s_zero, 16)

        def stack_sync(n):
            sp, b, half, slot = nc.sync, n // 2, n % 2, n % 2
            if half == 0:
                sp.wait_ge(s_part, PARTS * (b + 1))
                if b >= 2:
                    sp.wait_ge(s_stack[0], STACKS * (b - 1))
                    sp.wait_ge(s_stack[1], STACKS * (b - 1))
                for which, pieces in ((0, 3), (1, 5)):
                    for k in range(pieces):
                        sp.dma_start(parts_d[b % 2, which, :, k, :, :], part[:, b % 2, which, k % 3, :]).then_inc(s_store, 16)
                sp.wait_ge(s_gpart, GPARTS * (b + 1))
                for n2 in range(2):
                    sp.dma_start(gates_d[b % 2, n2], gp[:, n2, :, :]).then_inc(s_store, 16)
                sp.wait_ge(s_store, STORES * (b + 1))
            if n >= 2:
                sp.wait_ge(s_S, UNITS * 2 * (n - 1))
            heads = slice(8 * half, 8 * half + 8)
            for k in range(3):
                sp.dma_start(QS[24 * k:24 * k + 24, slot, :, :],
                             parts_d[b % 2, 0, heads, 0:3, :, :].rearrange("h k d t -> (k d) h t")).then_inc(s_stack[slot], 16)
                sp.dma_start(KS[24 * k:24 * k + 24, slot, :, :],
                             parts_d[b % 2, 1, heads, k:k + 3, :, :].rearrange("h k d t -> (k d) h t")).then_inc(s_stack[slot], 16)
            if n >= 2:
                sp.wait_ge(s_D, 8 * (n - 1))
            sp.dma_start(QS[96:99, slot, :, :], gates_d[b % 2, 0, heads].rearrange("h k t -> k h t")).then_inc(s_stack[slot], 16)
            sp.dma_start(KS[99:102, slot, :, :], gates_d[b % 2, 1, heads].rearrange("h k t -> k h t")).then_inc(s_stack[slot], 16)

        def const_pool():
            g = nc.gpsimd

            def part1(t, v):
                link(g.memset(t[:], v), who="pool")

            def triangle(t, op, fill, base, pattern, cm):
                g.affine_select(out=t[:], in_=t[:], compare_op=op, fill=fill, base=base,
                                pattern=pattern, channel_multiplier=cm).then_inc(s_const, 1)

            part1(ident, 0.0)
            triangle(ident, ALU.not_equal, 1.0, 0, [[-1, P]], 1)
            part1(tri, 1.0)
            triangle(tri, ALU.is_ge, 0.0, 0, [[1, P]], -1)
            g.memset(zeros[:, :], 0.0).then_inc(s_const, 1)
            g.memset(onesb[:, :], 1.0).then_inc(s_const, 1)
            g.memset(ones[:, :], 1.0).then_inc(s_const, 1)
            g.memset(va[:, :, :, HS:VW], 1.0).then_inc(s_const, 1)
            link(g.memset(mhalf[:, :], -0.5), who="pool")
            norm_root(0, 0)
            part1(identb, 0.0)
            triangle(identb, ALU.not_equal, 1.0, 0, [[-1, P]], 1)
            part1(negmask, 0.0)
            triangle(negmask, ALU.is_ge, NEG, 0, [[0, TB], [1, P]], -1)
            norm_root(0, 1)
            bound_pool(0)
            part1(trib, 1.0)
            triangle(trib, ALU.is_ge, 0.0, -1, [[1, P]], -1)
            g.iota(iom8[:, :], [[1, NE]], base=-8, channel_multiplier=0, allow_small_or_imprecise_dtypes=True).then_inc(s_const, 1)
            g.iota(iojob[:, :], [[1, JOBS]], base=0, channel_multiplier=0, allow_small_or_imprecise_dtypes=True).then_inc(s_const, 1)
            g.iota(io128[:, :], [[P, HT]], base=0, channel_multiplier=0, allow_small_or_imprecise_dtypes=True).then_inc(s_const, 1)
            part1(carry1, 1.0)
            g.memset(carry1[:, :, 0:1], 0.0).then_inc(s_const, 1)
            bound_pool(1)
            for n in range(len(PAIR)):
                decayed_pool(0, n)

        def bound_pool(hf):
            g = nc.gpsimd
            g.wait_ge(s_mx, 4 * (hf + 1))
            b2 = slice(2 * hf, 2 * hf + 2)
            g.partition_all_reduce(mxa[:, b2, :].rearrange("p b n -> p (b n)"), mx[:, b2, :].rearrange("p b n -> p (b n)"),
                                   P, bass.bass_isa.ReduceOp.max).then_inc(s_mxa, 1)

        def weights_tensor():
            pe = nc.tensor
            pe.wait_ge(s_const, 1)
            pe.wait_ge(s_w, 48)
            for n in range(3):
                pe.transpose(ps[:, 7, P * n:P * n + P], Wrows[:, n, :], ident[:, :])
            pe.transpose(ps[:, 7, 3 * P:3 * P + H], Wgr[:, :], ident[0:H, 0:H])
            pe.transpose(ps[:, 7, 3 * P + H:3 * P + H + NE], gwr[:, :], ident[0:NE, 0:NE]).then_inc(s_wT, 1)

        def proj_tensor(b):
            pe = nc.tensor
            if b >= 2:
                pe.wait_ge(s_xT, b - 1)
            turn_tensor(0, b, b % 2)
            pe.wait_ge(s_xT, b + 1)
            if b == 0:
                pe.wait_ge(s_wTc, 2)
            for n in range(2):
                if b:
                    pe.wait_ge(s_qk, 2 * b - 1 + n)
                pe.matmul(ps[:, 2 + n, :], WT[:, C * n:C * n + C], xT[:, T * b:T * b + T],
                          start=True, stop=True).then_inc(s_qkp, 1)
            if b:
                pe.wait_ge(s_vz, 2 * b)
            for t in range(TB):
                i = TB * b + t
                ins = pe.matmul(ps[:, 4 + t // 2, 256 * (t % 2):256 * (t % 2) + C + H], xT[:, P * i:P * i + P],
                                WT[:, 2 * C:3 * C + H], start=True, stop=True)
            ins.then_inc(s_vzp, 1)

        def gates_tensor(hf):
            pe = nc.tensor
            pe.wait_ge(s_lg, hf + 1)
            pe.wait_ge(s_const, 5)
            if hf:
                pe.wait_ge(s_gt, 1)
            for o, m in ((0, tri), (HT * H, ones)):
                ins = pe.matmul(ps[:, 6, o:o + HT * H], m[:, :], lg[:, HT * hf:HT * hf + HT, :].rearrange("p t h -> p (t h)"),
                                start=True, stop=True)
            ins.then_inc(s_gp, 1)
            pe.wait_ge(s_gt, hf + 1)
            for b in range(2 * hf, 2 * hf + 2):
                if b == 0:
                    pe.wait_ge(s_wTc, 2)
                else:
                    pe.wait_ge(s_gT, b)
                for i in range(TB):
                    ins = pe.transpose(ps[0:H, 7, P * i:P * i + P], Gt[:, b, i, :], ident[:, :])
                ins.then_inc(s_gTp, 1)

        def proj_scalar(b):
            a = nc.scalar
            if b == 0:
                a.wait_ge(s_wT, 1)
                a.activation(WT[:, :], ps[:, 7, 0:3 * C + H], ACT.Copy).then_inc(s_wTc, 1)
                a.activation(gwT[:, :], ps[:, 7, 3 * C + H:3 * C + H + NE], ACT.Copy).then_inc(s_wTc, 1)
            turn_scalar(0, b, b % 2)
            for n in range(2):
                a.wait_ge(s_qkp, 2 * b + n + 1)
                a.activation(qk[:, n, b, :], ps[:, 2 + n, :], ACT.Copy).then_inc(s_qk, 1)
            a.wait_ge(s_vzp, b + 1)
            a.wait_ge(s_const, 6)
            for t in range(0, TB, 2):
                i = TB * b + t
                src = ps[:, 4 + t // 2, :].rearrange("p (n c) -> p n c", n=2)
                for k in range(2):
                    a.activation(va[:, i + k, :, 0:HS], src[:, k, 0:C].rearrange("p (h d) -> p h d", h=H), ACT.Copy)
                a.activation(z[:, i:i + 2, :], src[:, :, C:C + H], ACT.Copy).then_inc(s_vz, 1)

        def gates_scalar(hf):
            a = nc.scalar
            t = slice(HT * hf, HT * hf + HT)
            a.wait_ge(s_vz, 4 * (hf + 1))
            link(a.activation(az[:, t], z[:, t], ACT.Abs), who="act")
            link(a.activation(az[:, t], az[:, t], ACT.Exp, scale=-1.0), who="act")
            a.activation(az[:, t], az[:, t], ACT.Ln, bias=1.0).then_inc(s_l, 1)

        def decays_scalar(hf):
            a = nc.scalar
            b2 = slice(2 * hf, 2 * hf + 2)
            a.wait_ge(s_dif, hf + 1)
            a.activation(dec[:, b2], dec[:, b2], ACT.Exp).then_inc(s_exp, 1)
            a.activation(rowf[:, b2, 1:TB, :], rowf[:, b2, 1:TB, :], ACT.Exp).then_inc(s_exp, 1)

        def gates_vector(hf):
            v = nc.vector
            t = slice(HT * hf, HT * hf + HT)
            b2 = slice(2 * hf, 2 * hf + 2)
            v.wait_ge(s_l, hf + 1)
            v.scalar_tensor_tensor(lg[:, t], z[:, t], 0.0, az[:, t], ALU.min, SUB).then_inc(s_lg, 1)
            v.wait_ge(s_gp, hf + 1)
            own, whole = (ps[:, 6, o:o + HT * H].rearrange("p (b t h) -> p b t h", b=2, t=TB) for o in (0, HT * H))
            v.tensor_copy(Gt[:, b2, 0, :], own[:, :, 0])
            link(v.tensor_copy(Ct[:, b2, 1, :], whole[:, :, 0]))
            for i in range(2, TB):
                link(v.tensor_tensor(Ct[:, b2, i, :], Ct[:, b2, i - 1, :], whole[:, :, i - 1], ADD))
            v.tensor_tensor(Gt[:, b2, 1:TB, :], Ct[:, b2, 1:TB, :], own[:, :, 1:TB], ADD).then_inc(s_gt, 1)
            v.wait_ge(s_gt, hf + 1)
            n = 0
            for i in range(1, TB):
                v.tensor_tensor(dec[:, b2, n:n + i, :], bc(Ct[:, b2, i:i + 1, :], [P, 2, i, H]), Gt[:, b2, 0:i, :], SUB)
                n += i
            v.tensor_tensor(rowf[:, b2, 1:TB, :], Gt[:, b2, 1:TB, :], Ct[:, b2, 1:TB, :], SUB).then_inc(s_dif, 1)

        def gate_rows_vector(b):
            v = nc.vector
            v.wait_ge(s_gTp, b + 1)
            v.tensor_copy(GT[:, b, :], ps[0:H, 7, :]).then_inc(s_gT, 1)

        def bound_vector(hf):
            v = nc.vector
            for b in range(2 * hf, 2 * hf + 2):
                for n in range(2):
                    v.wait_ge(s_qk, 2 * b + n + 1)
                    v.tensor_reduce(mx[:, b, n:n + 1], qk[:, n, b, :], AX.X, ALU.max, apply_absolute_value=True).then_inc(s_mx, 1)

        def bound_scale_vector(hf):
            v = nc.vector
            b2 = slice(2 * hf, 2 * hf + 2)
            v.wait_ge(s_mxa, hf + 1)
            link(v.tensor_scalar(mxa[:, b2, :], mxa[:, b2, :], 1e-8, None, MUL))
            link(v.tensor_tensor(fs[:, b2], mxa[:, b2, 0], mxa[:, b2, 1], MUL))
            link(v.tensor_scalar(fs[:, b2], fs[:, b2], 1e-20, 1e30, ALU.max, ALU.min))
            link(v.reciprocal(fs[:, b2], fs[:, b2]))
            link(v.tensor_scalar(fs[:, b2], fs[:, b2], 1.25, 1.0, MUL, ALU.min))
            v.tensor_scalar(feps[:, b2], fs[:, b2], LOG_EPS, None, MUL).then_inc(s_fs, 1)

        def parts_vector(b, step):
            v = nc.vector
            pt = part[:, b % 2]
            done, gdone = PARTS * b, GPARTS * b
            if step == 0:
                if b >= 2:
                    v.wait_ge(s_store, STORES * (b - 1))
                v.tensor_scalar(qk[:, 0, b, :], qk[:, 0, b, :], fs[:, b:b + 1], None, MUL).then_inc(s_part, 1)
            elif step == 1:
                v.wait_ge(s_part, done + 1)
                for n in range(2):
                    v.tensor_copy(pt[:, n, 0, :], qk[:, n, b, :]).then_inc(s_part, 1)
            elif step == 2:
                v.wait_ge(s_part, done + 3)
                for n in range(2):
                    v.tensor_tensor(rest[:, n, :], qk[:, n, b, :], pt[:, n, 0, :], SUB).then_inc(s_part, 1)
            elif step == 3:
                v.wait_ge(s_part, done + 5)
                for n in range(2):
                    v.tensor_copy(pt[:, n, 1, :], rest[:, n, :]).then_inc(s_part, 1)
            elif step == 4:
                v.wait_ge(s_part, done + 7)
                for n in range(2):
                    v.tensor_tensor(pt[:, n, 2, :], rest[:, n, :], pt[:, n, 1, :], SUB).then_inc(s_part, 1)
            elif step == 5:
                if b:
                    v.wait_ge(s_store, STORES * b)
                v.wait_ge(s_gT, b + 1)
                v.tensor_copy(gp[:, 0, 0, :], GT[:, b, :]).then_inc(s_gpart, 1)
            elif step == 6:
                v.wait_ge(s_gpart, gdone + 1)
                v.tensor_tensor(gr[:, :], GT[:, b, :], gp[:, 0, 0, :], SUB).then_inc(s_gpart, 1)
            elif step == 7:
                v.wait_ge(s_gpart, gdone + 2)
                v.tensor_copy(gp[:, 0, 1, :], gr[:, :]).then_inc(s_gpart, 1)
            elif step == 8:
                v.wait_ge(s_gpart, gdone + 3)
                v.tensor_tensor(gp[:, 0, 2, :], gr[:, :], gp[:, 0, 1, :], SUB).then_inc(s_gpart, 1)
            elif step == 9:
                v.wait_ge(s_gpart, gdone + 4)
                v.tensor_scalar(gp[:, 1, :, :], gp[:, 0, :, :], -1.0, None, MUL).then_inc(s_gpart, 1)

        def decayed_pool(b, n):
            g = nc.gpsimd
            if n == 0:
                g.wait_ge(s_exp, 2 * (b // 2) + 2)
                g.wait_ge(s_vz, 2 * b + 2)
                if b >= 2:
                    g.wait_ge(s_pv, UNITS * NG * (b - 1))
            j = (OFF + [(k, k) for k in range(TB)])[n][1]
            if n < NOFF:
                g.tensor_tensor(vp[:, b % 2, n, :, :], va[:, TB * b + j, :, :],
                                bc(dec[:, b, n, :].unsqueeze(2), [P, H, VW]), MUL).then_inc(s_vp, 1)
            else:
                g.tensor_copy(vp[:, b % 2, n, :, :], va[:, TB * b + j, :, :]).then_inc(s_vp, 1)

        LAG = 4
        LAST = UNITS * (GROUPS + 2) + LAG + 4

        def at(U, offset, stage, width=1):
            G, n = divmod(U - offset, UNITS)
            if 0 <= G < GROUPS and n < width:
                stage(G, n)

        def scores_tensor(G, u):
            pe = nc.tensor
            b, g = divmod(G, NG)
            n, half = 2 * b + g // 2, g % 2
            slot = n % 2
            kind, r = PLAN[u]
            U = UNITS * G + u
            if u == 0 and half == 0:
                pe.wait_ge(s_stack[slot], STACKS * (b + 1))
            if U >= 3:
                pe.wait_ge(s_A, U - 2)
            bank = ps[:, BK_S + U % 3, :]

            def block(col, width, r, j, t0):
                h = 4 * half + r
                return pe.matmul(bank[:, col:col + width], KS[0:96, slot, h, P * j:P * j + P],
                                 QS[0:96, slot, h, t0:t0 + width], start=True, stop=True)

            if kind == "diag":
                for j in range(TB):
                    ins = block(P * j, P, r, j, P * j)
            elif kind == "far":
                block(0, 384, r, 0, P)
                ins = block(384, P, r, 2, 3 * P)
            else:
                block(0, 256, r, 1, 2 * P)
                ins = block(256, 256, r + 1, 1, 2 * P)
            ins.then_inc(s_S, 1)
            if kind == "diag":
                hh = GH * G + r
                if hh >= 2:
                    pe.wait_ge(s_E, hh - 1)
                h = 4 * half + r
                dst = ps[:, BK_D + hh % 2, :]
                for j in range(TB):
                    pe.matmul(dst[:, P * j:P * j + P], KS[96:102, slot, h, P * j:P * j + P], QS[96:102, slot, h, P * j:P * j + P],
                              start=(j == 0), stop=False, skip_group_check=True)
                pe.matmul(dst, identb[:, :], negmask[:, :, :].rearrange("p j t -> p (j t)"), start=False, stop=True,
                          skip_group_check=True).then_inc(s_D, 1)

        def sums_tensor(G, n):
            pe = nc.tensor
            b, g = divmod(G, NG)
            i, j = (OFF + [(k, k) for k in range(TB)])[n]
            if n == 0:
                pe.wait_ge(s_vp, len(PAIR) * (b + 1))
                pe.wait_ge(s_Q, UNITS * (G + 1))
                if G:
                    pe.wait_ge(s_Oo, G)
            if n == NOFF:
                pe.wait_ge(s_PD, GH * (G + 1))
                if G:
                    pe.wait_ge(s_Od, G)
            bank = BK_OFF if i != j else BK_DIA
            for r in range(GH):
                u, col = block_at(r, i, j)
                ins = pe.matmul(ps[32 * r:32 * r + VW, bank, P * i:P * i + P], vp[:, b % 2, n, GH * g + r, :],
                                PP[:, G % 2, u, col:col + P], start=(n in (0, NOFF)), stop=False, skip_group_check=True)
            ins.then_inc(s_pv, 1)

        def turn_sums_tensor(G, part2):
            pe = nc.tensor
            if part2:
                pe.wait_ge(s_Y, 2 * G + 1)
                pe.wait_ge(s_Od, G + 1)
            else:
                pe.wait_ge(s_Oo, G + 1)
                if G:
                    pe.wait_ge(s_Y, 2 * G)
            for k in range(4) if part2 else range(3):
                ins = pe.transpose(ps[:, BK_T, P * k:P * k + P], OT[:, (3 if part2 else 0) + k, :], ident[:, :])
            ins.then_inc(s_OT, 1)

        def heads_tensor():
            pe = nc.tensor
            pe.wait_ge(s_gT, B)
            pe.wait_ge(s_vz, 2 * B)
            pe.wait_ge(s_zb, 2)
            pe.wait_ge(s_fill, 64)
            pe.wait_ge(s_const, 8)
            for U in range(LAST):
                if U < UNITS * GROUPS:
                    scores_tensor(*divmod(U, UNITS))
                at(U, UNITS + LAG, lambda G, n: sums_tensor(G, n), UNITS)
                at(U, 2 * UNITS + LAG, lambda G, n: turn_sums_tensor(G, False))
                at(U, 2 * UNITS + LAG + 4, lambda G, n: turn_sums_tensor(G, True))
                prepare_heads_tensor(U)

        def heads_vector():
            v = nc.vector
            v.wait_ge(s_vz, 2 * B)
            for k in (BK_OFF, BK_DIA):
                v.memset(ps[:, k, :], 0.0).then_inc(s_zb, 1)
            for U in range(LAST):
                if U < UNITS * GROUPS:
                    v.wait_ge(s_S, U + 1)
                    if U >= 4:
                        v.wait_ge(s_Q, U - 3)
                    v.tensor_scalar(A[:, U % 4, :].bitcast(I32), ps[:, BK_S + U % 3, :].bitcast(I32),
                                    0x7fffffff, None, ALU.bitwise_and).then_inc(s_A, 1)
                at(U, 2 * UNITS + LAG + 1, lambda G, n: combine_vector(G, False))
                at(U, 2 * UNITS + LAG + 5, lambda G, n: combine_vector(G, True))
                b, k = divmod(U, UNITS * NG)
                if b + 1 < B and k % 2 == 0 and k < 20:
                    parts_vector(b + 1, k // 2)
                for stage in stages_at(IN_HEADS, U):
                    prepare_vector(0, stage)

        def combine_vector(G, part2):
            v = nc.vector
            b, g = divmod(G, NG)
            v.wait_ge(s_OT, 2 * G + 1 + part2)
            turned = ps[:, BK_T, :].rearrange("p (k r c) -> p k r c", r=GH, c=32)[:, :, :, 0:VW]
            hs = slice(GH * g, GH * g + GH)
            if not part2:
                v.tensor_tensor(tmp[:], turned[:, 0:3], bc(rowf[:, b, 1:TB, hs].unsqueeze(3), [P, 3, GH, VW]), MUL).then_inc(s_Y, 1)
                return
            v.wait_ge(s_Y, 2 * G + 1)
            link(v.tensor_copy(YS[:, 0, hs, :], turned[:, 0]))
            v.tensor_tensor(YS[:, 1:TB, hs, :], turned[:, 1:4], tmp[:], ADD).then_inc(s_Y, 1)
            v.wait_ge(s_Y, 2 * G + 2)
            if g == NG - 1:
                link(v.reciprocal(rn[:, :, :], YS[:, :, :, HS]))
                link(v.tensor_tensor(YS[:, :, :, 0:HS], YS[:, :, :, 0:HS], bc(rn[:, :, :].unsqueeze(3), [P, TB, H, HS]), MUL))
                xb = xt[:, TB * b:TB * b + TB, :].rearrange("p t (h d) -> p t h d", h=H)
                v.tensor_tensor(xb, xb, YS[:, :, :, 0:HS], ADD).then_inc(s_xa, 1)
                v.wait_ge(s_xa, b + 1)

        def square_scalar(G, u):
            a = nc.scalar
            b = G // NG
            U = UNITS * G + u
            a.wait_ge(s_A, U + 1)
            if G >= 2 and u == 0:
                a.wait_ge(s_pv, UNITS * (G - 1))
            a.activation(PP[:, G % 2, u, :], A[:, U % 4, :], ACT.Square, bias=feps[:, b:b + 1]).then_inc(s_Q, 1)

        def gate_scalar(G, r):
            a = nc.scalar
            hh = GH * G + r
            a.wait_ge(s_D, hh + 1)
            if hh >= 4:
                a.wait_ge(s_PD, hh - 3)
            a.activation(E[:, hh % 4, :], ps[:, BK_D + hh % 2, :], ACT.Exp).then_inc(s_E, 1)

        def take_sums_scalar(G, diagonal):
            a = nc.scalar
            a.wait_ge(s_pv, UNITS * G + (UNITS if diagonal else NOFF))
            if G:
                a.wait_ge(s_OT, 2 * G - 1 + diagonal)
            if diagonal:
                a.activation(OT[:, 3:7, :].rearrange("p k t -> p (k t)"), ps[:, BK_DIA, :], ACT.Copy).then_inc(s_Od, 1)
            else:
                a.activation(OT[:, 0:3, :].rearrange("p k t -> p (k t)"), ps[:, BK_OFF, P:512], ACT.Copy).then_inc(s_Oo, 1)

        def heads_scalar():
            a = nc.scalar
            a.wait_ge(s_fs, 2)
            for U in range(LAST):
                for stage in stages_at(IN_HEADS, U + 2):
                    if stage in ("turn0", "turn1"):
                        prepare_scalar(0, stage)
                if "exp" in stages_at(IN_HEADS, U):
                    prepare_scalar(0, "exp")
                at(U, 2 * UNITS + LAG - 4, lambda G, n: take_sums_scalar(G, False))
                if U < UNITS * GROUPS:
                    G, u = divmod(U, UNITS)
                    if PLAN[u][0] == "diag":
                        gate_scalar(G, PLAN[u][1])
                    square_scalar(G, u)
                at(U, 2 * UNITS + LAG, lambda G, n: take_sums_scalar(G, True))

        def heads_pool():
            g = nc.gpsimd
            for G in range(GROUPS):
                for r in range(GH):
                    u = PLAN.index(("diag", r))
                    hh = GH * G + r
                    g.wait_ge(s_E, hh + 1)
                    g.wait_ge(s_Q, UNITS * G + u + 1)
                    w = PP[:, G % 2, u, :]
                    g.tensor_tensor(w, w, E[:, hh % 4, :], MUL).then_inc(s_PD, 1)
                    prepare_heads_pool(UNITS * G + u)
                    n = GH * (G % NG) + r - GH - 2
                    if 0 <= n < len(PAIR) and G // NG + 1 < B:
                        decayed_pool(G // NG + 1, n)

        att.close()

        rows = sb("rows", [P, 4, C])
        rowsT = sb("rowsT", [P, 2, P])
        silu = sb("silu", [P, 2, HP])
        hid = sb("hid", [P, 2, HP])
        ysb = sb("ysb", [P, 4, C])
        wj = sb("wj", [P, 4, 2, HP])

        s_ww = sem("s_ww")
        s_lgp = sem("s_lgp")
        s_rd = sem("s_rd")
        s_re = sem("s_re")
        s_M = sem("s_M")
        s_rank = sem("s_rank")
        s_slot = sem("s_slot")
        s_job = sem("s_job")
        s_rk = sem("s_rk")
        s_scat = [sem("s_scat0"), sem("s_scat1")]
        s_row = [sem(f"s_row{k}") for k in range(4)]
        s_rTp = sem("s_rTp")
        s_rT = sem("s_rT")
        s_AB = sem("s_AB")
        s_silu = sem("s_silu")
        s_hid = sem("s_hid")
        s_pad = sem("s_pad")
        s_wj = sem("s_wj")
        s_yp = sem("s_yp")
        s_y = sem("s_y")
        s_yst = [sem(f"s_yst{k}") for k in range(4)]
        s_gat = [sem(f"s_gat{k}") for k in range(B)]
        s_xm = sem("s_xm")
        PJ = JOBS // 4

        def weights_sync():
            sp = nc.sync
            sp.wait_ge(s_part, PARTS * B)
            sp.wait_ge(s_gpart, GPARTS * B)
            sp.dma_start(w13[:, :, 0, 0:HID], w1.rearrange("e c h -> c e h")).then_inc(s_ww, 16)
            sp.dma_start(w13[:, :, 1, 0:HID], w3.rearrange("e c h -> c e h")).then_inc(s_ww, 16)
            sp.wait_ge(s_store, STORES * B)
            for k, (h0, hw) in enumerate(HC):
                sp.dma_start(w2s[0:hw, :, k, :], w2[:, h0:h0 + hw, :].rearrange("e p c -> p e c")).then_inc(s_ww, 16)

        IN_HEADS = {"stats0": 62, "stats1": 64, "stats2": 100, "stats3": 101, "apply0": 92, "apply1": 93, "apply2": 109,
                    "apply3": 110, "turn0": 102, "turn1": 112, "logits": 120, "softmax": 121, "exp": 122, "top": 124,
                    "first": 127, "second": 129, "ranks": 131, "slots": 132, "experts": 134, "scale": 135}
        IN_JOBS = {"stats": 0, "apply": 2, "turn0": 4, "turn1": 5, "logits": 6, "softmax": 6, "exp": 7,
                   "top": 8, "first": 9, "second": 10, "ranks": 12, "slots": 12, "experts": 13, "scale": 14}
        PEELED = 4

        def prep_bank(m):
            return ps[:, BK_T if m == 0 else 4, :]

        def prepare_tensor(m, stage, U=None):
            pe = nc.tensor
            n, hf = 1 + 2 * (m // 2), m % 2
            first_turn = 4 * n + 2 * hf
            if m == 0 and stage in ("turn0", "turn1", "logits", "ranks"):
                pe.wait_ge(s_Y, 2 * ((U - 2 * UNITS - LAG - 5) // UNITS + 1))
            if stage == "turn0":
                if m:
                    pe.wait_ge(s_rk, m)
                if m == 2:
                    pe.wait_ge(s_xT, 12)
                turn_tensor(n, 2 * hf, BK_T if m == 0 else 4)
            if stage == "turn1":
                pe.wait_ge(s_xT, first_turn + 1)
                turn_tensor(n, 2 * hf + 1, BK_T if m == 0 else 4)
            if stage == "logits":
                pe.wait_ge(s_xT, first_turn + 2)
                for i in range(HT):
                    ii = HT * hf + i
                    ins = pe.matmul(prep_bank(m)[:, NE * i:NE * i + NE], xT[:, P * ii:P * ii + P], gwT[:, :], start=True, stop=True)
                ins.then_inc(s_lgp, 1)
            if stage == "ranks":
                pe.wait_ge(s_M, m + 1)
                pe.wait_ge(s_const, NCONST)
                flat = chosen[:].rearrange("p t e -> p (t e)")
                pe.matmul(prep_bank(m)[:, 0:64], trib[:, :], flat, start=True, stop=True)
                pe.matmul(prep_bank(m)[:, 64:128], onesb[:, :], flat, start=True, stop=True).then_inc(s_rank, 1)

        def prepare_heads_tensor(U):
            for stage, place in IN_HEADS.items():
                if U == place:
                    prepare_tensor(0, stage, U)
            for place, sem_, c in ((IN_HEADS["turn0"] + 1, s_xT, 5), (IN_HEADS["turn1"] + 1, s_xT, 6),
                                   (IN_HEADS["softmax"] + 2, s_rd, 1), (IN_HEADS["slots"] + 1, s_rk, 1)):
                if U == place:
                    nc.tensor.wait_ge(sem_, c)

        def prepare_scalar(m, stage):
            a = nc.scalar
            n, hf = 1 + 2 * (m // 2), m % 2
            if stage in ("turn0", "turn1"):
                turn_scalar(n, 2 * hf + int(stage[-1]), BK_T if m == 0 else 4)
            if stage == "exp":
                a.wait_ge(s_rd, m + 1)
                a.activation(L8[:], L8[:], ACT.Exp).then_inc(s_re, 1)

        def stages_at(places, s):
            return [stage for stage, place in places.items() if place == s]

        def prepare_vector(m, stage):
            v = nc.vector
            n, hf = 1 + 2 * (m // 2), m % 2
            ht = slice(HT * hf, HT * hf + HT)

            def e8(ap):
                return bc(ap.unsqueeze(2), [P, HT, NE])

            def iom():
                return bc(iom8[:, :].unsqueeze(1), [P, HT, NE])

            if stage == "stats":
                if m >= 2:
                    v.wait_ge(s_xr, HT * (hf + 1))
                norm_stats(n, hf)
            if stage[:-1] == "stats":
                norm_stats(n, hf, int(stage[-1]))
            if stage[:-1] == "apply":
                norm_apply(n, hf, int(stage[-1]))
            if stage == "apply":
                norm_apply(n, hf)
            if stage == "softmax":
                v.wait_ge(s_lgp, m + 1)
                if m == 0:
                    v.wait_ge(s_eb, 16)
                    v.wait_ge(s_const, NCONST)
                lgt = prep_bank(m)[:, 0:64].rearrange("p (t e) -> p t e", e=NE)
                link(v.tensor_reduce(m1[:, :], lgt, AX.X, ALU.max))
                v.tensor_tensor(L8[:], lgt, e8(m1[:, :]), SUB).then_inc(s_rd, 1)
            if stage == "top":
                v.wait_ge(s_re, m + 1)
                link(v.tensor_reduce(m1[:, :], L8[:], AX.X, ADD))
                link(v.reciprocal(m1[:, :], m1[:, :]))
                link(v.tensor_tensor(L8[:], L8[:], e8(m1[:, :]), MUL))
                link(v.tensor_tensor(V8[:], L8[:], bc(ebt[:, :].unsqueeze(1), [P, HT, NE]), ADD))
            for k in range(TOPK):
                if stage != ("first", "second")[k]:
                    continue
                link(v.tensor_reduce(m1[:, :], V8[:], AX.X, ALU.max))
                link(v.tensor_tensor(Q8[:], V8[:], e8(m1[:, :]), ALU.is_equal))
                link(v.tensor_tensor(Q8[:], Q8[:], iom(), MUL))
                link(v.tensor_reduce(m2[:, :], Q8[:], AX.X, ALU.min))
                link(v.tensor_tensor(oh[:, k], iom(), e8(m2[:, :]), ALU.is_equal))
                if k == 0:
                    link(v.scalar_tensor_tensor(V8[:], oh[:, 0], NEG, V8[:], MUL, ADD))
                else:
                    v.tensor_tensor(chosen[:], oh[:, 0], oh[:, 1], ADD).then_inc(s_M, 1)
                link(v.tensor_tensor(Q8[:], oh[:, k], L8[:], MUL))
                link(v.tensor_reduce(wts[:, k, :], Q8[:], AX.X, ADD))
            if stage == "slots":
                v.wait_ge(s_rank, m + 1)
                rank = prep_bank(m)[:, 0:64].rearrange("p (t e) -> p t e", e=NE)
                tot = prep_bank(m)[:, 64:128].rearrange("p (t e) -> p e t", e=NE)
                v.tensor_copy(base[:], rank)
                v.tensor_copy(totE[:], tot).then_inc(s_rk, 1)
                v.wait_ge(s_rk, m + 1)
                link(v.tensor_tensor_scan(cumE[:].rearrange("p e t -> p (e t)"), carry1[:].rearrange("p e t -> p (e t)"),
                                          totE[:].rearrange("p e t -> p (e t)"), 0.0, MUL, ADD))
                link(v.tensor_tensor(cmp16[:], bc(cumE[:, :, HT - 1:HT], [P, NE, HT]), bc(io128[:, :].unsqueeze(1), [P, NE, HT]), ALU.is_gt))
                link(v.tensor_reduce(tiles[:, :], cmp16[:], AX.X, ADD))
                link(v.tensor_tensor_scan(ends[:, :], ones[:, 0:NE], tiles[:, :], 0.0, MUL, ADD))
                link(v.tensor_tensor(first[:, :], ends[:, :], tiles[:, :], SUB))
                link(v.tensor_scalar(first[:, :], first[:, :], float(P), None, MUL))
                link(v.tensor_tensor(cumE[:], cumE[:], totE[:], SUB))
                link(v.tensor_tensor(cumE[:], cumE[:], bc(first[:, :].unsqueeze(2), [P, NE, HT]), ADD))
                link(v.tensor_tensor(base[:], base[:], cumE[:].rearrange("p e t -> p t e"), ADD))
            if stage == "experts":
                for k in range(TOPK):
                    link(v.tensor_tensor(Q8[:], oh[:, k], base[:], MUL))
                    link(v.tensor_reduce(slotf[:, k, :], Q8[:], AX.X, ADD))
                if m >= 2:
                    v.wait_ge(s_xm, 2 * (m - 1))
                link(v.tensor_copy(slots[:, hf], slotf[:]))
                link(v.tensor_tensor(cmpj[:], bc(iojob[:, :].unsqueeze(2), [P, JOBS, NE]), bc(ends[:, :].unsqueeze(1), [P, JOBS, NE]), ALU.is_ge))
                link(v.tensor_reduce(jobf[:, :], cmpj[:], AX.X, ADD))
                link(v.tensor_scalar(jobf[:, :], jobf[:, :], float(NE - 1), None, ALU.min))
                v.tensor_copy(job_expert[:, hf, :], jobf[:, :]).then_inc(s_job, 1)
            if stage == "scale":
                for k in range(TOPK):
                    v.tensor_tensor(xs[k][:, ht, :], xh[:, ht, :], bc(wts[:, k, :].unsqueeze(2), [P, HT, C]), MUL).then_inc(s_slot, 1)

        def pad_pool():
            g = nc.gpsimd
            g.wait_ge(s_part, PARTS * B)
            g.wait_ge(s_gpart, GPARTS * B)
            g.memset(w13[:, :, :, HID:HP], 0.0).then_inc(s_pad, 1)

        HEAD_SCATTERS = [2, 2, 2, 1, 1, 1, 1, 1, 1]

        def prepare_heads_pool(U):
            if U == UNITS * 7:
                norm_root(1, 0, 0)
            if U == UNITS * 10 + 2:
                norm_root(1, 0, 1)
            if U >= UNITS * 13 + 7:
                turn = GH * (U // UNITS - 13) + [u for u in range(UNITS) if PLAN[u][0] == "diag"].index(U % UNITS) - 3
                for r in range(sum(HEAD_SCATTERS[:turn]), sum(HEAD_SCATTERS[:turn + 1])):
                    scatter_pool(0, r)

        def scatters_pool(m, rows=range(TOPK * HT)):
            for r in rows:
                scatter_pool(m, r)

        def scatter_pool(m, r):
            g, hf = nc.gpsimd, m % 2
            k, i = divmod(r, HT)
            if i == 0:
                g.wait_ge(s_slot, TOPK * m + k + 1)
            if r == 0:
                g.wait_ge(s_job, m + 1)
                g.wait_ge(s_zero, 32)
            g.indirect_dma_start(xr[hf], bass.IndirectOffsetOnAxis(ap=slots[:, hf, k, i:i + 1], axis=0),
                                 xs[k][:, HT * hf + i, :], None).then_inc(s_scat[hf], 16)

        def gather_pool(m):
            g, hf = nc.gpsimd, m % 2
            for k in range(4):
                g.wait_ge(s_yst[k], 16 * PJ * (m + 1))
            for i in range(HT):
                for k in range(TOPK):
                    g.indirect_dma_start(xs[k][:, HT * hf + i, :], None, yr[hf],
                                         bass.IndirectOffsetOnAxis(ap=slots[:, hf, k, i:i + 1], axis=0)).then_inc(s_gat[2 * hf + i // TB], 16)

        def add_vector(m):
            v, hf = nc.vector, m % 2
            for b in range(2 * hf, 2 * hf + 2):
                t = slice(TB * b, TB * b + TB)
                v.wait_ge(s_gat[b], 16 * TOPK * TB * (m // 2 + 1))
                link(v.tensor_tensor(xh[:, t, :], xs[0][:, t, :], xh[:, t, :], ADD))
                v.tensor_tensor(xt[:, t, :], xt[:, t, :], xh[:, t, :], ADD).then_inc(s_xm, 1)
            v.wait_ge(s_xm, 2 * (m + 1))

        def looped(eng, step, lo, hi, last):
            for s in range(4 * lo):
                step(s // 4, s % 4, s)
            with eng.Fori(lo, hi) as q:
                for k in range(4):
                    step(q, k, None)
            for s in range(4 * hi, last + 1):
                step(s // 4, s % 4, s)

        def before(q, k, d):
            return (q - (d - k + 3) // 4, (k - d) % 4)

        def after(q, k):
            return (q, k + 1) if k < 3 else (q + 1, 0)

        def jobs_sync(m):
            sp = nc.sync
            hf = m % 2
            sp.wait_ge(s_scat[hf], 16 * TOPK * HT * (m // 2 + 1))

            def load(q, k):
                sp.wait_ge(s_rTp, JOBS * m + 4 * q + k - 3)
                sp.dma_start(rows[:, k, :], xr[hf][bass.ds((4 * q + k) * P, P), :]).then_inc(s_row[k], 16)

            def store(q, k):
                sp.wait_ge(s_y, JOBS * m + 4 * q + k + 1)
                sp.dma_start(yr[hf][bass.ds((4 * q + k) * P, P), :], ysb[:, k, :]).then_inc(s_yst[k], 16)

            def step(q, k, s):
                if s is None or s < JOBS:
                    if s is None or m or s >= 4:
                        load(q, k)
                    else:
                        sp.dma_start(rows[:, k, :], xr[hf][P * k:P * k + P, :]).then_inc(s_row[k], 16)
                if s is None or s >= 5:
                    store(*before(q, k, 5))

            looped(sp, step, 2, PJ, JOBS + 4)

        def jobs_tensor(m):
            pe = nc.tensor
            hf = m % 2
            pe.wait_ge(s_job, m + 1)
            if m == 0:
                pe.wait_ge(s_ww, 16 * 5)

            def turn(q, k):
                J = JOBS * m + 4 * q + k
                pe.wait_ge(s_row[k], 16 * (PJ * m + q + 1))
                if m or not isinstance(J, int) or J >= 2:
                    pe.wait_ge(s_rT, J - 1)
                pe.transpose(ps[:, 5 + k % 2, 0:P], rows[:, k, :], ident[:, :]).then_inc(s_rTp, 1)

            def up(q, k):
                J = JOBS * m + 4 * q + k
                pe.wait_ge(s_wj, J + 1)
                pe.wait_ge(s_rT, J + 1)
                if m or not isinstance(J, int) or J >= 2:
                    pe.wait_ge(s_hid, J - 1)
                for w in range(2):
                    for c in range(len(HC)):
                        ins = pe.matmul(ps[:, 2 * (k % 2) + w, P * c:P * c + P],
                                        wj[:, k, w, P * c:P * c + P], rowsT[:, k % 2, :],
                                        start=True, stop=True)
                    ins.then_inc(s_AB, 1)

            def down(q, k):
                e = pe.value_load(job_expert[0:1, hf, bass.ds(4 * q + k, 1)], min_val=0, max_val=NE - 1)
                J = JOBS * m + 4 * q + k
                pe.wait_ge(s_hid, J + 1)
                if m or not isinstance(J, int) or J >= 1:
                    pe.wait_ge(s_y, J)
                for c, (h0, hw) in enumerate(HC):
                    ins = pe.matmul(ps[:, 7, 0:P], hid[0:hw, k % 2, P * c:P * c + P], w2s[0:hw, bass.ds(e, 1), c, :].squeeze(1),
                                    start=(c == 0), stop=(c == len(HC) - 1))
                ins.then_inc(s_yp, 1)

            def step(q, k, s):
                for stage in stages_at(IN_JOBS, s) if hf == 0 else []:
                    prepare_tensor(m + 1, stage)
                if m == 1 and s in (JOBS - 2, JOBS):
                    turn_rec_tensor((s - JOBS + 2) // 2)
                if s is None or s < JOBS - 1:
                    turn(*after(q, k))
                if s is None or s < JOBS:
                    up(q, k)
                if s is None or 1 <= s:
                    down(*before(q, k, 1))

            turn(0, 0)
            looped(pe, step, 1 if hf else PEELED, PJ - 2 if m == 1 else PJ - 1, JOBS)

        def jobs_scalar(m):
            a, hf = nc.scalar, m % 2

            def take_rows(q, k):
                J = JOBS * m + 4 * q + k
                a.wait_ge(s_rTp, J + 1)
                if m or not isinstance(J, int) or J >= 2:
                    a.wait_ge(s_AB, 2 * (J - 1))
                a.activation(rowsT[:, k % 2, :], ps[:, 5 + k % 2, 0:P], ACT.Copy).then_inc(s_rT, 1)

            def gate(q, k):
                J = JOBS * m + 4 * q + k
                a.wait_ge(s_AB, 2 * J + 1)
                if m or not isinstance(J, int) or J >= 2:
                    a.wait_ge(s_hid, J - 1)
                a.activation(silu[:, k % 2, :], ps[:, 2 * (k % 2), 0:HP], ACT.Silu).then_inc(s_silu, 1)

            def take_out(q, k):
                J = JOBS * m + 4 * q + k
                a.wait_ge(s_yp, J + 1)
                if m or not isinstance(J, int) or J >= 4:
                    a.wait_ge(s_yst[k], 16 * (PJ * m + q))
                a.activation(ysb[:, k, :], ps[:, 7, 0:P], ACT.Copy).then_inc(s_y, 1)

            def step(q, k, s):
                for stage in stages_at(IN_JOBS, s) if hf == 0 else []:
                    prepare_scalar(m + 1, stage)
                if m == 1 and s in (JOBS - 2, JOBS):
                    turn_scalar(2, (s - JOBS + 2) // 2, REC_T)
                if s is None or s < JOBS - 1:
                    take_rows(*after(q, k))
                if s is None or s < JOBS:
                    gate(q, k)
                if s is None or s >= 1:
                    take_out(*before(q, k, 1))

            take_rows(0, 0)
            looped(a, step, 1 if hf else PEELED, PJ - 2 if m == 1 else PJ - 1, JOBS)

        def jobs_vector(m):
            v = nc.vector
            hf = m % 2

            def take_weights(q, k):
                e = v.value_load(job_expert[0:1, hf, bass.ds(4 * q + k, 1)], min_val=0, max_val=NE - 1)
                J = JOBS * m + 4 * q + k
                if m or not isinstance(J, int) or J >= 4:
                    v.wait_ge(s_AB, 2 * (J - 3))
                v.tensor_copy(wj[:, k, :, :].rearrange("p w h -> p (w h)"),
                              w13[:, bass.ds(e, 1), :, :].rearrange("p e w h -> p (e w h)")).then_inc(s_wj, 1)

            def mix(q, k):
                J = JOBS * m + 4 * q + k
                v.wait_ge(s_silu, J + 1)
                v.wait_ge(s_AB, 2 * J + 2)
                if m or not isinstance(J, int) or J >= 2:
                    v.wait_ge(s_yp, J - 1)
                v.tensor_tensor(hid[:, k % 2, :], silu[:, k % 2, :], ps[:, 2 * (k % 2) + 1, 0:HP], MUL).then_inc(s_hid, 1)

            def step(q, k, s):
                if s is None or s < JOBS - 2:
                    take_weights(*after(*after(q, k)))
                mix(q, k)
                for stage in stages_at(IN_JOBS, s) if hf == 0 else []:
                    prepare_vector(m + 1, stage)
                if m == 1 and s == JOBS - 8:
                    add_vector(0)
                if m == 1 and s == JOBS - 6:
                    norm_stats(2, 0)
                if m == 1 and s == JOBS - 4:
                    norm_apply(2, 0)

            v.wait_ge(s_job, m + 1)
            if m == 0:
                v.wait_ge(s_ww, 16 * 5)
                v.wait_ge(s_pad, 1)
            take_weights(0, 0)
            take_weights(0, 1)
            looped(v, step, 1 if hf else PEELED, PJ - 2 if m == 1 else PJ - 1, JOBS - 1)

        win = sb("win", [P, 3, C])
        wout = sb("wout", [P, C])
        cw = sb("cw", [P, 2, C, CONV_K])
        wtap = sb("wtap", [P, 2, CONV_K, C])
        gn = sb("gn", [P, 1])
        sg = sb("sg", [P, 2, 4, T])
        gi = sb("gi", [P, 2, T])
        rec = sb("rec", [P, 2, T])
        gg = sb("gg", [P, 2, T])
        osq = sb("osq", [P, 2, T])
        og = sb("og", [P, 2, T])
        osb = sb("osb", [P, 2, T])
        msq = sb("msq", [P, B, TB])
        rms = sb("rms", [P, B, TB])

        s_wh = sem("s_wh")
        s_wtap = sem("s_wtap")
        s_raw = sem("s_raw")
        s_sig = sem("s_sig")
        s_gi = sem("s_gi")
        s_rec = sem("s_rec")
        s_gg = sem("s_gg")
        s_osq = sem("s_osq")
        s_og = sem("s_og")
        s_ho = sem("s_ho")
        s_osb = sem("s_osb")
        s_ms = sem("s_ms")
        s_rt = sem("s_rt")
        s_xr = sem("s_xr")

        def rec_sync():
            sp = nc.sync
            for k, w in enumerate((Wf, Wi, Wg)):
                sp.dma_start(win[:, k, :], w).then_inc(s_wh, 16)
            sp.dma_start(wout[:, :], Wo).then_inc(s_wh, 16)
            for k, w in enumerate((conv_f, conv_i)):
                sp.dma_start(cw[:, k, :, :].rearrange("p c n -> p (c n)"), w.rearrange("c n -> (c n)").partition_broadcast(P)).then_inc(s_wh, 16)
            sp.dma_start(gn[:, :], gnw.rearrange("(d a) -> d a", a=1)).then_inc(s_wh, 16)

        def taps_pool():
            g = nc.gpsimd
            g.wait_ge(s_wh, 16 * 7)
            for k in range(2):
                for tap in range(CONV_K):
                    g.tensor_tensor(wtap[:, k, tap, :], win[:, k, :], cw[:, k, :, tap], MUL).then_inc(s_wtap, 1)

        def raw_bank(b, k):
            return ps[:, 5 * (b % 2) + k, :]

        REC_T = 4

        def turn_rec_tensor(b):
            pe = nc.tensor
            if b:
                pe.wait_ge(s_xT, 8 + b)
            else:
                pe.wait_ge(s_rk, 2)
            turn_tensor(2, b, REC_T)

        def project_tensor(b, parts=(0, 1, 2)):
            for k in parts:
                project_part_tensor(b, k)

        def project_part_tensor(b, k):
            pe = nc.tensor
            if k == 0:
                pe.wait_ge(s_xT, 8 + b + 1)
                if b == 0:
                    pe.wait_ge(s_wtap, 2 * CONV_K)
                if b >= 2:
                    pe.wait_ge(s_ms, b - 1)
                    pe.wait_ge(s_osb, b - 1)
            if k == 2:
                pe.matmul(raw_bank(b, 2), win[:, 2, :], xT[:, T * b:T * b + T], start=True, stop=True).then_inc(s_raw, 1)
                return
            for d in range(CONV_K):
                ins = pe.matmul(raw_bank(b, k)[:, d:T], wtap[:, k, CONV_K - 1 - d, :], xT[:, T * b:T * b + T - d],
                                start=(d == 0), stop=(d == CONV_K - 1))
            ins.then_inc(s_raw, 1)

        def finish_tensor(b):
            pe = nc.tensor
            pe.wait_ge(s_og, b + 1)
            pe.wait_ge(s_osq, b + 1)
            for t in range(TB):
                pe.matmul(raw_bank(b, 1)[:, P * t:P * t + P], og[:, b % 2, P * t:P * t + P], wout[:, :], start=True, stop=True)
            for t in range(TB):
                ins = pe.matmul(raw_bank(b, 0)[:, t:t + 1], osq[:, b % 2, P * t:P * t + P], ones[:, 0:1], start=True, stop=True)
            ins.then_inc(s_ho, 1)

        def sigmoids_scalar(b):
            a = nc.scalar
            a.wait_ge(s_raw, 3 * b + 1)
            if b >= 2:
                a.wait_ge(s_rec, b - 1)
                a.wait_ge(s_gg, b - 1)
            a.activation(sg[:, b % 2, 1, :], raw_bank(b, 0), ACT.Sigmoid, scale=-1.0).then_inc(s_sig, 1)
            a.activation(sg[:, b % 2, 0, :], raw_bank(b, 0), ACT.Sigmoid).then_inc(s_sig, 1)
            a.wait_ge(s_raw, 3 * b + 2)
            a.activation(sg[:, b % 2, 2, :], raw_bank(b, 1), ACT.Sigmoid).then_inc(s_sig, 1)
            a.wait_ge(s_raw, 3 * b + 3)
            a.activation(sg[:, b % 2, 3, :], raw_bank(b, 2), ACT.Sigmoid).then_inc(s_sig, 1)

        def squares_scalar(b):
            a = nc.scalar
            a.wait_ge(s_rec, b + 1)
            if b >= 2:
                a.wait_ge(s_ho, b - 1)
            a.activation(osq[:, b % 2, :], rec[:, b % 2, :], ACT.Square).then_inc(s_osq, 1)

        def take_output_scalar(b):
            a = nc.scalar
            a.wait_ge(s_ho, b + 1)
            if b >= 2:
                a.wait_ge(s_xr, TB * (b - 1))
            a.activation(osb[:, b % 2, :], raw_bank(b, 1), ACT.Copy).then_inc(s_osb, 1)

        def recur_vector(b):
            v = nc.vector
            v.wait_ge(s_sig, 4 * b + 3)
            link(v.tensor_tensor(gi[:, b % 2, :], raw_bank(b, 1), sg[:, b % 2, 2, :], MUL))
            v.tensor_tensor(gi[:, b % 2, :], gi[:, b % 2, :], sg[:, b % 2, 1, :], MUL).then_inc(s_gi, 1)
            v.wait_ge(s_gi, b + 1)
            if b >= 2:
                v.wait_ge(s_osq, b - 1)
                v.wait_ge(s_og, b - 1)
            v.tensor_tensor_scan(rec[:, b % 2, :], sg[:, b % 2, 0, :], gi[:, b % 2, :], 0.0, MUL, ADD).then_inc(s_rec, 1)
            v.wait_ge(s_sig, 4 * b + 4)
            v.scalar_tensor_tensor(gg[:, b % 2, :], raw_bank(b, 2), gn[:, 0:1], sg[:, b % 2, 3, :], MUL, MUL).then_inc(s_gg, 1)

        def output_vector(b):
            v = nc.vector
            v.wait_ge(s_ho, b + 1)
            v.tensor_scalar(msq[:, b, :], raw_bank(b, 0)[:, 0:TB], 1.0 / C, LN_EPS, MUL, ADD).then_inc(s_ms, 1)
            v.wait_ge(s_rt, b + 1)
            v.wait_ge(s_osb, b + 1)
            for t in range(TB):
                i = TB * b + t
                v.scalar_tensor_tensor(xt[:, i, :], osb[:, b % 2, P * t:P * t + P], rms[:, b, t:t + 1], xt[:, i, :], MUL, ADD).then_inc(s_xr, 1)

        def product_pool(b):
            g = nc.gpsimd
            g.wait_ge(s_gg, b + 1)
            g.wait_ge(s_rec, b + 1)
            if b >= 2:
                g.wait_ge(s_ho, b - 1)
            g.tensor_tensor(og[:, b % 2, :], rec[:, b % 2, :], gg[:, b % 2, :], MUL).then_inc(s_og, 1)

        def rms_pool(b):
            g = nc.gpsimd
            g.wait_ge(s_ms, b + 1)
            g.tensor_tensor(rms[:, b, :], msq[:, b, :], mhalf[:, 0:TB], ALU.pow).then_inc(s_rt, 1)

        block = ctx.enter_context(nc.Block())

        @block.sync
        def _(sp):
            proj_sync()
            fill_sync()
            sp.wait_ge(s_fill, 64)
            for n in range(2 * B):
                stack_sync(n)
                if n == 1:
                    clear_sync()
            weights_sync()
            sp.wait_ge(s_xa, B)
            jobs_sync(0)
            rec_sync()
            for m in range(1, 4):
                jobs_sync(m)
            for b in range(B):
                sp.wait_ge(s_xm, B + b + 1)
                sp.dma_start(out_rows[:, TB * b:TB * b + TB, :], xt[:, TB * b:TB * b + TB, :]).then_inc(s_out, 16)
            sp.wait_ge(s_out, 16 * B)

        @block.gpsimd
        def _(g):
            const_pool()
            heads_pool()
            pad_pool()
            for r in range(sum(HEAD_SCATTERS), TOPK * HT):
                scatter_pool(0, r)
            norm_root(1, 1)
            scatters_pool(1)
            gather_pool(0)
            taps_pool()
            norm_root(2, 0)
            gather_pool(1)
            product_pool(0)
            product_pool(1)
            norm_root(2, 1)
            rms_pool(0)
            rms_pool(1)
            norm_root(3, 0)
            product_pool(2)
            scatters_pool(2, range(0, 8))
            product_pool(3)
            scatters_pool(2, range(8, 12))
            rms_pool(2)
            scatters_pool(2, range(12, 16))
            rms_pool(3)
            norm_root(3, 1)
            scatters_pool(3)
            gather_pool(2)
            gather_pool(3)

        @block.scalar
        def _(a):
            proj_scalar(0)
            proj_scalar(1)
            gates_scalar(0)
            proj_scalar(2)
            proj_scalar(3)
            decays_scalar(0)
            gates_scalar(1)
            decays_scalar(1)
            heads_scalar()
            jobs_scalar(0)
            jobs_scalar(1)
            sigmoids_scalar(0)
            sigmoids_scalar(1)
            squares_scalar(0)
            squares_scalar(1)
            take_output_scalar(0)
            take_output_scalar(1)
            turn_scalar(2, 2, REC_T)
            turn_scalar(2, 3, REC_T)
            sigmoids_scalar(2)
            prepare_scalar(2, "turn0")
            prepare_scalar(2, "turn1")
            prepare_scalar(2, "exp")
            sigmoids_scalar(3)
            for b in (2, 3):
                squares_scalar(b)
                take_output_scalar(b)
            jobs_scalar(2)
            jobs_scalar(3)

        @block.tensor
        def _(pe):
            weights_tensor()
            proj_tensor(0)
            proj_tensor(1)
            proj_tensor(2)
            gates_tensor(0)
            proj_tensor(3)
            gates_tensor(1)
            heads_tensor()
            jobs_tensor(0)
            jobs_tensor(1)
            pe.wait_ge(s_y, 2 * JOBS)
            project_tensor(0)
            project_tensor(1)
            finish_tensor(0)
            finish_tensor(1)
            turn_rec_tensor(2)
            turn_rec_tensor(3)
            project_tensor(2)
            prepare_tensor(2, "turn0")
            prepare_tensor(2, "turn1")
            prepare_tensor(2, "logits")
            project_tensor(3, (0,))
            prepare_tensor(2, "ranks")
            project_tensor(3, (1, 2))
            finish_tensor(2)
            finish_tensor(3)
            pe.wait_ge(s_ms, B)
            pe.wait_ge(s_osb, B)
            jobs_tensor(2)
            jobs_tensor(3)

        @block.vector
        def _(v):
            v.wait_ge(s_x, 64)
            for hf in range(2):
                norm_stats(0, hf)
                norm_apply(0, hf)
            bound_vector(0)
            bound_scale_vector(0)
            for k in range(5):
                parts_vector(0, k)
            gates_vector(0)
            gate_rows_vector(0)
            gate_rows_vector(1)
            for k in range(5, 10):
                parts_vector(0, k)
            bound_vector(1)
            gates_vector(1)
            gate_rows_vector(2)
            bound_scale_vector(1)
            gate_rows_vector(3)
            heads_vector()
            jobs_vector(0)
            jobs_vector(1)
            recur_vector(0)
            recur_vector(1)
            add_vector(1)
            norm_stats(2, 1)
            norm_apply(2, 1)
            output_vector(0)
            output_vector(1)
            for stage in ("stats", "apply"):
                prepare_vector(2, stage)
            recur_vector(2)
            for stage in ("softmax", "top", "first", "second", "slots", "experts", "scale"):
                prepare_vector(2, stage)
            recur_vector(3)
            output_vector(2)
            output_vector(3)
            jobs_vector(2)
            jobs_vector(3)
            add_vector(2)
            add_vector(3)


_INS = ['L0_attn_a_x', 'L0_attn_a_W', 'L0_attn_b_Wi', 'L0_attn_b_Wf', 'L0_attn_b_Wg', 'L0_attn_b_conv_i',
        'L0_attn_b_conv_f', 'L0_attn_b_g_norm_weight', 'L0_attn_b_Wo', 'L0_ffn_gate_w', 'L0_ffn_expert_bias',
        'L0_ffn_w1', 'L0_ffn_w2', 'L0_ffn_w3']


def kernel(**inputs):
    import numpy as _np
    import concourse.bacc as _bacc
    from concourse import mybir as _mybir
    from concourse.bass_utils import run_bass_kernel_spmd as _run

    nc = _bacc.Bacc("TRN2", target_bir_lowering=False, num_devices=1)
    arrays, args = {}, []
    for name in _INS:
        a = _np.ascontiguousarray(inputs[name])
        arrays[f"in_{name}_dram"] = a
        args.append(nc.dram_tensor(f"in_{name}_dram", a.shape, _mybir.dt.from_np(a.dtype), kind="ExternalInput").ap())
    args.append(nc.dram_tensor("out_0_dram", (B, T, C), F32, kind="ExternalOutput").ap())
    build(nc, *args)
    r = _run(nc, [arrays], core_ids=[0])
    return r.results[0]["out_0_dram"]
```
